# Optimizing a Trainium2 kernel written in Bass

```python
import numpy as np
import jax
import jax.numpy as jnp

def _softmax(x, axis=-1):
    return jax.nn.softmax(x, axis=axis)

def _gelu(x):
    return jax.nn.gelu(x, approximate=True)

def _silu(x):
    return jax.nn.silu(x)

def _sigmoid(x):
    return jax.nn.sigmoid(x)

def _layernorm(x, axis=-1, eps=1e-05):
    m = jnp.mean(x, axis=axis, keepdims=True)
    v = jnp.var(x, axis=axis, keepdims=True)
    return (x - m) / jnp.sqrt(v + eps)

def _scatter_add(tgt, idx, src, axis=0):
    return tgt.at[idx].add(src)

def _segment_sum(src, seg, n):
    return jax.ops.segment_sum(src, seg, n)
kernel_name = 'mk_flamingo_gated_d2_seqx_r2_2346ac'

def setup_inputs(seed: int=0):
    np.random.seed(seed)
    _w = jnp.asarray

    def _rec_inputs():
        import jax
        import jax.numpy as jnp
        _rk = jax.random.key(seed)
        x = 4.136e-05 + 0.9999 * jax.random.normal(jax.random.fold_in(_rk, 1), (8, 512, 512), jnp.float32)
        _lenS = 512 - jax.random.randint(jax.random.fold_in(_rk, 7), (8,), 0, max(1, 512 // 4) + 1, jnp.int32)
        _lenS2 = 512 - jax.random.randint(jax.random.fold_in(_rk, 8), (8,), 0, max(1, 512 // 4) + 1, jnp.int32)
        _ctx_2048P = jax.random.normal(jax.random.fold_in(_rk, 11), (8, 16, 1024), jnp.float32)
        _ctx_2048c = jax.random.dirichlet(jax.random.fold_in(_rk, 511), 0.3 * jnp.ones((16,), jnp.float32), (8, 512))
        _ctx_2048t = jnp.einsum('bsk,bkd->bsd', _ctx_2048c, _ctx_2048P)
        _ctx_2048t = _ctx_2048t * jax.lax.rsqrt(jnp.mean(jnp.square(_ctx_2048t)) + 1e-12) * 0.953939
        ctx_2048 = -0.000392918 + 0.999932 * (_ctx_2048t + 0.3 * jax.random.normal(jax.random.fold_in(_rk, 611), (8, 512, 1024), jnp.float32))
        itok_Bx1_68_817 = jax.random.randint(jax.random.fold_in(_rk, 12), (8, 1), 68, 409, jnp.int32)
        _validS = jnp.arange(512)[None, :] < _lenS[:, None]
        _validS2 = jnp.arange(512)[None, :] < _lenS2[:, None]
        _causal = jnp.tril(jnp.ones((512, 512), dtype=bool))
        mask_BxS2_ik0 = jnp.where(jnp.broadcast_to(_validS2[:, :], (8, 512)), 0, 1).astype(jnp.int32)
        _g = jax.random.normal(jax.random.fold_in(_rk, 9001), (2, 2), jnp.float32)
        _g = jnp.sign(_g) * jnp.maximum(jnp.abs(_g), 1.0) + (_g == 0) * 1.0
        g_xattn = _g[0]
        g_ffn = _g[1]
        return (x, ctx_2048, itok_Bx1_68_817, mask_BxS2_ik0, g_xattn, g_ffn)
    x, ctx_2048, itok_Bx1_68_817, mask_BxS2_ik0, g_xattn, g_ffn = _rec_inputs()

    def _L0_xattn_setup():
        import jax, jax.numpy as jnp
        import numpy as np
        UNITS = 512
        NUM_HEADS = 16
        MASK_VALUE = -1000000000000.0

        def _split_heads(x, n):
            B, S, D = x.shape
            return x.reshape(B, S, n, D // n).transpose(0, 2, 1, 3)
        key = jax.random.key(seed)
        k1, k2, k3, k4 = jax.random.split(key, 4)
        B, S = (8, 512)
        memory = jax.random.normal(k1, (B, S, 2 * UNITS), dtype=jnp.float32)
        query = jax.random.normal(k2, (B, S, UNITS), dtype=jnp.float32)
        b = jax.random.normal(k3, (S,), dtype=jnp.float32)
        seq_len = jax.random.randint(k4, (B, 1), 0, S, dtype=jnp.int32)
        return {'memory': memory, 'query': query, 'b': b, 'seq_len': seq_len}
    _L0_xattn_all = _L0_xattn_setup()
    _L0_xattn_in = {k: v for k, v in _L0_xattn_all.items() if k in ('b',)}
    del _L0_xattn_all

    def _L0_ffn_setup():
        import jax, jax.numpy as jnp
        import numpy as np
        D_MODEL = 512
        key = jax.random.key(seed)
        k_x, k_w, k_a1, k_a2 = jax.random.split(key, 4)
        x = jax.random.normal(k_x, (4, 1024, D_MODEL), dtype=jnp.float32)
        weight = jax.random.normal(k_w, (D_MODEL, D_MODEL), dtype=jnp.float32) * 0.02
        aux_weight1 = jax.random.normal(k_a1, (D_MODEL, D_MODEL), dtype=jnp.float32) * 0.02
        aux_weight2 = jax.random.normal(k_a2, (D_MODEL, D_MODEL), dtype=jnp.float32) * 0.02
        bias = jnp.zeros((D_MODEL,), dtype=jnp.float32)
        return {'x': x, 'weight': weight, 'aux_weight1': aux_weight1, 'aux_weight2': aux_weight2, 'bias': bias}
    _L0_ffn_all = _L0_ffn_setup()
    _L0_ffn_in = {k: v for k, v in _L0_ffn_all.items() if k in ('weight', 'aux_weight1', 'aux_weight2', 'bias')}
    del _L0_ffn_all

    def _L1_xattn_setup():
        import jax, jax.numpy as jnp
        import numpy as np
        UNITS = 512
        NUM_HEADS = 8

        def _split_heads(x, n):
            B, S, D = x.shape
            return x.reshape(B, S, n, D // n).transpose(0, 2, 1, 3)
        key = jax.random.key(seed)
        k1, k2, k3 = jax.random.split(key, 3)
        B, S = (8, 512)
        memory = jax.random.normal(k1, (B, S, 2 * UNITS), dtype=jnp.float32)
        query = jax.random.normal(k2, (B, S, UNITS), dtype=jnp.float32)
        seq_mask = jax.random.randint(k3, (B, S), 0, 2, dtype=jnp.int32)
        b = jnp.zeros((1,), dtype=jnp.float32)
        return {'memory': memory, 'query': query, 'seq_mask': seq_mask, 'b': b}
    _L1_xattn_all = _L1_xattn_setup()
    _L1_xattn_in = {k: v for k, v in _L1_xattn_all.items() if k in ('b',)}
    del _L1_xattn_all

    def _L1_ffn_setup():
        import jax, jax.numpy as jnp
        import numpy as np
        BLOCK = 32
        W_BITS = 4
        ACT_BITS = 16

        def act_qdq(x):
            qmax = 2.0 ** (ACT_BITS - 1) - 1.0
            scale = jnp.maximum(jnp.max(jnp.abs(x)) / qmax, 1e-12)
            return jnp.clip(jnp.round(x / scale), -qmax - 1.0, qmax) * scale

        def fixed_qdq_u16(x):
            scale = 1.0 / 65536.0
            return jnp.clip(jnp.round(x / scale), 0.0, 65535.0) * scale

        def lpbq_dequant(w):
            O, I = w.shape
            qmax = 2.0 ** (W_BITS - 1) - 1.0
            wb = w.reshape(O, I // BLOCK, BLOCK)
            s = jnp.maximum(jnp.max(jnp.abs(wb), axis=-1, keepdims=True) / qmax, 1e-12)
            wq = jnp.clip(jnp.round(wb / s), -qmax - 1.0, qmax) * s
            return wq.reshape(O, I)
        key = jax.random.key(seed)
        k1, k2, k3, k4 = jax.random.split(key, 4)
        B, S, H, I = (2, 2048, 512, 1536)
        x = jax.random.normal(k1, (B, S, H), jnp.float32)
        w_gate = jax.random.normal(k2, (I, H), jnp.float32) * 0.02
        w_up = jax.random.normal(k3, (I, H), jnp.float32) * 0.02
        w_down = jax.random.normal(k4, (H, I), jnp.float32) * 0.02
        return {'x': x, 'w_gate': w_gate, 'w_up': w_up, 'w_down': w_down}
    _L1_ffn_all = _L1_ffn_setup()
    _L1_ffn_in = {k: v for k, v in _L1_ffn_all.items() if k in ('w_gate', 'w_up', 'w_down')}
    del _L1_ffn_all
    return {'x': x, 'ctx_2048': ctx_2048, 'itok_Bx1_68_817': itok_Bx1_68_817, 'mask_BxS2_ik0': mask_BxS2_ik0, 'g_xattn': g_xattn, 'g_ffn': g_ffn, 'L0_xattn_b': _L0_xattn_in['b'], 'L0_ffn_weight': _L0_ffn_in['weight'], 'L0_ffn_aux_weight1': _L0_ffn_in['aux_weight1'], 'L0_ffn_aux_weight2': _L0_ffn_in['aux_weight2'], 'L0_ffn_bias': _L0_ffn_in['bias'], 'L1_xattn_b': _L1_xattn_in['b'], 'L1_ffn_w_gate': _L1_ffn_in['w_gate'], 'L1_ffn_w_up': _L1_ffn_in['w_up'], 'L1_ffn_w_down': _L1_ffn_in['w_down']}

def reference(x, ctx_2048, itok_Bx1_68_817, mask_BxS2_ik0, g_xattn, g_ffn, L0_xattn_b, L0_ffn_weight, L0_ffn_aux_weight1, L0_ffn_aux_weight2, L0_ffn_bias, L1_xattn_b, L1_ffn_w_gate, L1_ffn_w_up, L1_ffn_w_down):
    import jax
    import jax.numpy as jnp

    def _L0_xattn_ref(memory, query, b, seq_len):
        import jax, jax.numpy as jnp
        import numpy as np
        UNITS = 512
        NUM_HEADS = 16
        MASK_VALUE = -1000000000000.0

        def _split_heads(x, n):
            B, S, D = x.shape
            return x.reshape(B, S, n, D // n).transpose(0, 2, 1, 3)
        B, S, _ = query.shape
        dh = UNITS // NUM_HEADS
        k_mem, v_mem = jnp.split(memory, 2, axis=2)
        Q = _split_heads(query, NUM_HEADS) * dh ** (-0.5)
        Kh = _split_heads(k_mem, NUM_HEADS)
        Vh = _split_heads(v_mem, NUM_HEADS)
        logits = jnp.einsum('bhqd,bhkd->bhqk', Q, Kh) + b
        valid = (jnp.arange(S)[None, :] < seq_len[:, 0:1]).astype(jnp.float32)
        logits = logits + MASK_VALUE * (1.0 - valid)[:, None, None, :]
        weights = jax.nn.softmax(logits, axis=-1)
        out = jnp.einsum('bhqk,bhkd->bhqd', weights, Vh)
        return out.transpose(0, 2, 1, 3).reshape(B, S, UNITS)

    def _L0_ffn_ref(x, weight, aux_weight1, aux_weight2, bias):
        import jax, jax.numpy as jnp
        import numpy as np
        D_MODEL = 512
        h = jnp.einsum('btc,cd->btd', x, weight)
        h = jnp.einsum('btc,cd->btd', h, aux_weight1)
        h = jnp.einsum('btc,cd->btd', h, aux_weight2)
        return jnp.tanh(h + bias)

    def _L1_xattn_ref(memory, query, seq_mask, b):
        import jax, jax.numpy as jnp
        import numpy as np
        UNITS = 512
        NUM_HEADS = 8

        def _split_heads(x, n):
            B, S, D = x.shape
            return x.reshape(B, S, n, D // n).transpose(0, 2, 1, 3)
        H = NUM_HEADS
        depth = UNITS // H
        Q = _split_heads(query, H) * depth ** (-0.5)
        k_mem, v_mem = jnp.split(memory, 2, axis=2)
        K = _split_heads(k_mem, H)
        V = _split_heads(v_mem, H)
        logits = jnp.einsum('bhqd,bhkd->bhqk', Q, K) + b[0]
        mask = seq_mask.astype(jnp.float32)[:, None, None, :]
        logits = logits + -1e+30 * (1.0 - mask)
        weights = jax.nn.softmax(logits, axis=-1)
        out = jnp.einsum('bhqk,bhkd->bhqd', weights, V)
        B, _, S, _ = out.shape
        return out.transpose(0, 2, 1, 3).reshape(B, S, UNITS)

    def _L1_ffn_ref(x, w_gate, w_up, w_down):
        import jax, jax.numpy as jnp
        import numpy as np
        BLOCK = 32
        W_BITS = 4
        ACT_BITS = 16

        def act_qdq(x):
            qmax = 2.0 ** (ACT_BITS - 1) - 1.0
            scale = jnp.maximum(jnp.max(jnp.abs(x)) / qmax, 1e-12)
            return jnp.clip(jnp.round(x / scale), -qmax - 1.0, qmax) * scale

        def fixed_qdq_u16(x):
            scale = 1.0 / 65536.0
            return jnp.clip(jnp.round(x / scale), 0.0, 65535.0) * scale

        def lpbq_dequant(w):
            O, I = w.shape
            qmax = 2.0 ** (W_BITS - 1) - 1.0
            wb = w.reshape(O, I // BLOCK, BLOCK)
            s = jnp.maximum(jnp.max(jnp.abs(wb), axis=-1, keepdims=True) / qmax, 1e-12)
            wq = jnp.clip(jnp.round(wb / s), -qmax - 1.0, qmax) * s
            return wq.reshape(O, I)
        x = act_qdq(x)
        up = act_qdq(x @ lpbq_dequant(w_up).T)
        gate = act_qdq(x @ lpbq_dequant(w_gate).T)
        sig = fixed_qdq_u16(jax.nn.sigmoid(gate))
        gate = act_qdq(gate * sig)
        o = act_qdq(gate * up)
        return o @ lpbq_dequant(w_down).T
    x = x + jnp.tanh(g_xattn[0]) * _L0_xattn_ref(ctx_2048, _layernorm(x, axis=-1), L0_xattn_b, itok_Bx1_68_817)
    x = x + jnp.tanh(g_ffn[0]) * _L0_ffn_ref(_layernorm(x, axis=-1), L0_ffn_weight, L0_ffn_aux_weight1, L0_ffn_aux_weight2, L0_ffn_bias)
    x = x + jnp.tanh(g_xattn[1]) * _L1_xattn_ref(ctx_2048, _layernorm(x, axis=-1), mask_BxS2_ik0, L1_xattn_b)
    x = x + jnp.tanh(g_ffn[1]) * _L1_ffn_ref(_layernorm(x, axis=-1), L1_ffn_w_gate, L1_ffn_w_up, L1_ffn_w_down)
    return x

_drawn_inputs = setup_inputs


def setup_inputs(seed=0):
    import zlib

    import numpy as np

    out = dict(_drawn_inputs(seed))
    spreads = {'g_ffn': (-1.0, 0.2), 'L0_ffn_bias': (0.0, 0.1)}
    factors = {}
    for name, (base, spread) in spreads.items():
        noise = np.random.default_rng([zlib.crc32(name.encode()), seed]).standard_normal(out[name].shape)
        drawn = base * np.exp(spread * noise) if base else spread * noise
        out[name] = jnp.asarray(drawn.astype(out[name].dtype))
    for name, factor in factors.items():
        out[name] = (out[name] * factor).astype(out[name].dtype)
    return out
```

```python
from contextlib import ExitStack

import concourse.bass as bass
import numpy as np
from concourse import mybir

F32 = mybir.dt.float32
F32R = mybir.dt.float32r
BF16 = mybir.dt.bfloat16
F16 = mybir.dt.float16
I32 = mybir.dt.int32
I16 = mybir.dt.int16
U16 = mybir.dt.uint16
ALU = mybir.AluOpType
ACT = mybir.ActivationFunctionType
AX = mybir.AxisListType
RMAX = bass.bass_isa.ReduceOp.max

P = 128
B, S, D = 8, 512, 512
T = S // P
C = D // P
H0, H1 = 16, 8
DH0, DH1 = D // H0, D // H1
G = H0 // 4
OFF = 4
EPS = 1e-5
MASK0, MASK1 = 1e12, 1e30
BIG = 3e38

SEGMENTS = [(0, 0), (0, 1), (1, 0), (0, 2), (0, 3), (1, 1), (1, 2), (1, 3)]
UNITS = [(k, layer, t, h) for k, (layer, t) in enumerate(SEGMENTS) for h in range(H1 if layer else H0)]
NU = len(UNITS)
START = {seg: next(u for u, x in enumerate(UNITS) if x[0] == k) for k, seg in enumerate(SEGMENTS)}
END = {seg: START[seg] + (H1 if seg[0] else H0) for seg in SEGMENTS}
LAG_T, LAG_LO, LAG_PV = 1, 2, 3
ST = 3 * DH0
NORMS = ("q", "f", "y")
Q_SCALE = (-DH0 ** -0.5, -DH1 ** -0.5)


class Held:

    def __init__(self, sem):
        self.act, self.dve, self.pool, self.sp = (sem("held_" + e) for e in ("act", "dve", "pool", "sp"))


def bank_of(what):
    if what[0].endswith("_turn") and what[0] != "f_turn":
        return "ad"[what[2] % 2]
    if what[0] == "f_turn":
        return "a"
    return "d" if what[0] == "f_mm" and what[2] == 1 else None


def holds(what):
    return "d" if what[0] == "f_mm" else bank_of(what)


def schedule():
    at = {}

    def put(slot, *what):
        at.setdefault(slot, []).append(what)

    for t in range(T):
        e = END[0, t] + LAG_PV
        put(e, "end0", t)
        put(e + 1, "norm", "f", t)
        put(e + 3, "f_turn", t)
        put(e + 4, "f_mm", t, 0)
        put(e + 5, "f_mm", t, 1)
        put(e + 7, "f_out", t)
        put(e + 8, "norm", "q", (1, t))
        for g in range(G):
            put(e + 10 + g // 2, "q_turn", (1, t), g)
        e = END[1, t] + LAG_PV
        put(e, "end1", t)
        put(e + 1, "norm", "y", t)
        put(e + 2, "y_out", t)
        s = (START[0, t + 1] if t + 1 < T else NU) - 8
        put(s, "norm", "q", (0, t))
        for g in range(G):
            put(s + 3 + g // 2, "q_turn", (0, t), g)
    put(30, "bias")
    for kc in range(T):
        slot = 20 + 14 * kc
        put(slot, "kv_split", kc)
        slot += 3
        for g in range(G):
            slot += 1
            while any(holds(w) == "ad"[g % 2] for w in at.get(slot, [])):
                slot += 1
            put(slot, "k_turn", kc, g)
    for jobs in at.values():
        used = [holds(w) for w in jobs if holds(w)]
        assert len(used) == len(set(used)), jobs
    return at


AT = schedule()
JOBS = [w for s in sorted(AT) for w in AT[s]]
STEPS = max(AT) + 2
PROLOGUE = [("bias",)]
for _kc in range(T):
    PROLOGUE += [("kv_split", _kc)] + [("k_turn", _kc, g) for g in range(G)]
PROLOGUE += [("norm", "q", (0, T - 1))] + [("q_turn", (0, T - 1), g) for g in range(G)]


def number(want):
    return tuple({w: n for n, w in enumerate(w for w in jobs if want(w))} for jobs in (PROLOGUE, JOBS))


BANK_NO = {k: number(lambda w: bank_of(w) == k) for k in "ad"}
NORM_NO = {j: number(lambda w: w[:2] == ("norm", j)) for j in NORMS}
KV_NO = number(lambda w: w[0] == "kv_split")
BIAS_NO = number(lambda w: w[0] == "bias")


def jobs_at(slot):
    return [w for w in AT.get(slot - 1, []) if bank_of(w)] + [w for w in AT.get(slot, []) if not bank_of(w)]


class Place:

    def __init__(self, pair=None, par=0):
        self.pair, self.par = pair, par
        self.bi = None if pair is None else 2 * pair + par
        self.next_par = 0 if pair is None else 1 - par
        self.next_b = 0 if pair is None else (2 * pair + 1 if par == 0 else (2 * pair + 2) % B)

    def count(self, numbers, what, each=1, more=0):
        pre, per = numbers
        if self.bi is None:
            return OFF + each * pre[what] + more
        return self.bi * (each * len(per)) + each * (len(pre) + per[what]) + more + OFF

    def unit(self, u):
        return self.bi * NU + (u + 1 + OFF)

    def nth(self, per, k):
        return self.bi * per + (k + OFF)


def tile_of_q0(place, t):
    return (place.par, t + 1) if t + 1 < T else (place.next_par, 0)


def fold_weights(nc, sb, sem, dram, banks, ident, w_ffn):
    w_in = [sb(f"w_in{k}", [P, C, D], F32) for k in range(4)]
    w_leftT = sb("w_leftT", [P, C, P], F32)
    loaded = sem("w_loaded")
    turned = sem("w_turned")
    done = sem("w_done")
    moved = sem("w_moved")

    def pe_program(pe):
        pe.wait_ge(loaded, 16 * 4)
        for n in range(2 * C):
            left, right = (w_in[1], w_in[2]) if n < C else (w_in[0], w_in[3])
            if n:
                pe.wait_ge(moved, 2 * n - 1)
            for c in range(C):
                last = nc.tensor.transpose(banks[0][:, P * c:P * c + P], left[:, n % C, P * c:P * c + P], ident[:, :])
            last.then_inc(turned, 1)
            pe.wait_ge(moved, 2 * n + 1)
            for c in range(C):
                last = nc.tensor.matmul(banks[1][:, :], w_leftT[:, c, :], right[:, c, :], start=(c == 0), stop=(c == C - 1))
            last.then_inc(done, 1)

    def dve_program(dve):
        for n in range(2 * C):
            out = w_in[3] if n < C else w_ffn
            dve.wait_ge(turned, n + 1)
            if n:
                dve.wait_ge(done, n)
            nc.vector.tensor_copy(w_leftT[:, :, :].rearrange("p c i -> p (c i)"), banks[0][:, :]).then_inc(moved, 1)
            dve.wait_ge(done, n + 1)
            nc.vector.tensor_copy(out[:, n % C, :], banks[1][:, :]).then_inc(moved, 1)

    def sp_program(sp):
        sp.dma_start(ident[:, :], dram["ident"]).then_inc(loaded, 16)
        for k, name in ((1, "L0_ffn_aux_weight1"), (2, "L0_ffn_aux_weight2"), (0, "L0_ffn_weight")):
            sp.dma_start(w_in[k][:, :, :], dram[name].rearrange("(c p) d -> p c d", p=P)).then_inc(loaded, 16)

    def idle(_):
        pass

    return pe_program, idle, dve_program, idle, sp_program


def phase1(nc, sb, sem, held, dram, gates, banks, ident, w_ffn):
    iota = sb("iota", [P, S], F32)
    half = sb("half", [P, 1], F32)
    b0_row = sb("b0_row", [P, S], F32)
    b1_col = sb("b1_col", [P, 1], F32)
    ffn_bias = sb("ffn_bias", [P, D], F32)
    seq_i = sb("seq_i", [P, B], I32)
    seq_f = sb("seq_f", [P, B], F32)
    nbias = sb("nbias", [P, 2, 2, S], F32)
    x = sb("x", [P, 2, T, D], F32)
    kv = sb("kv", [P, 2, 2 * D], F32)
    kT = sb("kT", [P, 2, H0, S], F32R)
    v = sb("v", [P, 2, T, 3, D], BF16)
    v_rest = sb("v_rest", [P, D], F32)
    qT = [sb("q0T", [P, 2, H0, P], F32R), sb("q1T", [P, 2, H0, P], F32R)]
    parts = {j: sb("parts_" + j, [P, H0, 3, DH0], F32R) for j in ("q", "k")}
    xn = {j: sb("xn_" + j, [P, D], F32) for j in NORMS}
    stat = {j: sb("stat_" + j, [P, 6], F32) for j in NORMS}
    mv = {j: sb("mv_" + j, [P, 2], F32) for j in NORMS}
    rstd = {j: sb("rstd_" + j, [P, 3], F32) for j in NORMS}
    xnT = sb("xnT", [P, C, P], F32)
    f_out = sb("f_out", [P, D], F32)
    p = sb("p", [P, 2, S], F32)
    pT_hi = sb("pT_hi", [P, 3, S], F16)
    pT_lo = sb("pT_lo", [P, 2, S], F16)
    nmax = sb("nmax", [P, 4], F32)
    rsum = [sb("rsum0", [P, 2, H0], F32), sb("rsum1", [P, 2, H1], F32)]
    rinv = [sb("rinv0", [P, H0], F32), sb("rinv1", [P, H1], F32)]
    o_sb = [sb("o_sb0", [P, D], F32), sb("o_sb1", [P, D], F32)]
    ymax = sb("ymax", [P, T], F32)
    yall = dram["yall"]

    s_bank, pT_bank, o_bank, misc = banks[0:2], banks[2:4], banks[4:6], {"a": banks[6], "d": banks[7]}

    consts_in = sem("consts_in")
    gates_ready = sem("gates_ready")
    seq_ready = sem("seq_ready")
    x_in = [sem("x_in0"), sem("x_in1")]
    kv_in = [sem("kv_in0"), sem("kv_in1")]
    mask_in = sem("mask_in")
    x_store, y_store = sem("x_store"), sem("y_store")
    bias_step = sem("bias_step")
    s_ready = sem("s_ready")
    max_ready = sem("max_ready")
    exp_done = sem("exp_done")
    pT_ready = sem("pT_ready")
    hi_done = sem("hi_done")
    lo_done = sem("lo_done")
    pv_done = sem("pv_done")
    filled = {"a": sem("a_filled"), "d": sem("d_filled")}
    freed = {"a": sem("a_freed"), "d": sem("d_freed")}
    stats = {j: sem("stats_" + j) for j in NORMS}
    rs_step = {j: sem("rs_step_" + j) for j in NORMS}
    normed = {j: sem("normed_" + j) for j in NORMS}
    hi_part = {j: sem("hi_part_" + j) for j in parts}
    lo_part = {j: sem("lo_part_" + j) for j in parts}
    v_step = sem("v_step")
    end_step = [sem("end_step0"), sem("end_step1")]
    x_step = [sem("x_step0"), sem("x_step1")]
    f_tanh = sem("f_tanh")
    f_step = sem("f_step")
    y_max = sem("y_max")

    def mask_row(par):
        return nbias[:, par, 1, :].bitcast(I32)

    N_CONSTS = 16 * 7

    def x_tile(place, j, t):
        if j == "q":
            layer, t = t
            par, t = (place.par, t) if layer else tile_of_q0(place, t)
        else:
            par = place.par
        return x[:, par, t, :]

    def emptied(what, place):
        if what[0] == "f_turn":
            return xnT[:, :, :].rearrange("p c i -> p (c i)"), misc["a"][:, :]
        kind, a, g = what
        bank = misc[bank_of(what)][0:ST, :].rearrange("p (k i) -> p k i", k=4)
        if kind == "k_turn":
            return kT[0:ST, place.next_par, 4 * g:4 * g + 4, P * a:P * a + P], bank
        layer, t = a
        t = t if layer else tile_of_q0(place, t)[1]
        return qT[layer][0:ST, t % 2, 4 * g:4 * g + 4, :], bank

    def wait_turned(eng, place, j, what):
        jobs = PROLOGUE if place.bi is None else JOBS
        turns = [w for w in jobs if w[0] == j + "_turn"]
        before = [w for w in turns if jobs.index(w) < jobs.index(what)]
        if not before and place.bi is None:
            return
        for k in "ad":
            w = [w for w in (before or turns) if bank_of(w) == k][-1]
            n = place.count(BANK_NO[k], w, 1, 1)
            eng.wait_ge(filled[k], n if before else n - len(BANK_NO[k][1]))

    def pe_job(pe, place, what):
        kind, k = what[0], bank_of(what)
        if kind in ("q_turn", "k_turn"):
            j, g = kind[0], what[2]
            if g == 0:
                no, w = (KV_NO, ("kv_split", what[1])) if j == "k" else (NORM_NO[j], ("norm", j, what[1]))
                pe.wait_ge(hi_part[j], place.count(no, w, 1, 1))
                pe.wait_ge(lo_part[j], place.count(no, w, 1, 1))
            pe.wait_ge(freed[k], place.count(BANK_NO[k], what))
            for n in range(4):
                h = 4 * g + n
                src = parts[j][:, h, :, :].bitcast(F32).rearrange("p a d -> p (a d)")
                last = nc.tensor.transpose(misc[k][0:ST, P * n:P * n + P], src, ident[:, :])
            last.then_inc(filled[k], 1)
        elif kind == "f_turn":
            pe.wait_ge(normed["f"], place.count(NORM_NO["f"], ("norm", "f", what[1]), 1, 1))
            pe.wait_ge(freed["a"], place.count(BANK_NO["a"], what))
            for c in range(C):
                last = nc.tensor.transpose(misc["a"][:, P * c:P * c + P], xn["f"][:, P * c:P * c + P], ident[:, :])
            last.then_inc(filled["a"], 1)
        elif kind == "f_mm":
            if what[2] == 0:
                pe.wait_ge(freed["a"], place.count(BANK_NO["a"], ("f_turn", what[1]), 1, 1))
                pe.wait_ge(freed["d"], place.count(BANK_NO["d"], ("f_mm", what[1], 1)))
            for c in range(2 * what[2], 2 * what[2] + 2):
                last = nc.tensor.matmul(misc["d"][:, :], xnT[:, c, :], w_ffn[:, c, :], start=(c == 0), stop=(c == C - 1))
            if what[2] == 1:
                last.then_inc(filled["d"], 1)

    def pe_scores(pe, place, u):
        _, layer, t, h = UNITS[u]
        if h == 0:
            job = t if layer else t - 1
            for k, g in (("a", G - 2), ("d", G - 1)):
                if job >= 0:
                    pe.wait_ge(freed[k], place.count(BANK_NO[k], ("q_turn", (layer, job), g), 1, 1))
                else:
                    pe.wait_ge(freed[k], place.bi * len(BANK_NO[k][1]) + (len(BANK_NO[k][0]) + OFF))
            if u == 0:
                pe.wait_ge(v_step, place.bi * (4 * T) + (4 * T + OFF))
        pe.wait_ge(exp_done, place.unit(u - 2))
        stacks = [2 * h, 2 * h + 1] if layer else [h]
        for n, k in enumerate(stacks):
            last = nc.tensor.matmul(s_bank[u % 2][:, :], qT[layer][0:ST, t % 2, k, :],
                                    kT[0:ST, place.par, k, :], start=(n == 0), stop=(n == len(stacks) - 1))
        last.then_inc(s_ready, 1)

    def pe_turn(pe, place, u):
        pe.wait_ge(exp_done, place.unit(u))
        pe.wait_ge(lo_done, place.unit(u - 2))
        for c in range(T):
            last = nc.tensor.transpose(pT_bank[u % 2][:, P * c:P * c + P], p[:, u % 2, P * c:P * c + P], ident[:, :])
        last.then_inc(pT_ready, 1)

    def pe_values(pe, place, u):
        k, layer, t, h = UNITS[u]
        dh = DH1 if layer else DH0
        if h == 0:
            was = SEGMENTS[k - 2]
            pe.wait_ge(end_step[was[0]], place.nth(3 * T, 3 * was[1] + 3 - (3 * T if k < 2 else 0)))
        pe.wait_ge(lo_done, place.unit(u))
        terms = [(c, part, n) for c in range(T) for part, n in ((0, 0), (0, 1), (0, 2), (1, 0), (1, 1))]
        for i, (c, part, n) in enumerate(terms):
            pT = pT_lo[:, u % 2, :] if part else pT_hi[:, u % 3, :]
            last = nc.tensor.matmul(o_bank[k % 2][:, dh * h:dh * h + dh], pT[:, P * c:P * c + P],
                                    v[:, place.par, c, n, dh * h:dh * h + dh], start=(i == 0), stop=(i == len(terms) - 1))
        last.then_inc(pv_done, 1)

    def pe_program(pe):
        for s in (s_ready, pT_ready, pv_done, *filled.values()):
            pe.sem_inc(s, OFF)
        pe.wait_ge(consts_in, N_CONSTS)
        for what in PROLOGUE:
            pe_job(pe, Place(), what)
        with pe.Fori(0, B // 2) as pair:
            for par in (0, 1):
                place = Place(pair, par)
                for s in range(STEPS):
                    if s < NU:
                        pe_scores(pe, place, s)
                    if 0 <= s - LAG_T < NU:
                        pe_turn(pe, place, s - LAG_T)
                    for what in AT.get(s, []):
                        pe_job(pe, place, what)
                    if 0 <= s - LAG_PV < NU:
                        pe_values(pe, place, s - LAG_PV)

    def act_job(act, place, what):
        kind = what[0]
        if kind == "norm" and what[1] in parts:
            j = what[1]
            act.wait_ge(normed[j], place.count(NORM_NO[j], what, 1, 1))
            wait_turned(act, place, j, what)
            split_high(j, xn[j][:, :])
        elif kind == "kv_split":
            kc = what[1]
            act.wait_ge(kv_in[kc % 2], kv_loaded(place, kc))
            wait_turned(act, place, "k", what)
            split_high("k", kv[:, kc % 2, 0:D])
        elif bank_of(what) == "a":
            act.wait_ge(filled["a"], place.count(BANK_NO["a"], what, 1, 1))
            if kind == "f_turn":
                act.wait_ge(filled["d"], place.count(BANK_NO["d"], ("f_mm", what[1], 1)))
            out, bank = emptied(what, place)
            nc.scalar.activation(out, bank, ACT.Copy).then_inc(freed["a"], 1)
        elif kind == "f_out":
            act.wait_ge(freed["d"], place.count(BANK_NO["d"], ("f_mm", what[1], 1), 1, 1))
            nc.scalar.activation(f_out[:, :], f_out[:, :], ACT.Tanh).then_inc(f_tanh, 1)

    def high_and_low(j):
        if j == "k":
            return parts[j][:, :, 0:2, :], parts[j][:, :, 2, :]
        return parts[j][:, :, 0:3:2, :], parts[j][:, :, 1, :]

    def split_high(j, src):
        src = src.rearrange("p (h d) -> p h d", h=H0).unsqueeze(2).broadcast_to([P, H0, 2, DH0])
        nc.scalar.activation(high_and_low(j)[0], src, ACT.Copy).then_inc(hi_part[j], 1)

    def kv_loaded(place, kc):
        n = kc // 2 + 1
        return 16 * n if place.bi is None else place.bi * 32 + 16 * (2 + n)

    def act_exp(act, place, u):
        _, layer, t, h = UNITS[u]
        act.wait_ge(max_ready, place.unit(u))
        act.wait_ge(pT_ready, place.unit(u - 2))
        if h == 0:
            act.wait_ge(end_step[layer], place.nth(3 * T, 3 * t - 3))
        nc.scalar.activation(p[:, u % 2, :], s_bank[u % 2][:, :], ACT.Exp, bias=nmax[:, u % 4:u % 4 + 1], scale=-1.0,
                             accum_out=rsum[layer][:, t % 2, h:h + 1]).then_inc(exp_done, 1)

    def act_hi(act, place, u):
        act.wait_ge(pT_ready, place.unit(u))
        act.wait_ge(pv_done, place.unit(u - 3))
        nc.scalar.activation(pT_hi[:, u % 3, :], pT_bank[u % 2][:, :], ACT.Copy).then_inc(hi_done, 1)

    def act_program(act):
        for s in (exp_done, hi_done, freed["a"], *hi_part.values(), f_tanh):
            act.sem_inc(s, OFF)
        act.wait_ge(consts_in, N_CONSTS)
        nc.scalar.activation(gates[:, :], gates[:, :], ACT.Tanh).then_inc(gates_ready, 1)
        for what in PROLOGUE:
            act_job(act, Place(), what)
        with act.Fori(0, B // 2) as pair:
            for par in (0, 1):
                place = Place(pair, par)
                for s in range(STEPS):
                    if s < NU:
                        act_exp(act, place, s)
                    if 0 <= s - LAG_T < NU:
                        act_hi(act, place, s - LAG_T)
                    for what in jobs_at(s):
                        act_job(act, place, what)

    def dve_max(dve, place, u):
        _, layer, t, h = UNITS[u]
        dve.wait_ge(s_ready, place.unit(u))
        dve.wait_ge(exp_done, place.unit(u - 4))
        dve.sem_inc(held.dve, 1)
        out = s_bank[u % 2][:, :]
        nc.vector.tensor_tensor_reduce(out, out, nbias[:, place.par, layer, :], 1.0, BIG, ALU.add, ALU.min,
                                       nmax[:, u % 4:u % 4 + 1]).then_inc(max_ready, 1)

    def dve_lo(dve, place, u):
        dve.wait_ge(hi_done, place.unit(u))
        dve.wait_ge(pv_done, place.unit(u - 2))
        nc.vector.tensor_tensor(pT_lo[:, u % 2, :], pT_bank[u % 2][:, :], pT_hi[:, u % 3, :],
                                ALU.subtract).then_inc(lo_done, 1)

    def dve_job(dve, place, what):
        kind = what[0]
        if kind == "norm":
            j, t = what[1:]
            if j == "q" and t == (0, T - 1):
                par = place.next_par
                if place.bi is None:
                    dve.wait_ge(x_in[0], 16)
                else:
                    dve.wait_ge(x_in[par], place.pair * 16 + (16 if par else 32))
            elif j == "f":
                dve.wait_ge(x_step[0], place.nth(T, t + 1))
            elif j == "q" and t[0] == 1:
                dve.wait_ge(f_step, place.nth(2 * T, 2 * t[1] + 2))
            elif j == "y":
                dve.wait_ge(x_step[1], place.nth(T, t + 1))
            dve.wait_ge(normed[j], place.count(NORM_NO[j], what))
            nc.vector.bn_stats(stat[j][:, :], x_tile(place, j, t)).then_inc(stats[j], 1)
            dve.wait_ge(stats[j], place.count(NORM_NO[j], what, 2, 1))
            dve.sem_inc(held.dve, 1)
            nc.vector.bn_aggr(mv[j][:, :], stat[j][:, :]).then_inc(stats[j], 1)
        elif bank_of(what) == "d" and kind != "f_mm":
            dve.wait_ge(filled["d"], place.count(BANK_NO["d"], what, 1, 1))
            out, bank = emptied(what, place)
            nc.vector.tensor_copy(out, bank).then_inc(freed["d"], 1)
        elif kind in ("end0", "end1"):
            layer, t = int(kind[3]), what[1]
            dh, heads = (DH1, H1) if layer else (DH0, H0)
            k, u = SEGMENTS.index((layer, t)), END[layer, t] - 1
            dve.wait_ge(exp_done, place.unit(u))
            nc.vector.reciprocal(rinv[layer][:, :], rsum[layer][:, t % 2, :]).then_inc(end_step[layer], 1)
            dve.wait_ge(end_step[layer], place.nth(3 * T, 3 * t + 1))
            nc.vector.tensor_scalar(rinv[layer][:, :], rinv[layer][:, :], gates[:, layer:layer + 1], None,
                                    ALU.mult).then_inc(end_step[layer], 1)
            dve.wait_ge(end_step[layer], place.nth(3 * T, 3 * t + 2))
            dve.wait_ge(pv_done, place.unit(u))
            dve.wait_ge(x_step[layer], place.nth(T, t))
            nc.vector.tensor_tensor(o_sb[layer][:, :].rearrange("p (h d) -> p h d", h=heads),
                                    o_bank[k % 2][:, :].rearrange("p (h d) -> p h d", h=heads),
                                    rinv[layer][:, :].unsqueeze(2).broadcast_to([P, heads, dh]),
                                    ALU.mult).then_inc(end_step[layer], 1)
        elif kind == "f_mm" and what[2] == 1:
            dve.wait_ge(filled["d"], place.count(BANK_NO["d"], what, 1, 1))
            dve.wait_ge(f_step, place.nth(2 * T, 2 * what[1]))
            nc.vector.tensor_tensor(f_out[:, :], misc["d"][:, :], ffn_bias[:, :], ALU.add).then_inc(freed["d"], 1)
        elif kind == "y_out":
            t = what[1]
            dve.wait_ge(normed["y"], place.count(NORM_NO["y"], ("norm", "y", t), 1, 1))
            nc.vector.tensor_reduce(yall[:, bass.ds(place.bi * T + t, 1)], xn["y"][:, :], AX.X, ALU.max,
                                    apply_absolute_value=True).then_inc(y_max, 1)
        elif kind == "bias":
            par = place.next_par
            col = seq_f[:, 0:1] if place.bi is None else seq_f[:, bass.ds(place.next_b, 1)]
            dve.wait_ge(mask_in, 16 if place.bi is None else place.bi * 16 + 32)
            nc.vector.tensor_scalar(nbias[:, par, 0, :], iota[:, :], col, MASK0, ALU.is_ge, ALU.mult).then_inc(bias_step, 1)
            nc.vector.tensor_scalar(nbias[:, par, 1, :], mask_row(par), -MASK1, MASK1, ALU.mult, ALU.add).then_inc(bias_step, 1)
            dve.wait_ge(bias_step, place.count(BIAS_NO, what, 4, 2))
            nc.vector.tensor_tensor(nbias[:, par, 0, :], nbias[:, par, 0, :], b0_row[:, :], ALU.subtract).then_inc(bias_step, 1)
            nc.vector.tensor_scalar(nbias[:, par, 1, :], nbias[:, par, 1, :], b1_col[:, 0:1], None,
                                    ALU.subtract).then_inc(bias_step, 1)
            dve.wait_ge(bias_step, place.count(BIAS_NO, what, 4, 4))

    def dve_program(dve):
        for s in (max_ready, lo_done, freed["d"], *stats.values(), y_max, bias_step):
            dve.sem_inc(s, OFF)
        for s in end_step:
            dve.sem_inc(s, OFF)
        dve.wait_ge(consts_in, N_CONSTS)
        nc.vector.tensor_copy(seq_f[:, :], seq_i[:, :]).then_inc(seq_ready, 1)
        nc.vector.memset(half[:, :], -0.5).then_inc(seq_ready, 1)
        dve.wait_ge(seq_ready, 2)
        dve.wait_ge(gates_ready, 1)
        for what in PROLOGUE:
            dve_job(dve, Place(), what)
        with dve.Fori(0, B // 2) as pair:
            for par in (0, 1):
                place = Place(pair, par)
                for s in range(STEPS):
                    if s < NU:
                        dve_max(dve, place, s)
                    if 0 <= s - LAG_LO < NU:
                        dve_lo(dve, place, s - LAG_LO)
                    for what in jobs_at(s):
                        dve_job(dve, place, what)

    def split_low(pool, place, j, numbers, what, src):
        pool.wait_ge(hi_part[j], place.count(numbers, what, 1, 1))
        high, low = high_and_low(j)
        nc.gpsimd.tensor_tensor(low, src.rearrange("p (h d) -> p h d", h=H0), high[:, :, 0, :].bitcast(F32),
                                ALU.subtract).then_inc(lo_part[j], 1)

    def pool_job(pool, place, what):
        kind = what[0]
        if kind == "norm":
            j, t = what[1:]
            n = NORM_NO[j]
            pool.wait_ge(stats[j], place.count(n, what, 2, 2))
            pool.wait_ge(normed[j], place.count(n, what))
            pool.sem_inc(held.pool, 1)
            nc.gpsimd.tensor_scalar(rstd[j][:, 0:1], mv[j][:, 1:2], EPS, None, ALU.add).then_inc(rs_step[j], 1)
            pool.wait_ge(rs_step[j], place.count(n, what, 3, 1))
            nc.gpsimd.tensor_tensor(rstd[j][:, 1:2], rstd[j][:, 0:1], half[:, :], ALU.pow).then_inc(rs_step[j], 1)
            pool.wait_ge(rs_step[j], place.count(n, what, 3, 2))
            pool.sem_inc(held.pool, 1)
            nc.gpsimd.tensor_scalar(rstd[j][:, 2:3], rstd[j][:, 1:2], Q_SCALE[t[0]] if j == "q" else 1.0, None,
                                    ALU.mult).then_inc(rs_step[j], 1)
            pool.wait_ge(rs_step[j], place.count(n, what, 3, 3))
            if j in parts:
                pool.wait_ge(lo_part[j], place.count(n, what))
            elif j == "f":
                pool.wait_ge(filled["a"], place.count(BANK_NO["a"], ("f_turn", (t - 1) % T), 1, 1 - (len(BANK_NO["a"][1]) if t == 0 else 0)))
            else:
                pool.wait_ge(y_max, place.count(n, what))
                pool.wait_ge(y_store, place.bi * (16 * T) + 16 * (t + 1))
            pool.sem_inc(held.pool, 1)
            nc.gpsimd.tensor_scalar(xn[j][:, :], x_tile(place, j, t), mv[j][:, 0:1], rstd[j][:, 2:3], ALU.subtract,
                                    ALU.mult).then_inc(normed[j], 1)
            if j in parts:
                pool.wait_ge(normed[j], place.count(n, what, 1, 1))
                split_low(pool, place, j, n, what, xn[j][:, :])
        elif kind == "kv_split":
            kc = what[1]
            pool.wait_ge(kv_in[kc % 2], kv_loaded(place, kc))
            split_low(pool, place, "k", KV_NO, what, kv[:, kc % 2, 0:D])
            vals, out = kv[:, kc % 2, D:2 * D], v[:, place.next_par, kc]
            if place.bi is not None:
                pool.wait_ge(pv_done, place.unit(-1))
            pool.sem_inc(held.pool, 1)
            nc.gpsimd.tensor_scalar(out[:, 0, :], vals, 1.0, 1.0, ALU.mult, ALU.mult).then_inc(v_step, 1)
            pool.wait_ge(v_step, place.count(KV_NO, what, 4, 1))
            nc.gpsimd.tensor_tensor(v_rest[:, :], vals, out[:, 0, :], ALU.subtract).then_inc(v_step, 1)
            pool.wait_ge(v_step, place.count(KV_NO, what, 4, 2))
            pool.sem_inc(held.pool, 1)
            nc.gpsimd.tensor_scalar(out[:, 1, :], v_rest[:, :], 1.0, 1.0, ALU.mult, ALU.mult).then_inc(v_step, 1)
            pool.wait_ge(v_step, place.count(KV_NO, what, 4, 3))
            nc.gpsimd.tensor_tensor(out[:, 2, :], v_rest[:, :], out[:, 1, :], ALU.subtract).then_inc(v_step, 1)
            pool.wait_ge(v_step, place.count(KV_NO, what, 4, 4))
        elif kind in ("end0", "end1"):
            layer, t = int(kind[3]), what[1]
            xt = x[:, place.par, t, :]
            pool.wait_ge(end_step[layer], place.nth(3 * T, 3 * t + 3))
            nc.gpsimd.tensor_tensor(xt, xt, o_sb[layer][:, :], ALU.add).then_inc(x_step[layer], 1)
        elif kind == "f_out":
            t = what[1]
            xt = x[:, place.par, t, :]
            pool.wait_ge(f_tanh, place.nth(T, t + 1))
            pool.sem_inc(held.pool, 1)
            nc.gpsimd.tensor_scalar(f_out[:, :], f_out[:, :], gates[:, 2:3], 1.0, ALU.mult, ALU.mult).then_inc(f_step, 1)
            pool.wait_ge(f_step, place.nth(2 * T, 2 * t + 1))
            nc.gpsimd.tensor_tensor(xt, xt, f_out[:, :], ALU.add).then_inc(f_step, 1)

    def pool_program(pool):
        for s in (*rs_step.values(), *normed.values(), *lo_part.values(), v_step, *x_step, f_step):
            pool.sem_inc(s, OFF)
        pool.wait_ge(seq_ready, 2)
        pool.wait_ge(gates_ready, 1)
        for what in PROLOGUE:
            pool_job(pool, Place(), what)
        with pool.Fori(0, B // 2) as pair:
            for par in (0, 1):
                place = Place(pair, par)
                for s in range(STEPS):
                    for what in AT.get(s, []):
                        pool_job(pool, place, what)

    def rows(ap, b):
        return ap[b].rearrange("(t p) d -> p t d", p=P)

    def spread(ap, n):
        return ap.partition_broadcast(P)

    def sp_program(sp):
        sp.sem_inc(x_store, 16)
        sp.sem_inc(y_store, 16)
        sp.dma_start(iota[:, :], dram["iota"].partition_broadcast(P)).then_inc(consts_in, 16)
        sp.dma_start(b0_row[:, :], dram["L0_xattn_b"].partition_broadcast(P)).then_inc(consts_in, 16)
        sp.dma_start(b1_col[:, :], dram["L1_xattn_b"].partition_broadcast(P)).then_inc(consts_in, 16)
        sp.dma_start(ffn_bias[:, :], dram["L0_ffn_bias"].partition_broadcast(P)).then_inc(consts_in, 16)
        sp.dma_start(seq_i[:, :], dram["itok_Bx1_68_817"].rearrange("b o -> (b o)").partition_broadcast(P)).then_inc(consts_in, 16)
        sp.dma_start(gates[:, 0:2], dram["g_xattn"].partition_broadcast(P)).then_inc(consts_in, 16)
        sp.dma_start(gates[:, 2:4], dram["g_ffn"].partition_broadcast(P)).then_inc(consts_in, 16)
        sp.dma_start(x[:, 0, :, :], rows(dram["x"], 0)).then_inc(x_in[0], 16)
        sp.dma_start(mask_row(0), dram["mask_BxS2_ik0"][0].partition_broadcast(P)).then_inc(mask_in, 16)
        for kc in range(T):
            load_kv(sp, Place(), kc)
        with sp.Fori(0, B // 2) as pair:
            for par in (0, 1):
                place = Place(pair, par)
                sp.wait_ge(x_store, place.bi * (16 * T) + 16)
                sp.wait_ge(x_step[1], place.nth(T, 0))
                sp.dma_start(x[:, 1 - par, :, :], rows(dram["x"], place.next_b)).then_inc(x_in[1 - par], 16)
                sp.wait_ge(max_ready, place.unit(-1))
                sp.dma_start(mask_row(1 - par), dram["mask_BxS2_ik0"][place.next_b].partition_broadcast(P)).then_inc(mask_in, 16)
                for what in JOBS:
                    if what[0] == "kv_split":
                        load_kv(sp, place, what[1])
                    elif what[0] == "y_out":
                        t = what[1]
                        sp.wait_ge(x_step[1], place.nth(T, t + 1))
                        sp.dma_start(dram["x_mid"][place.bi * T + t], x[:, par, t, :]).then_inc(x_store, 16)
                        sp.wait_ge(normed["y"], place.count(NORM_NO["y"], ("norm", "y", t), 1, 1))
                        sp.dma_start(dram["y_mid"][place.bi * T + t], xn["y"][:, :]).then_inc(y_store, 16)
        sp.wait_ge(x_store, 16 * (B * T + 1))
        sp.wait_ge(y_store, 16 * (B * T + 1))

    def load_kv(sp, place, kc):
        if place.bi is not None or kc >= 2:
            what = ("kv_split", kc)
            sp.wait_ge(hi_part["k"], place.count(KV_NO, what, 1, -1))
            sp.sem_inc(held.sp, 1)
            sp.wait_ge(v_step, place.count(KV_NO, what, 4, -4))
        sp.dma_start(kv[:, kc % 2, :], dram["ctx_2048"][place.next_b, P * kc:P * kc + P, :]).then_inc(kv_in[kc % 2], 16)

    return pe_program, act_program, dve_program, pool_program, sp_program


I = 1536
N_BLK = B * S // 512
IT = I // P
PAIRS = IT // 2
GROUPS = IT // 4
QMAX = 32767.0
WMAX = 7.0
WBLK = 32
SIG = 65536.0
ROUND = 1.5 * 2 ** 23
TINY = 1e-12
SCALARS = ("x_scale", "x_inv", "gate_scale", "gate_c", "g2_unit", "g2_scale", "g2_c", "up_scale", "up_c",
           "o_unit", "o_scale", "o_c", "out_factor")


class Turns:

    def __init__(self, nc, sb, sem, held, name, banks, ident):
        self.nc, self.held, self.banks, self.ident = nc, held, banks, ident
        self.raw = sb(name + "_raw", [P, 2, D], F32)
        self.src = sb(name + "_src", [P, 2, D], F32)
        self.size = sb(name + "_size", [P, 2, D // WBLK], F32)
        self.scale = sb(name + "_scale", [P, 2, D // WBLK], F32)
        self.inv = sb(name + "_inv", [P, 2, D // WBLK], F32)
        self.loaded = [sem(name + "_loaded0"), sem(name + "_loaded1")]
        self.w_step = sem(name + "_w_step")
        self.quantised = sem(name + "_quantised")
        self.restored = sem(name + "_restored")
        self.turned = sem(name + "_turned")
        self.high = sem(name + "_high")
        self.low = sem(name + "_low")

    def load(self, sp, n, k, source):
        sp.wait_ge(self.restored, n - 1 + OFF)
        sp.dma_start(self.raw[:, k, :], source).then_inc(self.loaded[k], 16)

    def quantise_x(self, dve, n, half_n, k, x_inv):
        dve.wait_ge(self.loaded[k], 16 * half_n + 16)
        self.nc.vector.tensor_scalar(self.raw[:, k, :], self.raw[:, k, :], x_inv[:, 0:1], ROUND,
                                     ALU.mult, ALU.add).then_inc(self.quantised, 1)

    def quantise_w(self, dve, n, half_n, n4, k):
        size, scale, inv = self.size[:, k, :], self.scale[:, k, :], self.inv[:, k, :]
        dve.wait_ge(self.loaded[k], 16 * half_n + 16)
        self.nc.vector.tensor_reduce(size, self.raw[:, k, :].rearrange("p (b w) -> p b w", w=WBLK), AX.X, ALU.max,
                                     apply_absolute_value=True).then_inc(self.w_step, 1)
        dve.wait_ge(self.restored, n - 1 + OFF)
        dve.wait_ge(self.w_step, n4 + 1 + OFF)
        self.nc.vector.tensor_scalar(scale, size, 1.0 / WMAX, TINY, ALU.mult, ALU.max).then_inc(self.w_step, 1)
        dve.wait_ge(self.w_step, n4 + 2 + OFF)
        self.nc.vector.reciprocal(inv, scale).then_inc(self.w_step, 1)
        dve.wait_ge(self.w_step, n4 + 3 + OFF)
        blocks = self.raw[:, k, :].rearrange("p (b w) -> p b w", w=WBLK)
        self.nc.vector.tensor_tensor(blocks, blocks, inv.unsqueeze(2).broadcast_to([P, D // WBLK, WBLK]),
                                     ALU.mult).then_inc(self.w_step, 1)
        dve.wait_ge(self.w_step, n4 + 4 + OFF)
        self.nc.vector.tensor_scalar(self.raw[:, k, :], self.raw[:, k, :], ROUND, -ROUND, ALU.add,
                                     ALU.add).then_inc(self.quantised, 1)

    def restore_x(self, pool, n, k):
        pool.wait_ge(self.quantised, n + 1 + OFF)
        pool.wait_ge(self.turned, n - 1 + OFF)
        pool.sem_inc(self.held.pool, 1)
        self.nc.gpsimd.tensor_scalar(self.src[:, k, :], self.raw[:, k, :], -ROUND, 1.0, ALU.add,
                                     ALU.mult).then_inc(self.restored, 1)

    def restore_w(self, pool, n, k):
        pool.wait_ge(self.quantised, n + 1 + OFF)
        pool.wait_ge(self.turned, n - 1 + OFF)
        self.nc.gpsimd.tensor_tensor(self.src[:, k, :].rearrange("p (b w) -> p b w", w=WBLK),
                                     self.raw[:, k, :].rearrange("p (b w) -> p b w", w=WBLK),
                                     self.scale[:, k, :].unsqueeze(2).broadcast_to([P, D // WBLK, WBLK]),
                                     ALU.mult).then_inc(self.restored, 1)

    def transpose(self, pe, n, k):
        pe.wait_ge(self.restored, n + 1 + OFF)
        pe.wait_ge(self.low, n - 1 + OFF)
        for c in range(4):
            last = self.nc.tensor.transpose(self.banks[k][:, P * c:P * c + P], self.src[:, k, P * c:P * c + P],
                                            self.ident[:, :])
        last.then_inc(self.turned, 1)

    def put_high(self, act, n, k, out):
        act.wait_ge(self.turned, n + 1 + OFF)
        act.sem_inc(self.held.act, 1)
        self.nc.scalar.activation(out, self.banks[k][:, :].rearrange("p (c i) -> p c i", i=P),
                                  ACT.Copy).then_inc(self.high, 1)

    def put_low(self, dve, n, k, out, high):
        dve.wait_ge(self.high, n + 1 + OFF)
        self.nc.vector.tensor_tensor(out, self.banks[k][:, :].rearrange("p (c i) -> p c i", i=P),
                                     high.bitcast(F32), ALU.subtract).then_inc(self.low, 1)

    def start(self, engines):
        for eng, s in (("dve", self.quantised), ("dve", self.w_step), ("dve", self.low), ("pool", self.restored),
                       ("pe", self.turned), ("act", self.high)):
            if eng in engines:
                engines[eng].sem_inc(s, OFF)


class Scales:

    def __init__(self, nc, sem, name):
        self.nc, self.step, self.n = nc, sem(name), 0

    def then(self, dve, inst):
        inst.then_inc(self.step, 1)
        self.n += 1
        dve.wait_ge(self.step, self.n)

    def mult(self, dve, out, a, b):
        self.then(dve, self.nc.vector.tensor_scalar(out[:, 0:1], a[:, 0:1], b if isinstance(b, float) else b[:, 0:1],
                                                    None, ALU.mult))

    def scale(self, dve, scale, size, unit, c):
        self.mult(dve, c, size, unit)
        self.then(dve, self.nc.vector.tensor_scalar(scale[:, 0:1], c[:, 0:1], 1.0 / QMAX, TINY, ALU.mult, ALU.max))
        self.then(dve, self.nc.vector.reciprocal(c[:, 0:1], scale[:, 0:1]))
        self.mult(dve, c, c, unit)


def quantised_products(nc, sb, sem, held, dram, banks, ident, sc, w_hl, name, acc_name, gate_q, weights, gates):
    up = gate_q is not None
    turns = Turns(nc, sb, sem, held, name, [banks[6], banks[7]], ident)
    acc = [(banks[2 * k], banks[2 * k + 1]) for k in range(3)]
    x_hl = sb(name + "_x_hl", [P, 2, 2, C, 512], F32R)
    out = sb(name + "_out", [P, 2, 2, 512], F32)
    cols = sb(name + "_cols", [P, N_BLK * PAIRS], F32)
    tops = sb(name + "_tops", [P, 4], F32)
    acc_ready, acc_out, acc_max = sem(name + "_acc_ready"), sem(name + "_acc_out"), sem(name + "_acc_max")
    stored = [sem(name + "_stored0"), sem(name + "_stored1")]
    col_top, top = sem(name + "_col_top"), sem(name + "_top")
    scalars_ready = sem(name + "_scalars_ready")
    scales = Scales(nc, sem, name + "_scales")
    n_weights = 12 * len(weights)
    if up:
        work = sb(name + "_work", [P, 2, 1024], F32)
        cols2 = sb(name + "_cols2", [P, N_BLK * PAIRS], F32)
        gate_in = [sem(name + "_gate_in0"), sem(name + "_gate_in1")]
        gate_done, sigmoid_done = sem(name + "_gate_done"), sem(name + "_sigmoid_done")
        sig_step = sem(name + "_sig_step")
        g2_done, g2_max = sem(name + "_g2_done"), sem(name + "_g2_max")

    def w_dst(m, part, i):
        return weights[m][1][:, part, :, bass.ds(i * P, P)]

    def x_dst(par, part, j):
        return x_hl[:, par, part, :, P * j:P * j + P]

    def x_items(blk, next_par):
        return [(j + 1, n_weights + 4 * blk + 4 + j, 2 * blk + (n_weights + 4 + j) // 2, j % 2, j) for j in range(4)]

    def each_block(eng, body):
        with eng.Fori(0, N_BLK // 2) as two:
            for par in (0, 1):
                body(2 * two + par, par)

    def first_x():
        return [(n_weights + j, (n_weights + j) // 2, j % 2, j) for j in range(4)]

    def sp_program(sp):
        for m, (w, _) in enumerate(weights):
            with sp.Fori(0, 3) as r:
                for k in range(4):
                    turns.load(sp, 12 * m + 4 * r + k, k % 2, w[bass.ds((4 * r + k) * P, P), :])
        for n, half_n, k, j in first_x():
            turns.load(sp, n, k, dram["y_mid"][j])

        def block(blk, par):
            items = {s: rest for s, *rest in x_items(blk, 1 - par)}
            for s in range(PAIRS):
                u = blk * PAIRS + s
                if s in items:
                    n, _, k, j = items[s]
                    turns.load(sp, n, k, dram["y_mid"][((blk + 1) % N_BLK) * 4 + j])
                if up:
                    sp.wait_ge(g2_max, u - 1 + OFF)
                    sp.dma_start(work[:, s % 2, :], dram["gate"][u]).then_inc(gate_in[s % 2], 16)
                sp.wait_ge(acc_out, u + 1 + OFF)
                sp.dma_start(dram[acc_name][u], out[:, s % 2, :, :].rearrange("p a i -> p (a i)")).then_inc(stored[s % 2], 16)

        for s in stored:
            sp.sem_inc(s, 16)
        each_block(sp, block)
        for s in stored:
            sp.wait_ge(s, 16 * (N_BLK * PAIRS // 2 + 1))

    def pe_program(pe):
        turns.start({"pe": pe})
        pe.sem_inc(acc_ready, OFF)
        for m in range(len(weights)):
            with pe.Fori(0, 3) as r:
                for k in range(4):
                    turns.transpose(pe, 12 * m + 4 * r + k, k % 2)
        for n, _, k, j in first_x():
            turns.transpose(pe, n, k)
        pe.wait_ge(turns.low, n_weights + OFF)

        def block(blk, par):
            items = {s: rest for s, *rest in x_items(blk, 1 - par)}
            pe.wait_ge(turns.high, n_weights + 4 * blk + 4 + OFF)
            pe.wait_ge(turns.low, n_weights + 4 * blk + 4 + OFF)
            for s in range(PAIRS):
                u = blk * PAIRS + s
                pe.wait_ge(acc_out, u - 2 + OFF)
                pe.wait_ge(acc_max, u - 2 + OFF)
                for half in (0, 1):
                    i = 2 * s + half
                    terms = [(a, b, c) for a, b in ((0, 0), (0, 1), (1, 0)) for c in range(C)]
                    for t, (a, b, c) in enumerate(terms):
                        last = nc.tensor.matmul(acc[s % 3][half][:, :], w_hl[:, a, c, P * i:P * i + P],
                                                x_hl[:, par, b, c, :], start=(t == 0), stop=(t == len(terms) - 1))
                last.then_inc(acc_ready, 1)
                if s in items:
                    n, _, k, j = items[s]
                    turns.transpose(pe, n, k)

        each_block(pe, block)

    def act_program(act):
        turns.start({"act": act})
        act.sem_inc(acc_out, OFF)
        if up:
            act.sem_inc(gate_done, OFF)
            act.sem_inc(sigmoid_done, OFF)
        for m in range(len(weights)):
            with act.Fori(0, 3) as r:
                for k in range(4):
                    turns.put_high(act, 12 * m + 4 * r + k, k % 2, w_dst(m, 0, 4 * r + k))
        for n, _, k, j in first_x():
            turns.put_high(act, n, k, x_dst(0, 0, j))

        def block(blk, par):
            items = {s: rest for s, *rest in x_items(blk, 1 - par)}
            for s in range(PAIRS):
                u = blk * PAIRS + s
                if s in items:
                    n, _, k, j = items[s]
                    act.wait_ge(acc_ready, 6 * blk + OFF)
                    turns.put_high(act, n, k, x_dst(1 - par, 0, j))
                act.wait_ge(acc_ready, u + 1 + OFF)
                act.wait_ge(stored[s % 2], 48 * blk + (16 * (s // 2) + 16))
                for half in (0, 1):
                    last = nc.scalar.activation(out[:, s % 2, half, :], acc[s % 3][half][:, :], ACT.Copy)
                last.then_inc(acc_out, 1)
                if up:
                    gq = gate_q[:, bass.ds(u, 1), :].rearrange("p a i -> p (a i)")
                    act.wait_ge(gate_in[s % 2], 48 * blk + (16 * (s // 2) + 16))
                    act.sem_inc(held.act, 1)
                    nc.scalar.activation(gq, work[:, s % 2, :], ACT.Copy, scale=sc["gate_c"][:, 0:1]).then_inc(gate_done, 1)
                    act.wait_ge(gate_done, u + 1 + OFF)
                    act.sem_inc(held.act, 1)
                    nc.scalar.activation(work[:, s % 2, :], gq, ACT.Sigmoid, scale=sc["gate_scale"][:, 0:1]).then_inc(sigmoid_done, 1)

        each_block(act, block)

    def dve_program(dve):
        turns.start({"dve": dve})
        dve.sem_inc(acc_max, OFF)
        if up:
            dve.sem_inc(g2_done, OFF)
            dve.sem_inc(g2_max, OFF)
        else:
            nc.vector.tensor_reduce(tops[:, 0:1], dram["yall"][:, :], AX.X, ALU.max).then_inc(col_top, 1)
            dve.wait_ge(top, 1)
            scales.scale(dve, sc["x_scale"], tops[:, 1:2], 1.0, sc["x_inv"])
        for m in range(len(weights)):
            with dve.Fori(0, 3) as r:
                for k in range(4):
                    n = 12 * m + 4 * r + k
                    turns.quantise_w(dve, n, 6 * m + 2 * r + k // 2, 48 * m + 16 * r + 4 * k, k % 2)
                    if k:
                        turns.put_low(dve, n - 1, (k - 1) % 2, w_dst(m, 1, 4 * r + k - 1), w_dst(m, 0, 4 * r + k - 1))
                turns.put_low(dve, 12 * m + 4 * r + 3, 1, w_dst(m, 1, 4 * r + 3), w_dst(m, 0, 4 * r + 3))
        for n, half_n, k, j in first_x():
            turns.quantise_x(dve, n, half_n, k, sc["x_inv"])
            turns.put_low(dve, n, k, x_dst(0, 1, j), x_dst(0, 0, j))

        def block(blk, par):
            items = {s: rest for s, *rest in x_items(blk, 1 - par)}
            for s in range(PAIRS):
                u = blk * PAIRS + s
                if s in items:
                    n, half_n, k, j = items[s]
                    turns.quantise_x(dve, n, half_n, k, sc["x_inv"])
                dve.wait_ge(acc_out, u + 1 + OFF)
                nc.vector.tensor_reduce(cols[:, bass.ds(u, 1)], out[:, s % 2, :, :].rearrange("p a i -> p (a i)"), AX.X,
                                        ALU.max, apply_absolute_value=True).then_inc(acc_max, 1)
                if s in items:
                    turns.put_low(dve, n, k, x_dst(1 - par, 1, j), x_dst(1 - par, 0, j))
                if up:
                    dve.wait_ge(gate_done, u + 1 + OFF)
                    dve.wait_ge(sig_step, 2 * u + 2 + OFF)
                    nc.vector.tensor_tensor(work[:, s % 2, :], gate_q[:, bass.ds(u, 1), :].rearrange("p a i -> p (a i)"),
                                            work[:, s % 2, :], ALU.mult).then_inc(g2_done, 1)
                    dve.wait_ge(g2_done, u + 1 + OFF)
                    nc.vector.tensor_reduce(cols2[:, bass.ds(u, 1)], work[:, s % 2, :], AX.X, ALU.max,
                                            apply_absolute_value=True).then_inc(g2_max, 1)

        each_block(dve, block)
        dve.wait_ge(acc_max, N_BLK * PAIRS + OFF)
        nc.vector.tensor_reduce(tops[:, 2:3], cols[:, :], AX.X, ALU.max).then_inc(col_top, 1)
        dve.wait_ge(top, 1 if up else 2)
        if not up:
            scales.scale(dve, sc["gate_scale"], tops[:, 3:4], sc["x_scale"], sc["gate_c"])
        else:
            scales.scale(dve, sc["up_scale"], tops[:, 3:4], sc["x_scale"], sc["up_c"])
            scales.mult(dve, sc["g2_unit"], sc["gate_scale"], 1.0 / SIG)
            dve.wait_ge(g2_max, N_BLK * PAIRS + OFF)
            nc.vector.tensor_reduce(tops[:, 0:1], cols2[:, :], AX.X, ALU.max).then_inc(col_top, 1)
            dve.wait_ge(top, 2)
            scales.scale(dve, sc["g2_scale"], tops[:, 1:2], sc["g2_unit"], sc["g2_c"])
            scales.mult(dve, sc["o_unit"], sc["g2_scale"], sc["up_scale"])

    def pool_program(pool):
        turns.start({"pool": pool})
        if up:
            pool.sem_inc(sig_step, OFF)
        else:
            pool.wait_ge(col_top, 1)
            nc.gpsimd.partition_all_reduce(tops[:, 1:2], tops[:, 0:1], P, RMAX).then_inc(top, 1)
        for m in range(len(weights)):
            with pool.Fori(0, 3) as r:
                for k in range(4):
                    turns.restore_w(pool, 12 * m + 4 * r + k, k % 2)
        for n, _, k, j in first_x():
            turns.restore_x(pool, n, k)

        def block(blk, par):
            items = {s: rest for s, *rest in x_items(blk, 1 - par)}
            for s in range(PAIRS):
                u = blk * PAIRS + s
                if s in items:
                    n, _, k, j = items[s]
                    turns.restore_x(pool, n, k)
                if up:
                    pool.wait_ge(sigmoid_done, u + 1 + OFF)
                    pool.sem_inc(held.pool, 1)
                    nc.gpsimd.tensor_scalar(work[:, s % 2, :], work[:, s % 2, :], SIG, ROUND, ALU.mult,
                                            ALU.add).then_inc(sig_step, 1)
                    pool.wait_ge(sig_step, 2 * u + 1 + OFF)
                    pool.sem_inc(held.pool, 1)
                    nc.gpsimd.tensor_scalar(work[:, s % 2, :], work[:, s % 2, :], ROUND, SIG - 1, ALU.subtract,
                                            ALU.min).then_inc(sig_step, 1)

        each_block(pool, block)
        pool.wait_ge(col_top, 1 if up else 2)
        nc.gpsimd.partition_all_reduce(tops[:, 3:4], tops[:, 2:3], P, RMAX).then_inc(top, 1)
        if up:
            pool.wait_ge(col_top, 2)
            nc.gpsimd.partition_all_reduce(tops[:, 1:2], tops[:, 0:1], P, RMAX).then_inc(top, 1)

    return pe_program, act_program, dve_program, pool_program, sp_program


N_GRP = N_BLK * GROUPS


def product_sizes(nc, sb, sem, held, dram, banks, ident, sc, w_hl, gate_q, gates):
    turns = Turns(nc, sb, sem, held, "b", [banks[6], banks[7]], ident)
    up_f = sb("up_f", [P, 2, 2048], F32)
    work = sb("b_work", [P, 2, 2048], F32)
    up_q = sb("b_up_q", [P, 2, 2048], I16)
    cols = sb("b_cols", [P, N_GRP], F32)
    tops = sb("b_tops", [P, 2], F32)
    up_in = [sem("up_in0"), sem("up_in1")]
    stored = [sem("b_stored0"), sem("b_stored1")]
    sigmoid_done, g2_quantised = sem("b_sigmoid_done"), sem("g2_quantised")
    up_quantised = sem("up_quantised")
    g2_done, o_done, o_max = sem("b_g2_done"), sem("b_o_done"), sem("b_o_max")
    sig_step = sem("b_sig_step")
    col_top, top = sem("b_col_top"), sem("b_top")
    scales = Scales(nc, sem, "b_scales")
    w_down = dram["L1_ffn_w_down"]
    g_all = gate_q[:, :, :].rearrange("p u i -> p (u i)")

    def gq(n):
        return g_all[:, bass.ds(n * 2048, 2048)]

    def w_dst(part, g, r):
        return w_hl[:, part, bass.ds(4 * g, 4), P * r:P * r + P]

    def each_group(eng, body):
        with eng.Fori(0, N_GRP // 2) as two:
            for par in (0, 1):
                body(2 * two + par, par, two)

    def sp_program(sp):
        for s in stored:
            sp.sem_inc(s, 16)
        with sp.Fori(0, GROUPS) as g:
            for r in range(4):
                turns.load(sp, 4 * g + r, r % 2, w_down[P * r:P * r + P, bass.ds(g * 512, 512)])

        def load(n, slot):
            sp.dma_start(up_f[:, slot, :].rearrange("p (u i) -> p u i", u=2),
                         dram["up"][bass.ds(2 * n, 2)].rearrange("u p i -> p u i")).then_inc(up_in[slot], 16)

        def group(n, par, two):
            sp.wait_ge(o_max, n + OFF)
            load((n + 1) % N_GRP, 1 - par)
            sp.wait_ge(up_quantised, n + 1 + OFF)
            sp.dma_start(dram["up_q"][n], up_q[:, par, :]).then_inc(stored[par], 16)

        load(0, 0)
        each_group(sp, group)
        sp.wait_ge(up_in[0], 16 * (N_GRP // 2 + 1))
        for s in stored:
            sp.wait_ge(s, 16 * (N_GRP // 2 + 1))

    def pe_program(pe):
        turns.start({"pe": pe})
        with pe.Fori(0, GROUPS) as g:
            for r in range(4):
                turns.transpose(pe, 4 * g + r, r % 2)

    def act_program(act):
        turns.start({"act": act})
        for s in (sigmoid_done, g2_quantised, up_quantised):
            act.sem_inc(s, OFF)
        with act.Fori(0, GROUPS) as g:
            for r in range(4):
                turns.put_high(act, 4 * g + r, r % 2, w_dst(0, g, r))

        def group(n, par, two):
            act.wait_ge(o_done, n - 1 + OFF)
            act.wait_ge(g2_quantised, n - 1 + OFF)
            act.sem_inc(held.act, 1)
            nc.scalar.activation(work[:, par, :], gq(n), ACT.Sigmoid, scale=sc["gate_scale"][:, 0:1]).then_inc(sigmoid_done, 1)
            act.wait_ge(up_in[par], 16 * two + 16)
            act.wait_ge(stored[par], 16 * two + 16)
            nc.scalar.activation(up_q[:, par, :], up_f[:, par, :], ACT.Copy, scale=sc["up_c"][:, 0:1]).then_inc(up_quantised, 1)
            act.wait_ge(g2_done, n + 1 + OFF)
            act.sem_inc(held.act, 1)
            nc.scalar.activation(gq(n), work[:, par, :], ACT.Copy, scale=sc["g2_c"][:, 0:1]).then_inc(g2_quantised, 1)

        each_group(act, group)

    def dve_program(dve):
        turns.start({"dve": dve})
        for s in (g2_done, o_done, o_max):
            dve.sem_inc(s, OFF)
        with dve.Fori(0, GROUPS) as g:
            for r in range(4):
                n = 4 * g + r
                turns.quantise_w(dve, n, 2 * g + r // 2, 16 * g + 4 * r, r % 2)
                if r:
                    turns.put_low(dve, n - 1, (r - 1) % 2, w_dst(1, g, r - 1), w_dst(0, g, r - 1))
            turns.put_low(dve, 4 * g + 3, 1, w_dst(1, g, 3), w_dst(0, g, 3))

        def group(n, par, two):
            dve.wait_ge(sig_step, 2 * n + 2 + OFF)
            nc.vector.tensor_tensor(work[:, par, :], gq(n), work[:, par, :], ALU.mult).then_inc(g2_done, 1)
            dve.wait_ge(g2_quantised, n + 1 + OFF)
            dve.wait_ge(up_quantised, n + 1 + OFF)
            nc.vector.tensor_tensor(up_f[:, par, :], gq(n), up_q[:, par, :], ALU.mult).then_inc(o_done, 1)
            dve.wait_ge(o_done, n + 1 + OFF)
            nc.vector.tensor_reduce(cols[:, bass.ds(n, 1)], up_f[:, par, :], AX.X, ALU.max,
                                    apply_absolute_value=True).then_inc(o_max, 1)

        each_group(dve, group)
        dve.wait_ge(o_max, N_GRP + OFF)
        nc.vector.tensor_reduce(tops[:, 0:1], cols[:, :], AX.X, ALU.max).then_inc(col_top, 1)
        dve.wait_ge(top, 1)
        scales.scale(dve, sc["o_scale"], tops[:, 1:2], sc["o_unit"], sc["o_c"])
        scales.mult(dve, sc["out_factor"], sc["o_scale"], gates[:, 3:4])

    def pool_program(pool):
        turns.start({"pool": pool})
        pool.sem_inc(sig_step, OFF)
        with pool.Fori(0, GROUPS) as g:
            for r in range(4):
                turns.restore_w(pool, 4 * g + r, r % 2)

        def group(n, par, two):
            pool.wait_ge(sigmoid_done, n + 1 + OFF)
            pool.sem_inc(held.pool, 1)
            nc.gpsimd.tensor_scalar(work[:, par, :], work[:, par, :], SIG, ROUND, ALU.mult, ALU.add).then_inc(sig_step, 1)
            pool.wait_ge(sig_step, 2 * n + 1 + OFF)
            pool.sem_inc(held.pool, 1)
            nc.gpsimd.tensor_scalar(work[:, par, :], work[:, par, :], ROUND, SIG - 1, ALU.subtract,
                                    ALU.min).then_inc(sig_step, 1)

        each_group(pool, group)
        pool.wait_ge(col_top, 1)
        nc.gpsimd.partition_all_reduce(tops[:, 1:2], tops[:, 0:1], P, RMAX).then_inc(top, 1)

    return pe_program, act_program, dve_program, pool_program, sp_program


def down_product(nc, sb, sem, held, dram, banks, sc, w_hl, gate_q):
    up_q = sb("c_up_q", [P, 2, 2048], I16)
    prod = sb("c_prod", [P, 2048], F32)
    o_hl = sb("o_hl", [P, 2, 2, 2048], F32R)
    x_mid = sb("c_x_mid", [P, 4, D], F32)
    res = sb("c_res", [P, 2, D], F32)
    up_in = [sem("c_up_in0"), sem("c_up_in1")]
    x_in = [sem(f"c_x_in{j}") for j in range(4)]
    stored = [sem("c_stored0"), sem("c_stored1")]
    prod_done = sem("c_prod_done")
    o_quantised, high = sem("c_o_quantised"), sem("c_high")
    low = sem("c_low")
    o_used = sem("c_o_used")
    acc_ready = sem("c_acc_ready")
    acc_out = sem("c_acc_out")
    added = sem("c_added")
    out = dram["out"].rearrange("b (t p) d -> (b t) p d", p=P)
    g_all = gate_q[:, :, :].rearrange("p u i -> p (u i)")
    SLOTS = 2 * GROUPS

    def two_blocks(eng, body):
        with eng.Fori(0, N_BLK // 2) as two:
            for k in range(SLOTS):
                body(SLOTS * two + k, k, two)

    def sp_program(sp):
        for s in stored:
            sp.sem_inc(s, 16)

        def load_x(t, j):
            sp.dma_start(x_mid[:, j, :], dram["x_mid"][t]).then_inc(x_in[j], 16)

        def turn_over(first):
            for j in range(4):
                sp.wait_ge(added, first + j + 1 + OFF)
                sp.dma_start(out[first + j], res[:, j % 2, :]).then_inc(stored[j % 2], 16)
                load_x((first + 4 + j) % (4 * N_BLK), j)

        for j in range(4):
            load_x(j, j)
        with sp.Fori(0, N_BLK // 2) as two:
            for k in range(SLOTS):
                n = SLOTS * two + k
                sp.wait_ge(low, n - 1 + OFF)
                sp.dma_start(up_q[:, k % 2, :], dram["up_q"][n]).then_inc(up_in[k % 2], 16)
                if k == GROUPS:
                    turn_over(8 * two)
            turn_over(8 * two + 4)
        for j in range(4):
            sp.wait_ge(x_in[j], 16 * (N_BLK + 1))
        for s in stored:
            sp.wait_ge(s, 16 * (N_BLK * 2 + 1))

    def pe_program(pe):
        pe.sem_inc(o_used, OFF)
        pe.sem_inc(acc_ready, OFF)

        def group(n, k, two):
            b, g = divmod(k, GROUPS)
            pe.wait_ge(high, n + 1 + OFF)
            pe.wait_ge(low, n + 1 + OFF)
            if g == 0:
                pe.wait_ge(acc_out, 8 * two + (4 * b - 4 + OFF))
            for i in range(4):
                for j in range(4):
                    for a, b_ in ((0, 0), (0, 1), (1, 0)):
                        last = nc.tensor.matmul(banks[4 * b + j][:, :],
                                                o_hl[:, k % 2, a, 512 * i + P * j:512 * i + P * j + P],
                                                w_hl[:, b_, 4 * g + i, :], start=(g == 0 and i == 0 and (a, b_) == (0, 0)),
                                                stop=(g == GROUPS - 1 and i == 3 and (a, b_) == (1, 0)))
                    if g == GROUPS - 1 and i == 3 and j < 3:
                        last.then_inc(acc_ready, 1)
            last.then_inc(o_used, 1)

        two_blocks(pe, group)

    def act_program(act):
        act.sem_inc(o_quantised, OFF)
        act.sem_inc(high, OFF)

        def group(n, k, two):
            act.wait_ge(prod_done, n + 1 + OFF)
            nc.scalar.activation(up_q[:, k % 2, :], prod[:, :], ACT.Copy, scale=sc["o_c"][:, 0:1]).then_inc(o_quantised, 1)
            act.wait_ge(o_quantised, n + 1 + OFF)
            act.wait_ge(o_used, n - 1 + OFF)
            nc.scalar.activation(o_hl[:, k % 2, 0, :], up_q[:, k % 2, :], ACT.Copy).then_inc(high, 1)

        two_blocks(act, group)

    def dve_program(dve):
        dve.sem_inc(prod_done, OFF)
        dve.sem_inc(low, OFF)
        dve.sem_inc(acc_out, OFF)

        def results(first, b, two):
            for j in range(4):
                if j < 3:
                    dve.wait_ge(acc_ready, 6 * two + (3 * b + j + 1 + OFF))
                else:
                    dve.wait_ge(o_used, SLOTS * two + (GROUPS * (b + 1) + OFF))
                dve.wait_ge(stored[j % 2], 8 * first + (16 * (j // 2) + 16))
                nc.vector.tensor_scalar(res[:, j % 2, :], banks[4 * b + j][:, :], sc["out_factor"][:, 0:1], None,
                                        ALU.mult).then_inc(acc_out, 1)

        with dve.Fori(0, N_BLK // 2) as two:
            for k in range(SLOTS):
                n = SLOTS * two + k
                dve.wait_ge(up_in[k % 2], 48 * two + (16 * (k // 2) + 16))
                dve.wait_ge(o_quantised, n + OFF)
                nc.vector.tensor_tensor(prod[:, :], g_all[:, bass.ds(n * 2048, 2048)], up_q[:, k % 2, :],
                                        ALU.mult).then_inc(prod_done, 1)
                dve.wait_ge(high, n + 1 + OFF)
                nc.vector.tensor_tensor(o_hl[:, k % 2, 1, :], up_q[:, k % 2, :], o_hl[:, k % 2, 0, :].bitcast(F32),
                                        ALU.subtract).then_inc(low, 1)
                if k == GROUPS:
                    results(8 * two, 0, two)
            results(8 * two + 4, 1, two)

    def pool_program(pool):
        pool.sem_inc(added, OFF)

        def add(first, two, b):
            for j in range(4):
                pool.wait_ge(acc_out, first + j + 1 + OFF)
                pool.wait_ge(x_in[j], 32 * two + (16 * b + 16))
                nc.gpsimd.tensor_tensor(res[:, j % 2, :], res[:, j % 2, :], x_mid[:, j, :], ALU.add).then_inc(added, 1)

        with pool.Fori(0, N_BLK // 2) as two:
            add(8 * two, two, 0)
            add(8 * two + 4, two, 1)

    return pe_program, act_program, dve_program, pool_program, sp_program


def run_block(nc, pe_program, act_program, dve_program, pool_program, sp_program):
    with nc.Block() as block:
        @block.sync
        def _(sp):
            sp_program(sp)

        @block.scalar
        def _(act):
            act_program(act)

        @block.tensor
        def _(pe):
            pe_program(pe)

        @block.vector
        def _(dve):
            dve_program(dve)

        @block.gpsimd
        def _(pool):
            pool_program(pool)


def build(nc, dram):
    with ExitStack() as ctx:
        def sem(name):
            return ctx.enter_context(nc.semaphore(name))

        def buffers(stage):
            return lambda name, shape, dt: stage.enter_context(nc.sbuf_tensor(name, shape, dt))

        sb = buffers(ctx)
        held = Held(sem)
        gates = sb("gates", [P, 4], F32)
        ident = sb("ident", [P, P], F32)
        dram["yall"] = sb("yall", [P, B * T], F32)
        sc = {name: sb("the_" + name, [P, 1], F32) for name in SCALARS}
        banks = [ctx.enter_context(nc.psum_tensor(f"bank{k}", [P, 512], F32)) for k in range(8)]
        phase = ctx.enter_context(ExitStack())
        w_ffn = phase.enter_context(nc.sbuf_tensor("w_ffn", [P, C, D], F32))
        with ExitStack() as stage:
            run_block(nc, *fold_weights(nc, buffers(stage), sem, dram, banks, ident, w_ffn))
        with ExitStack() as stage:
            one = phase1(nc, buffers(stage), sem, held, dram, gates, banks, ident, w_ffn)
            run_block(nc, *one)
        phase.close()
        w_hl = sb("w_hl", [P, 2 * C * I], F32R)
        up_hl = w_hl[:, :].rearrange("p (a c i) -> p a c i", a=2, c=C)
        down_hl = w_hl[:, :].rearrange("p (a i d) -> p a i d", a=2, i=IT)
        with ExitStack() as stage:
            gate_hl = buffers(stage)("gate_hl", [P, 2, C, I], F32R)
            run_block(nc, *quantised_products(nc, buffers(stage), sem, held, dram, banks, ident, sc, gate_hl, "gate_stage", "gate", None,
                                              [(dram["L1_ffn_w_gate"], gate_hl), (dram["L1_ffn_w_up"], up_hl)], gates))
        gate_q = sb("gate_q", [P, N_BLK * PAIRS, 1024], I16)
        with ExitStack() as stage:
            run_block(nc, *quantised_products(nc, buffers(stage), sem, held, dram, banks, ident, sc, up_hl, "up_stage", "up", gate_q,
                                              [], gates))
        with ExitStack() as stage:
            run_block(nc, *product_sizes(nc, buffers(stage), sem, held, dram, banks, ident, sc, down_hl, gate_q, gates))
        with ExitStack() as stage:
            run_block(nc, *down_product(nc, buffers(stage), sem, held, dram, banks, sc, down_hl, gate_q))


INPUTS = ("x", "ctx_2048", "itok_Bx1_68_817", "mask_BxS2_ik0", "g_xattn", "g_ffn", "L0_xattn_b", "L0_ffn_weight",
          "L0_ffn_aux_weight1", "L0_ffn_aux_weight2", "L0_ffn_bias", "L1_xattn_b", "L1_ffn_w_gate", "L1_ffn_w_up",
          "L1_ffn_w_down")


def kernel(**inputs):
    import concourse.bacc as bacc
    from concourse.bass_utils import run_bass_kernel_spmd

    nc = bacc.Bacc("TRN2", target_bir_lowering=False, num_devices=1)
    arrays = {name: np.ascontiguousarray(inputs[name]) for name in INPUTS}
    arrays["ident"] = np.eye(P, dtype=np.float32)
    arrays["iota"] = np.arange(S, dtype=np.float32)
    dram = {name: nc.dram_tensor("in_" + name, a.shape, mybir.dt.from_np(a.dtype), kind="ExternalInput").ap()
            for name, a in arrays.items()}
    dram["out"] = nc.dram_tensor("out", (B, S, D), F32, kind="ExternalOutput").ap()
    for name, shape, dt in SCRATCH:
        dram[name] = nc.dram_tensor(name, shape, dt, kind="Internal").ap()
    build(nc, dram)
    return run_bass_kernel_spmd(nc, [{"in_" + name: a for name, a in arrays.items()}], core_ids=[0]).results[0]["out"]


SCRATCH = (("x_mid", (B * T, P, D), F32), ("y_mid", (B * T, P, D), F32), ("gate", (N_BLK * PAIRS, P, 1024), F32),
           ("up", (N_BLK * PAIRS, P, 1024), F32), ("up_q", (N_GRP, P, 2048), I16))
```

```python
from contextlib import ExitStack

import concourse.bass as bass
import numpy as np
from concourse import mybir

F32 = mybir.dt.float32
F32R = mybir.dt.float32r
BF16 = mybir.dt.bfloat16
F16 = mybir.dt.float16
I32 = mybir.dt.int32
I16 = mybir.dt.int16
U16 = mybir.dt.uint16
ALU = mybir.AluOpType
ACT = mybir.ActivationFunctionType
AX = mybir.AxisListType
RMAX = bass.bass_isa.ReduceOp.max

P = 128
B, S, D = 8, 512, 512
T = S // P
C = D // P
H0, H1 = 16, 8
DH0, DH1 = D // H0, D // H1
G = H0 // 4
OFF = 8
EPS = 1e-5
MASK0, MASK1 = 1e12, 1e30
BIG = 3e38

SEGMENTS = [(layer, t) for layer in (0, 1) for t in range(T)]
UNITS = [(k, layer, t, h) for k, (layer, t) in enumerate(SEGMENTS) for h in range(H1 if layer else H0)]
NU = len(UNITS)
START = {seg: next(u for u, x in enumerate(UNITS) if x[0] == k) for k, seg in enumerate(SEGMENTS)}
END = {seg: START[seg] + (H1 if seg[0] else H0) for seg in SEGMENTS}
LAG_T, LAG_LO, LAG_PV = 2, 3, 5
ST = 3 * DH0
NORMS = ("q", "f", "y")
Q_SCALE = (-DH0 ** -0.5, -DH1 ** -0.5)


class Held:

    def __init__(self, sem):
        self.act, self.dve, self.pool, self.sp = (sem("held_" + e) for e in ("act", "dve", "pool", "sp"))


def bank_of(what):
    if what[0].endswith("_turn") and what[0] != "f_turn":
        return "ad"[what[2] % 2]
    if what[0] == "f_turn":
        return "a"
    return "d" if what[0] == "f_mm" and what[2] == 1 else None


def holds(what):
    return "d" if what[0] == "f_mm" else bank_of(what)


def schedule():
    at = {}

    def put(slot, *what):
        at.setdefault(slot, []).append(what)

    def norm(slot, j, t):
        put(slot, "norm", j, t)
        put(slot + 2, "xn", j, t)

    def queries(slot, t, turn):
        norm(slot, "q", t)
        put(slot + 3, "q_split", t)
        while any(holds(w) for k in (0, 1) for w in at.get(turn + k, [])):
            turn += 1
        for g in range(G):
            put(turn + g // 2, "q_turn", t, g)

    for t in range(T):
        e = END[0, t] + LAG_PV
        put(e, "end0", t)
        norm(e + 2, "f", t)
        put(e + 5, "f_turn", t)
        put(e + 7, "f_mm", t, 0)
        put(e + 8, "f_mm", t, 1)
        put(e + 10, "f_out", t)
        e = END[1, t] + LAG_PV
        put(e, "end1", t)
        norm(e + 2, "y", t)
        put(e + 5, "y_out", t)
    for t, slot in enumerate((6, 22, 40, NU - 9)):
        queries(slot, (0, t), slot + 5)
    for t in range(T):
        slot = END[0, t] + LAG_PV + 12
        queries(slot, (1, t), max(slot + 5, END[1, t - 2] + 1 if t >= 2 else 0))
    put(30, "bias")
    for kc in range(T):
        slot = 24 + 16 * kc
        put(slot, "kv_split", kc)
        slot += 5
        for g in range(G):
            slot += 1
            while any(holds(w) == "ad"[g % 2] for w in at.get(slot, [])):
                slot += 1
            put(slot, "k_turn", kc, g)
    for jobs in at.values():
        used = [holds(w) for w in jobs if holds(w)]
        assert len(used) == len(set(used)), jobs
    return at


AT = schedule()
JOBS = [w for s in sorted(AT) for w in AT[s]]
WRAP = max(AT) + 2 - NU
assert all(w[0] in ("end1", "y_out") or w[1:2] == ("y",) for s, jobs in AT.items() if s >= NU - 1 for w in jobs)
PROLOGUE = [("bias",)]
for _kc in range(T):
    PROLOGUE += [("kv_split", _kc)] + [("k_turn", _kc, g) for g in range(G)]
PROLOGUE += [("norm", "q", (0, T - 1)), ("xn", "q", (0, T - 1)), ("q_split", (0, T - 1))] + [("q_turn", (0, T - 1), g) for g in range(G)]


def number(want):
    return tuple({w: n for n, w in enumerate(w for w in jobs if want(w))} for jobs in (PROLOGUE, JOBS))


BANK_NO = {k: number(lambda w: bank_of(w) == k) for k in "ad"}
NORM_NO = {j: number(lambda w: w[:2] == ("norm", j)) for j in NORMS}
KV_NO = number(lambda w: w[0] == "kv_split")
BIAS_NO = number(lambda w: w[0] == "bias")


def emptying_at(slot):
    return [w for w in AT.get(slot - 1, []) if bank_of(w)]


def others_at(slot):
    return [w for w in AT.get(slot, []) if not bank_of(w)]


class Place:

    def __init__(self, pair=None, par=0):
        self.pair, self.par = pair, par
        self.bi = None if pair is None else 2 * pair + par
        self.next_par = 0 if pair is None else 1 - par
        self.next_b = 0 if pair is None else (2 * pair + 1 if par == 0 else (2 * pair + 2) % B)

    def count(self, numbers, what, each=1, more=0):
        pre, per = numbers
        if self.bi is None:
            return OFF + each * pre[what] + more
        return self.bi * (each * len(per)) + each * (len(pre) + per[what]) + more + OFF

    def unit(self, u):
        return self.bi * NU + (u + 1 + OFF)

    def nth(self, per, k):
        return self.bi * per + (k + OFF)


def run_slots(eng, slot):
    def batch(now, after):
        for s in range(WRAP, NU):
            slot(s, now, None)
        for s in range(WRAP):
            slot(s, after, now)

    for s in range(WRAP):
        slot(s, Place(0, 0), None)
    with eng.Fori(0, B // 2 - 1) as pair:
        batch(Place(pair, 0), Place(pair, 1))
        batch(Place(pair, 1), Place(pair + 1, 0))
    pair = B // 2 - 1
    batch(Place(pair, 0), Place(pair, 1))
    batch(Place(pair, 1), None)


def units_at(s, now, before, lag=0):
    place, u = (now, s - lag) if s >= lag else (before, s - lag + NU)
    return [(place, u)] if place else []


def steps_at(s, now, before, jobs_at=lambda s: AT.get(s, [])):
    return [(before, w) for w in jobs_at(s + NU) if before] + [(now, w) for w in jobs_at(s) if now]


def tile_of_q0(place, t):
    return (place.par, t + 1) if t + 1 < T else (place.next_par, 0)


def fold_weights(nc, sb, sem, dram, banks, ident, w_ffn):
    w_in = [sb(f"w_in{k}", [P, C, D], F32) for k in range(4)]
    w_leftT = sb("w_leftT", [P, C, P], F32)
    loaded = sem("w_loaded")
    turned = sem("w_turned")
    done = sem("w_done")
    moved = sem("w_moved")

    def pe_program(pe):
        pe.wait_ge(loaded, 16 * 4)
        for n in range(2 * C):
            left, right = (w_in[1], w_in[2]) if n < C else (w_in[0], w_in[3])
            if n:
                pe.wait_ge(moved, 2 * n - 1)
            for c in range(C):
                last = nc.tensor.transpose(banks[0][:, P * c:P * c + P], left[:, n % C, P * c:P * c + P], ident[:, :])
            last.then_inc(turned, 1)
            pe.wait_ge(moved, 2 * n + 1)
            for c in range(C):
                last = nc.tensor.matmul(banks[1][:, :], w_leftT[:, c, :], right[:, c, :], start=(c == 0), stop=(c == C - 1))
            last.then_inc(done, 1)

    def dve_program(dve):
        for n in range(2 * C):
            out = w_in[3] if n < C else w_ffn
            dve.wait_ge(turned, n + 1)
            if n:
                dve.wait_ge(done, n)
            nc.vector.tensor_copy(w_leftT[:, :, :].rearrange("p c i -> p (c i)"), banks[0][:, :]).then_inc(moved, 1)
            dve.wait_ge(done, n + 1)
            nc.vector.tensor_copy(out[:, n % C, :], banks[1][:, :]).then_inc(moved, 1)

    def sp_program(sp):
        sp.dma_start(ident[:, :], dram["ident"]).then_inc(loaded, 16)
        for k, name in ((1, "L0_ffn_aux_weight1"), (2, "L0_ffn_aux_weight2"), (0, "L0_ffn_weight")):
            sp.dma_start(w_in[k][:, :, :], dram[name].rearrange("(c p) d -> p c d", p=P)).then_inc(loaded, 16)

    def idle(_):
        pass

    return pe_program, idle, dve_program, idle, sp_program


def phase1(nc, sb, sem, held, dram, gates, banks, ident, w_ffn):
    iota = sb("iota", [P, S], F32)
    half = sb("half", [P, 1], F32)
    b0_row = sb("b0_row", [P, S], F32)
    b1_col = sb("b1_col", [P, 1], F32)
    ffn_bias = sb("ffn_bias", [P, D], F32)
    seq_i = sb("seq_i", [P, B], I32)
    seq_f = sb("seq_f", [P, B], F32)
    nbias = sb("nbias", [P, 2, 2, S], F32)
    x = sb("x", [P, 2, T, D], F32)
    kv = sb("kv", [P, 2, 2 * D], F32)
    kT = sb("kT", [P, 2, H0, S], F32R)
    v = sb("v", [P, 2, T, 3, D], BF16)
    v_rest = sb("v_rest", [P, D], F32)
    qT = [sb("q0T", [P, 2, H0, P], F32R), sb("q1T", [P, 2, H0, P], F32R)]
    parts = {j: sb("parts_" + j, [P, H0, 3, DH0], F32R) for j in ("q", "k")}
    xn = {j: sb("xn_" + j, [P, D], F32) for j in NORMS}
    stat = {j: sb("stat_" + j, [P, 6], F32) for j in NORMS}
    mv = {j: sb("mv_" + j, [P, 2], F32) for j in NORMS}
    rstd = {j: sb("rstd_" + j, [P, 3], F32) for j in NORMS}
    xnT = sb("xnT", [P, C, P], F32)
    f_out = sb("f_out", [P, D], F32)
    p = sb("p", [P, 2, S], F32)
    pT_hi = sb("pT_hi", [P, 4, S], F16)
    pT_lo = sb("pT_lo", [P, 3, S], F16)
    nmax = sb("nmax", [P, 4], F32)
    rsum = [sb("rsum0", [P, 2, H0], F32), sb("rsum1", [P, 2, H1], F32)]
    rinv = [sb("rinv0", [P, H0], F32), sb("rinv1", [P, H1], F32)]
    o_sb = [sb("o_sb0", [P, D], F32), sb("o_sb1", [P, D], F32)]
    ymax = sb("ymax", [P, T], F32)
    yall = dram["yall"]

    s_bank, pT_bank, o_bank, misc = banks[0:2], banks[2:4], banks[4:6], {"a": banks[6], "d": banks[7]}

    consts_in = sem("consts_in")
    gates_ready = sem("gates_ready")
    seq_ready = sem("seq_ready")
    x_in = [sem("x_in0"), sem("x_in1")]
    kv_in = [sem("kv_in0"), sem("kv_in1")]
    mask_in = sem("mask_in")
    x_store, y_store = sem("x_store"), sem("y_store")
    bias_step = sem("bias_step")
    s_ready = sem("s_ready")
    max_ready = sem("max_ready")
    exp_done = sem("exp_done")
    pT_ready = sem("pT_ready")
    hi_done = sem("hi_done")
    lo_done = sem("lo_done")
    pv_done = sem("pv_done")
    filled = {"a": sem("a_filled"), "d": sem("d_filled")}
    freed = {"a": sem("a_freed"), "d": sem("d_freed")}
    stats = {j: sem("stats_" + j) for j in NORMS}
    rs_step = {j: sem("rs_step_" + j) for j in NORMS}
    normed = {j: sem("normed_" + j) for j in NORMS}
    hi_part = {j: sem("hi_part_" + j) for j in parts}
    lo_part = {j: sem("lo_part_" + j) for j in parts}
    v_step = sem("v_step")
    end_step = [sem("end_step0"), sem("end_step1")]
    x_step = [sem("x_step0"), sem("x_step1")]
    f_tanh = sem("f_tanh")
    f_step = sem("f_step")
    y_max = sem("y_max")

    def mask_row(par):
        return nbias[:, par, 1, :].bitcast(I32)

    N_CONSTS = 16 * 7

    def x_tile(place, j, t):
        if j == "q":
            layer, t = t
            par, t = (place.par, t) if layer else tile_of_q0(place, t)
        else:
            par = place.par
        return x[:, par, t, :]

    def emptied(what, place):
        if what[0] == "f_turn":
            return xnT[:, :, :].rearrange("p c i -> p (c i)"), misc["a"][:, :]
        kind, a, g = what
        bank = misc[bank_of(what)][0:ST, :].rearrange("p (k i) -> p k i", k=4)
        if kind == "k_turn":
            return kT[0:ST, place.next_par, 4 * g:4 * g + 4, P * a:P * a + P], bank
        layer, t = a
        t = t if layer else tile_of_q0(place, t)[1]
        return qT[layer][0:ST, t % 2, 4 * g:4 * g + 4, :], bank

    def wait_turned(eng, place, j, what):
        jobs = PROLOGUE if place.bi is None else JOBS
        turns = [w for w in jobs if w[0] == j + "_turn"]
        before = [w for w in turns if jobs.index(w) < jobs.index(what)]
        if not before and place.bi is None:
            return
        for k in "ad":
            w = [w for w in (before or turns) if bank_of(w) == k][-1]
            n = place.count(BANK_NO[k], w, 1, 1)
            eng.wait_ge(filled[k], n if before else n - len(BANK_NO[k][1]))

    def pe_job(pe, place, what):
        kind, k = what[0], bank_of(what)
        if kind in ("q_turn", "k_turn"):
            j, g = kind[0], what[2]
            if g == 0:
                no, w = (KV_NO, ("kv_split", what[1])) if j == "k" else (NORM_NO[j], ("norm", j, what[1]))
                pe.wait_ge(hi_part[j], place.count(no, w, 1, 1))
                pe.wait_ge(lo_part[j], place.count(no, w, 1, 1))
            pe.wait_ge(freed[k], place.count(BANK_NO[k], what))
            for n in range(4):
                h = 4 * g + n
                src = parts[j][:, h, :, :].bitcast(F32).rearrange("p a d -> p (a d)")
                last = nc.tensor.transpose(misc[k][0:ST, P * n:P * n + P], src, ident[:, :])
            last.then_inc(filled[k], 1)
        elif kind == "f_turn":
            pe.wait_ge(normed["f"], place.count(NORM_NO["f"], ("norm", "f", what[1]), 1, 1))
            pe.wait_ge(freed["a"], place.count(BANK_NO["a"], what))
            for c in range(C):
                last = nc.tensor.transpose(misc["a"][:, P * c:P * c + P], xn["f"][:, P * c:P * c + P], ident[:, :])
            last.then_inc(filled["a"], 1)
        elif kind == "f_mm":
            if what[2] == 0:
                pe.wait_ge(freed["a"], place.count(BANK_NO["a"], ("f_turn", what[1]), 1, 1))
                pe.wait_ge(freed["d"], place.count(BANK_NO["d"], ("f_mm", what[1], 1)))
            for c in range(2 * what[2], 2 * what[2] + 2):
                last = nc.tensor.matmul(misc["d"][:, :], xnT[:, c, :], w_ffn[:, c, :], start=(c == 0), stop=(c == C - 1))
            if what[2] == 1:
                last.then_inc(filled["d"], 1)

    def pe_scores(pe, place, u):
        _, layer, t, h = UNITS[u]
        if h == 0:
            job = t if layer else t - 1
            for k, g in (("a", G - 2), ("d", G - 1)):
                if job >= 0:
                    pe.wait_ge(freed[k], place.count(BANK_NO[k], ("q_turn", (layer, job), g), 1, 1))
                else:
                    pe.wait_ge(freed[k], place.bi * len(BANK_NO[k][1]) + (len(BANK_NO[k][0]) + OFF))
            if u == 0:
                pe.wait_ge(v_step, place.bi * (4 * T) + (4 * T + OFF))
        pe.wait_ge(exp_done, place.unit(u - 2))
        stacks = [2 * h, 2 * h + 1] if layer else [h]
        for n, k in enumerate(stacks):
            last = nc.tensor.matmul(s_bank[u % 2][:, :], qT[layer][0:ST, t % 2, k, :],
                                    kT[0:ST, place.par, k, :], start=(n == 0), stop=(n == len(stacks) - 1))
        last.then_inc(s_ready, 1)

    def pe_turn(pe, place, u):
        pe.wait_ge(exp_done, place.unit(u))
        pe.wait_ge(lo_done, place.unit(u - 2))
        for c in range(T):
            last = nc.tensor.transpose(pT_bank[u % 2][:, P * c:P * c + P], p[:, u % 2, P * c:P * c + P], ident[:, :])
        last.then_inc(pT_ready, 1)

    def pe_values(pe, place, u):
        k, layer, t, h = UNITS[u]
        dh = DH1 if layer else DH0
        if h == 0:
            was = SEGMENTS[k - 2]
            pe.wait_ge(end_step[was[0]], place.nth(3 * T, 3 * was[1] + 3 - (3 * T if k < 2 else 0)))
        pe.wait_ge(lo_done, place.unit(u))
        terms = [(c, part, n) for c in range(T) for part, n in ((0, 0), (0, 1), (0, 2), (1, 0), (1, 1))]
        for i, (c, part, n) in enumerate(terms):
            pT = pT_lo[:, u % 3, :] if part else pT_hi[:, u % 4, :]
            last = nc.tensor.matmul(o_bank[k % 2][:, dh * h:dh * h + dh], pT[:, P * c:P * c + P],
                                    v[:, place.par, c, n, dh * h:dh * h + dh], start=(i == 0), stop=(i == len(terms) - 1))
        last.then_inc(pv_done, 1)

    def pe_program(pe):
        for s in (s_ready, pT_ready, pv_done, *filled.values()):
            pe.sem_inc(s, OFF)
        pe.wait_ge(consts_in, N_CONSTS)
        for what in PROLOGUE:
            pe_job(pe, Place(), what)

        def slot(s, now, before):
            for place, u in units_at(s, now, before):
                pe_scores(pe, place, u)
            for place, u in units_at(s, now, before, LAG_PV):
                pe_values(pe, place, u)
            for place, u in units_at(s, now, before, LAG_T):
                pe_turn(pe, place, u)
            for place, what in steps_at(s, now, before):
                pe_job(pe, place, what)

        run_slots(pe, slot)

    def act_job(act, place, what):
        kind = what[0]
        if kind == "q_split":
            act.wait_ge(normed["q"], place.count(NORM_NO["q"], ("norm", "q", what[1]), 1, 1))
            wait_turned(act, place, "q", what)
            split_high("q", xn["q"][:, :])
        elif kind == "kv_split":
            kc = what[1]
            act.wait_ge(kv_in[kc % 2], kv_loaded(place, kc))
            wait_turned(act, place, "k", what)
            split_high("k", kv[:, kc % 2, 0:D])
        elif bank_of(what) == "a":
            act.wait_ge(filled["a"], place.count(BANK_NO["a"], what, 1, 1))
            if kind == "f_turn":
                act.wait_ge(filled["d"], place.count(BANK_NO["d"], ("f_mm", what[1], 1)))
            out, bank = emptied(what, place)
            nc.scalar.activation(out, bank, ACT.Copy).then_inc(freed["a"], 1)
        elif kind == "f_out":
            act.wait_ge(freed["d"], place.count(BANK_NO["d"], ("f_mm", what[1], 1), 1, 1))
            nc.scalar.activation(f_out[:, :], f_out[:, :], ACT.Tanh).then_inc(f_tanh, 1)

    def high_and_low(j):
        if j == "k":
            return parts[j][:, :, 0:2, :], parts[j][:, :, 2, :]
        return parts[j][:, :, 0:3:2, :], parts[j][:, :, 1, :]

    def split_high(j, src):
        src = src.rearrange("p (h d) -> p h d", h=H0).unsqueeze(2).broadcast_to([P, H0, 2, DH0])
        nc.scalar.activation(high_and_low(j)[0], src, ACT.Copy).then_inc(hi_part[j], 1)

    def kv_loaded(place, kc):
        n = kc // 2 + 1
        return 16 * n if place.bi is None else place.bi * 32 + 16 * (2 + n)

    def act_exp(act, place, u):
        _, layer, t, h = UNITS[u]
        act.wait_ge(max_ready, place.unit(u))
        act.wait_ge(pT_ready, place.unit(u - 2))
        if h == 0:
            act.wait_ge(end_step[layer], place.nth(3 * T, 3 * t - 3))
        nc.scalar.activation(p[:, u % 2, :], s_bank[u % 2][:, :], ACT.Exp, bias=nmax[:, u % 4:u % 4 + 1], scale=-1.0,
                             accum_out=rsum[layer][:, t % 2, h:h + 1]).then_inc(exp_done, 1)

    def act_hi(act, place, u):
        act.wait_ge(pT_ready, place.unit(u))
        act.wait_ge(pv_done, place.unit(u - 4))
        nc.scalar.activation(pT_hi[:, u % 4, :], pT_bank[u % 2][:, :], ACT.Copy).then_inc(hi_done, 1)

    def act_program(act):
        for s in (exp_done, hi_done, freed["a"], *hi_part.values(), f_tanh):
            act.sem_inc(s, OFF)
        act.wait_ge(consts_in, N_CONSTS)
        nc.scalar.activation(gates[:, :], gates[:, :], ACT.Tanh).then_inc(gates_ready, 1)
        for what in PROLOGUE:
            act_job(act, Place(), what)

        def slot(s, now, before):
            for place, what in steps_at(s, now, before, emptying_at):
                act_job(act, place, what)
            for place, u in units_at(s, now, before):
                act_exp(act, place, u)
            for place, u in units_at(s, now, before, LAG_T):
                act_hi(act, place, u)
            for place, what in steps_at(s, now, before, others_at):
                act_job(act, place, what)

        run_slots(act, slot)

    def dve_max(dve, place, u):
        _, layer, t, h = UNITS[u]
        dve.wait_ge(s_ready, place.unit(u))
        dve.wait_ge(exp_done, place.unit(u - 4))
        dve.sem_inc(held.dve, 1)
        out = s_bank[u % 2][:, :]
        nc.vector.tensor_tensor_reduce(out, out, nbias[:, place.par, layer, :], 1.0, BIG, ALU.add, ALU.min,
                                       nmax[:, u % 4:u % 4 + 1]).then_inc(max_ready, 1)

    def dve_lo(dve, place, u):
        dve.wait_ge(hi_done, place.unit(u))
        dve.wait_ge(pv_done, place.unit(u - 3))
        nc.vector.tensor_tensor(pT_lo[:, u % 3, :], pT_bank[u % 2][:, :], pT_hi[:, u % 4, :],
                                ALU.subtract).then_inc(lo_done, 1)

    def dve_job(dve, place, what):
        kind = what[0]
        if kind == "norm":
            j, t = what[1:]
            if j == "q" and t == (0, T - 1):
                par = place.next_par
                if place.bi is None:
                    dve.wait_ge(x_in[0], 16)
                else:
                    dve.wait_ge(x_in[par], place.pair * 16 + (16 if par else 32))
            elif j == "f":
                dve.wait_ge(x_step[0], place.nth(T, t + 1))
            elif j == "q" and t[0] == 1:
                dve.wait_ge(f_step, place.nth(2 * T, 2 * t[1] + 2))
            elif j == "y":
                dve.wait_ge(x_step[1], place.nth(T, t + 1))
            dve.wait_ge(normed[j], place.count(NORM_NO[j], what))
            nc.vector.bn_stats(stat[j][:, :], x_tile(place, j, t)).then_inc(stats[j], 1)
            dve.wait_ge(stats[j], place.count(NORM_NO[j], what, 2, 1))
            dve.sem_inc(held.dve, 1)
            nc.vector.bn_aggr(mv[j][:, :], stat[j][:, :]).then_inc(stats[j], 1)
        elif kind == "xn":
            j, t = what[1:]
            n, what = NORM_NO[j], ("norm", j, t)
            if j in parts:
                dve.wait_ge(lo_part[j], place.count(n, what))
            elif j == "f":
                dve.wait_ge(filled["a"], place.count(BANK_NO["a"], ("f_turn", (t - 1) % T), 1, 1 - (len(BANK_NO["a"][1]) if t == 0 else 0)))
            else:
                dve.wait_ge(y_max, place.count(n, what))
                dve.wait_ge(y_store, place.bi * (16 * T) + 16 * (t + 1))
            dve.wait_ge(rs_step[j], place.count(n, what, 3, 3))
            nc.vector.tensor_scalar(xn[j][:, :], x_tile(place, j, t), mv[j][:, 0:1], rstd[j][:, 2:3], ALU.subtract,
                                    ALU.mult).then_inc(normed[j], 1)
        elif bank_of(what) == "d" and kind != "f_mm":
            dve.wait_ge(filled["d"], place.count(BANK_NO["d"], what, 1, 1))
            out, bank = emptied(what, place)
            nc.vector.tensor_copy(out, bank).then_inc(freed["d"], 1)
        elif kind in ("end0", "end1"):
            layer, t = int(kind[3]), what[1]
            dh, heads = (DH1, H1) if layer else (DH0, H0)
            k, u = SEGMENTS.index((layer, t)), END[layer, t] - 1
            dve.wait_ge(exp_done, place.unit(u))
            nc.vector.reciprocal(rinv[layer][:, :], rsum[layer][:, t % 2, :]).then_inc(end_step[layer], 1)
            dve.wait_ge(end_step[layer], place.nth(3 * T, 3 * t + 1))
            nc.vector.tensor_scalar(rinv[layer][:, :], rinv[layer][:, :], gates[:, layer:layer + 1], None,
                                    ALU.mult).then_inc(end_step[layer], 1)
            dve.wait_ge(end_step[layer], place.nth(3 * T, 3 * t + 2))
            dve.wait_ge(pv_done, place.unit(u))
            dve.wait_ge(x_step[layer], place.nth(T, t))
            nc.vector.tensor_tensor(o_sb[layer][:, :].rearrange("p (h d) -> p h d", h=heads),
                                    o_bank[k % 2][:, :].rearrange("p (h d) -> p h d", h=heads),
                                    rinv[layer][:, :].unsqueeze(2).broadcast_to([P, heads, dh]),
                                    ALU.mult).then_inc(end_step[layer], 1)
        elif kind == "f_mm" and what[2] == 1:
            dve.wait_ge(filled["d"], place.count(BANK_NO["d"], what, 1, 1))
            dve.wait_ge(f_step, place.nth(2 * T, 2 * what[1]))
            nc.vector.tensor_tensor(f_out[:, :], misc["d"][:, :], ffn_bias[:, :], ALU.add).then_inc(freed["d"], 1)
        elif kind == "y_out":
            t = what[1]
            dve.wait_ge(normed["y"], place.count(NORM_NO["y"], ("norm", "y", t), 1, 1))
            nc.vector.tensor_reduce(yall[:, bass.ds(place.bi * T + t, 1)], xn["y"][:, :], AX.X, ALU.max,
                                    apply_absolute_value=True).then_inc(y_max, 1)
        elif kind == "bias":
            par = place.next_par
            col = seq_f[:, 0:1] if place.bi is None else seq_f[:, bass.ds(place.next_b, 1)]
            dve.wait_ge(mask_in, 16 if place.bi is None else place.bi * 16 + 32)
            nc.vector.tensor_scalar(nbias[:, par, 0, :], iota[:, :], col, MASK0, ALU.is_ge, ALU.mult).then_inc(bias_step, 1)
            nc.vector.tensor_scalar(nbias[:, par, 1, :], mask_row(par), -MASK1, MASK1, ALU.mult, ALU.add).then_inc(bias_step, 1)
            dve.wait_ge(bias_step, place.count(BIAS_NO, what, 4, 2))
            nc.vector.tensor_tensor(nbias[:, par, 0, :], nbias[:, par, 0, :], b0_row[:, :], ALU.subtract).then_inc(bias_step, 1)
            nc.vector.tensor_scalar(nbias[:, par, 1, :], nbias[:, par, 1, :], b1_col[:, 0:1], None,
                                    ALU.subtract).then_inc(bias_step, 1)
            dve.wait_ge(bias_step, place.count(BIAS_NO, what, 4, 4))

    def dve_program(dve):
        for s in (max_ready, lo_done, freed["d"], *stats.values(), *normed.values(), y_max, bias_step):
            dve.sem_inc(s, OFF)
        for s in end_step:
            dve.sem_inc(s, OFF)
        dve.wait_ge(consts_in, N_CONSTS)
        nc.vector.tensor_copy(seq_f[:, :], seq_i[:, :]).then_inc(seq_ready, 1)
        nc.vector.memset(half[:, :], -0.5).then_inc(seq_ready, 1)
        dve.wait_ge(seq_ready, 2)
        dve.wait_ge(gates_ready, 1)
        for what in PROLOGUE:
            dve_job(dve, Place(), what)

        def slot(s, now, before):
            for place, what in steps_at(s, now, before, emptying_at):
                dve_job(dve, place, what)
            for place, u in units_at(s, now, before):
                dve_max(dve, place, u)
            for place, u in units_at(s, now, before, LAG_LO):
                dve_lo(dve, place, u)
            for place, what in steps_at(s, now, before, others_at):
                dve_job(dve, place, what)

        run_slots(dve, slot)

    def split_low(pool, place, j, numbers, what, src):
        pool.wait_ge(hi_part[j], place.count(numbers, what, 1, 1))
        high, low = high_and_low(j)
        nc.gpsimd.tensor_tensor(low, src.rearrange("p (h d) -> p h d", h=H0), high[:, :, 0, :].bitcast(F32),
                                ALU.subtract).then_inc(lo_part[j], 1)

    def pool_job(pool, place, what):
        kind = what[0]
        if kind == "norm":
            j, t = what[1:]
            n = NORM_NO[j]
            pool.wait_ge(stats[j], place.count(n, what, 2, 2))
            pool.wait_ge(normed[j], place.count(n, what))
            pool.sem_inc(held.pool, 1)
            nc.gpsimd.tensor_scalar(rstd[j][:, 0:1], mv[j][:, 1:2], EPS, None, ALU.add).then_inc(rs_step[j], 1)
            pool.wait_ge(rs_step[j], place.count(n, what, 3, 1))
            nc.gpsimd.tensor_tensor(rstd[j][:, 1:2], rstd[j][:, 0:1], half[:, :], ALU.pow).then_inc(rs_step[j], 1)
            pool.wait_ge(rs_step[j], place.count(n, what, 3, 2))
            pool.sem_inc(held.pool, 1)
            nc.gpsimd.tensor_scalar(rstd[j][:, 2:3], rstd[j][:, 1:2], Q_SCALE[t[0]] if j == "q" else 1.0, None,
                                    ALU.mult).then_inc(rs_step[j], 1)
        elif kind == "q_split":
            split_low(pool, place, "q", NORM_NO["q"], ("norm", "q", what[1]), xn["q"][:, :])
        elif kind == "kv_split":
            kc = what[1]
            pool.wait_ge(kv_in[kc % 2], kv_loaded(place, kc))
            split_low(pool, place, "k", KV_NO, what, kv[:, kc % 2, 0:D])
            vals, out = kv[:, kc % 2, D:2 * D], v[:, place.next_par, kc]
            if place.bi is not None:
                pool.wait_ge(pv_done, place.unit(-1))
            pool.sem_inc(held.pool, 1)
            nc.gpsimd.tensor_scalar(out[:, 0, :], vals, 1.0, 1.0, ALU.mult, ALU.mult).then_inc(v_step, 1)
            pool.wait_ge(v_step, place.count(KV_NO, what, 4, 1))
            nc.gpsimd.tensor_tensor(v_rest[:, :], vals, out[:, 0, :], ALU.subtract).then_inc(v_step, 1)
            pool.wait_ge(v_step, place.count(KV_NO, what, 4, 2))
            pool.sem_inc(held.pool, 1)
            nc.gpsimd.tensor_scalar(out[:, 1, :], v_rest[:, :], 1.0, 1.0, ALU.mult, ALU.mult).then_inc(v_step, 1)
            pool.wait_ge(v_step, place.count(KV_NO, what, 4, 3))
            nc.gpsimd.tensor_tensor(out[:, 2, :], v_rest[:, :], out[:, 1, :], ALU.subtract).then_inc(v_step, 1)
            pool.wait_ge(v_step, place.count(KV_NO, what, 4, 4))
        elif kind in ("end0", "end1"):
            layer, t = int(kind[3]), what[1]
            xt = x[:, place.par, t, :]
            pool.wait_ge(end_step[layer], place.nth(3 * T, 3 * t + 3))
            nc.gpsimd.tensor_tensor(xt, xt, o_sb[layer][:, :], ALU.add).then_inc(x_step[layer], 1)
        elif kind == "f_out":
            t = what[1]
            xt = x[:, place.par, t, :]
            pool.wait_ge(f_tanh, place.nth(T, t + 1))
            pool.sem_inc(held.pool, 1)
            nc.gpsimd.tensor_scalar(f_out[:, :], f_out[:, :], gates[:, 2:3], 1.0, ALU.mult, ALU.mult).then_inc(f_step, 1)
            pool.wait_ge(f_step, place.nth(2 * T, 2 * t + 1))
            nc.gpsimd.tensor_tensor(xt, xt, f_out[:, :], ALU.add).then_inc(f_step, 1)

    def pool_program(pool):
        for s in (*rs_step.values(), *lo_part.values(), v_step, *x_step, f_step):
            pool.sem_inc(s, OFF)
        pool.wait_ge(seq_ready, 2)
        pool.wait_ge(gates_ready, 1)
        for what in PROLOGUE:
            pool_job(pool, Place(), what)

        def slot(s, now, before):
            for place, what in steps_at(s, now, before):
                pool_job(pool, place, what)

        run_slots(pool, slot)

    def rows(ap, b):
        return ap[b].rearrange("(t p) d -> p t d", p=P)

    def spread(ap, n):
        return ap.partition_broadcast(P)

    def sp_program(sp):
        sp.sem_inc(x_store, 16)
        sp.sem_inc(y_store, 16)
        sp.dma_start(iota[:, :], dram["iota"].partition_broadcast(P)).then_inc(consts_in, 16)
        sp.dma_start(b0_row[:, :], dram["L0_xattn_b"].partition_broadcast(P)).then_inc(consts_in, 16)
        sp.dma_start(b1_col[:, :], dram["L1_xattn_b"].partition_broadcast(P)).then_inc(consts_in, 16)
        sp.dma_start(ffn_bias[:, :], dram["L0_ffn_bias"].partition_broadcast(P)).then_inc(consts_in, 16)
        sp.dma_start(seq_i[:, :], dram["itok_Bx1_68_817"].rearrange("b o -> (b o)").partition_broadcast(P)).then_inc(consts_in, 16)
        sp.dma_start(gates[:, 0:2], dram["g_xattn"].partition_broadcast(P)).then_inc(consts_in, 16)
        sp.dma_start(gates[:, 2:4], dram["g_ffn"].partition_broadcast(P)).then_inc(consts_in, 16)
        sp.dma_start(x[:, 0, :, :], rows(dram["x"], 0)).then_inc(x_in[0], 16)
        sp.dma_start(mask_row(0), dram["mask_BxS2_ik0"][0].partition_broadcast(P)).then_inc(mask_in, 16)
        for kc in range(T):
            load_kv(sp, Place(), kc)
        with sp.Fori(0, B // 2) as pair:
            for par in (0, 1):
                place = Place(pair, par)
                sp.wait_ge(x_store, place.bi * (16 * T) + 16)
                sp.wait_ge(x_step[1], place.nth(T, 0))
                sp.dma_start(x[:, 1 - par, :, :], rows(dram["x"], place.next_b)).then_inc(x_in[1 - par], 16)
                sp.wait_ge(max_ready, place.unit(-1))
                sp.dma_start(mask_row(1 - par), dram["mask_BxS2_ik0"][place.next_b].partition_broadcast(P)).then_inc(mask_in, 16)
                for what in JOBS:
                    if what[0] == "kv_split":
                        load_kv(sp, place, what[1])
                    elif what[0] == "y_out":
                        t = what[1]
                        sp.wait_ge(x_step[1], place.nth(T, t + 1))
                        sp.dma_start(dram["x_mid"][place.bi * T + t], x[:, par, t, :]).then_inc(x_store, 16)
                        sp.wait_ge(normed["y"], place.count(NORM_NO["y"], ("norm", "y", t), 1, 1))
                        sp.dma_start(dram["y_mid"][place.bi * T + t], xn["y"][:, :]).then_inc(y_store, 16)
        sp.wait_ge(x_store, 16 * (B * T + 1))
        sp.wait_ge(y_store, 16 * (B * T + 1))

    def load_kv(sp, place, kc):
        if place.bi is not None or kc >= 2:
            what = ("kv_split", kc)
            sp.wait_ge(hi_part["k"], place.count(KV_NO, what, 1, -1))
            sp.sem_inc(held.sp, 1)
            sp.wait_ge(v_step, place.count(KV_NO, what, 4, -4))
        sp.dma_start(kv[:, kc % 2, :], dram["ctx_2048"][place.next_b, P * kc:P * kc + P, :]).then_inc(kv_in[kc % 2], 16)

    return pe_program, act_program, dve_program, pool_program, sp_program


I = 1536
N_BLK = B * S // 512
IT = I // P
PAIRS = IT // 2
GROUPS = IT // 4
QMAX = 32767.0
WMAX = 7.0
WBLK = 32
SIG = 65536.0
ROUND = 1.5 * 2 ** 23
TINY = 1e-12
SCALARS = ("x_scale", "x_inv", "gate_scale", "gate_c", "g2_unit", "g2_scale", "g2_c", "up_scale", "up_c",
           "o_unit", "o_scale", "o_c", "out_factor")


class Turns:

    def __init__(self, nc, sb, sem, held, name, banks, ident):
        self.nc, self.held, self.banks, self.ident = nc, held, banks, ident
        self.raw = sb(name + "_raw", [P, 2, D], F32)
        self.src = sb(name + "_src", [P, 2, D], F32)
        self.size = sb(name + "_size", [P, 2, D // WBLK], F32)
        self.scale = sb(name + "_scale", [P, 2, D // WBLK], F32)
        self.inv = sb(name + "_inv", [P, 2, D // WBLK], F32)
        self.loaded = [sem(name + "_loaded0"), sem(name + "_loaded1")]
        self.w_step = sem(name + "_w_step")
        self.quantised = sem(name + "_quantised")
        self.restored = sem(name + "_restored")
        self.turned = sem(name + "_turned")
        self.high = sem(name + "_high")
        self.low = sem(name + "_low")

    def load(self, sp, n, k, source):
        sp.wait_ge(self.restored, n - 1 + OFF)
        sp.dma_start(self.raw[:, k, :], source).then_inc(self.loaded[k], 16)

    def quantise_x(self, dve, n, half_n, k, x_inv):
        dve.wait_ge(self.loaded[k], 16 * half_n + 16)
        self.nc.vector.tensor_scalar(self.raw[:, k, :], self.raw[:, k, :], x_inv[:, 0:1], ROUND,
                                     ALU.mult, ALU.add).then_inc(self.quantised, 1)

    def quantise_w(self, dve, n, half_n, n4, k):
        size, scale, inv = self.size[:, k, :], self.scale[:, k, :], self.inv[:, k, :]
        dve.wait_ge(self.loaded[k], 16 * half_n + 16)
        self.nc.vector.tensor_reduce(size, self.raw[:, k, :].rearrange("p (b w) -> p b w", w=WBLK), AX.X, ALU.max,
                                     apply_absolute_value=True).then_inc(self.w_step, 1)
        dve.wait_ge(self.restored, n - 1 + OFF)
        dve.wait_ge(self.w_step, n4 + 1 + OFF)
        self.nc.vector.tensor_scalar(scale, size, 1.0 / WMAX, TINY, ALU.mult, ALU.max).then_inc(self.w_step, 1)
        dve.wait_ge(self.w_step, n4 + 2 + OFF)
        self.nc.vector.reciprocal(inv, scale).then_inc(self.w_step, 1)
        dve.wait_ge(self.w_step, n4 + 3 + OFF)
        blocks = self.raw[:, k, :].rearrange("p (b w) -> p b w", w=WBLK)
        self.nc.vector.tensor_tensor(blocks, blocks, inv.unsqueeze(2).broadcast_to([P, D // WBLK, WBLK]),
                                     ALU.mult).then_inc(self.w_step, 1)
        dve.wait_ge(self.w_step, n4 + 4 + OFF)
        self.nc.vector.tensor_scalar(self.raw[:, k, :], self.raw[:, k, :], ROUND, -ROUND, ALU.add,
                                     ALU.add).then_inc(self.quantised, 1)

    def restore_x(self, pool, n, k):
        pool.wait_ge(self.quantised, n + 1 + OFF)
        pool.wait_ge(self.turned, n - 1 + OFF)
        pool.sem_inc(self.held.pool, 1)
        self.nc.gpsimd.tensor_scalar(self.src[:, k, :], self.raw[:, k, :], -ROUND, 1.0, ALU.add,
                                     ALU.mult).then_inc(self.restored, 1)

    def restore_w(self, pool, n, k):
        pool.wait_ge(self.quantised, n + 1 + OFF)
        pool.wait_ge(self.turned, n - 1 + OFF)
        self.nc.gpsimd.tensor_tensor(self.src[:, k, :].rearrange("p (b w) -> p b w", w=WBLK),
                                     self.raw[:, k, :].rearrange("p (b w) -> p b w", w=WBLK),
                                     self.scale[:, k, :].unsqueeze(2).broadcast_to([P, D // WBLK, WBLK]),
                                     ALU.mult).then_inc(self.restored, 1)

    def transpose(self, pe, n, k):
        pe.wait_ge(self.restored, n + 1 + OFF)
        pe.wait_ge(self.low, n - 1 + OFF)
        for c in range(4):
            last = self.nc.tensor.transpose(self.banks[k][:, P * c:P * c + P], self.src[:, k, P * c:P * c + P],
                                            self.ident[:, :])
        last.then_inc(self.turned, 1)

    def put_high(self, act, n, k, out):
        act.wait_ge(self.turned, n + 1 + OFF)
        act.sem_inc(self.held.act, 1)
        self.nc.scalar.activation(out, self.banks[k][:, :].rearrange("p (c i) -> p c i", i=P),
                                  ACT.Copy).then_inc(self.high, 1)

    def put_low(self, dve, n, k, out, high):
        dve.wait_ge(self.high, n + 1 + OFF)
        self.nc.vector.tensor_tensor(out, self.banks[k][:, :].rearrange("p (c i) -> p c i", i=P),
                                     high.bitcast(F32), ALU.subtract).then_inc(self.low, 1)

    def start(self, engines):
        for eng, s in (("dve", self.quantised), ("dve", self.w_step), ("dve", self.low), ("pool", self.restored),
                       ("pe", self.turned), ("act", self.high)):
            if eng in engines:
                engines[eng].sem_inc(s, OFF)


class Scales:

    def __init__(self, nc, sem, name):
        self.nc, self.step, self.n = nc, sem(name), 0

    def then(self, dve, inst):
        inst.then_inc(self.step, 1)
        self.n += 1
        dve.wait_ge(self.step, self.n)

    def mult(self, dve, out, a, b):
        self.then(dve, self.nc.vector.tensor_scalar(out[:, 0:1], a[:, 0:1], b if isinstance(b, float) else b[:, 0:1],
                                                    None, ALU.mult))

    def scale(self, dve, scale, size, unit, c):
        self.mult(dve, c, size, unit)
        self.then(dve, self.nc.vector.tensor_scalar(scale[:, 0:1], c[:, 0:1], 1.0 / QMAX, TINY, ALU.mult, ALU.max))
        self.then(dve, self.nc.vector.reciprocal(c[:, 0:1], scale[:, 0:1]))
        self.mult(dve, c, c, unit)


def quantised_products(nc, sb, sem, held, dram, banks, ident, sc, w_hl, name, acc_name, gate_q, first_w, next_w):
    up = gate_q is not None
    turns = Turns(nc, sb, sem, held, name, [banks[6], banks[7]], ident)
    acc = [(banks[2 * k], banks[2 * k + 1]) for k in range(3)]
    x_hl = sb(name + "_x_hl", [P, 2, 2, C, 512], F32R)
    out = sb(name + "_out", [P, 2, 2, 512], F32)
    cols = sb(name + "_cols", [P, N_BLK * PAIRS], F32)
    tops = sb(name + "_tops", [P, 4], F32)
    acc_ready, acc_out, acc_max = sem(name + "_acc_ready"), sem(name + "_acc_out"), sem(name + "_acc_max")
    stored = [sem(name + "_stored0"), sem(name + "_stored1")]
    col_top, top = sem(name + "_col_top"), sem(name + "_top")
    scales = Scales(nc, sem, name + "_scales")
    n_first = IT if first_w else 0
    per_block = 6 if next_w else 4
    if up:
        work = sb(name + "_work", [P, 3, 1024], F32)
        cols2 = sb(name + "_cols2", [P, N_BLK * PAIRS], F32)
        gate_in = [sem(f"{name}_gate_in{k}") for k in range(3)]
        gate_done, sigmoid_done = sem(name + "_gate_done"), sem(name + "_sigmoid_done")
        sig_done = sem(name + "_sig_done")
        g2_done, g2_max = sem(name + "_g2_done"), sem(name + "_g2_max")

    class Item:

        def __init__(self, blk, par, s, idx):
            before = n_first + 4 + per_block * par + idx
            self.n, self.half_n = two_n(per_block, blk, par, before)
            self.slot, self.par = before % 2, par
            self.kind, self.j = ("w", s // 5) if s in (0, 5) else ("x", s - 1)
            self.blk = blk

    def two_n(per, two, par, before):
        return two * (2 * per) + before, two * per + before // 2

    def items_of(two, par):
        steps = range(0, 6) if next_w else range(1, 5)
        return {s: Item(two, par, s, idx) for idx, s in enumerate(steps)}

    def w_item_tile(item):
        return (4 * item.blk + (2 * item.par + item.j)) % IT

    def w_dst(w, part, i):
        return w[:, part, :, bass.ds(i * P, P)]

    def x_dst(par, part, j):
        return x_hl[:, par, part, :, P * j:P * j + P]

    def item_dst(item, part):
        return w_dst(next_w[1], part, w_item_tile(item)) if item.kind == "w" else x_dst(1 - item.par, part, item.j)

    def load_item(sp, item):
        if item.kind == "w":
            source = next_w[0][bass.ds(w_item_tile(item) * P, P), :]
        else:
            source = dram["y_mid"][((2 * item.blk + item.par + 1) % N_BLK) * 4 + item.j]
        turns.load(sp, item.n, item.slot, source)

    def every_step(eng, step, lag=0):
        def blocks(two, at):
            for par in (0, 1):
                for s in range(PAIRS):
                    step(two, par, s, at(12 * two + 6 * par + s))

        blocks(0, lambda u: lambda k: u - k if u >= k else None)
        with eng.Fori(1, N_BLK // 2) as two:
            blocks(two, lambda u: lambda k: u - k)
        for s in range(lag):
            u = N_BLK * PAIRS + s
            step(N_BLK // 2, 0, s, lambda k, u=u: u - k if k and u - k < N_BLK * PAIRS else None)

    def first_x():
        return [(n_first + j, (n_first + j) // 2, j % 2, j) for j in range(4)]

    def sp_program(sp):
        if first_w:
            with sp.Fori(0, 3) as r:
                for k in range(4):
                    turns.load(sp, 4 * r + k, k % 2, first_w[0][bass.ds((4 * r + k) * P, P), :])
        for n, half_n, k, j in first_x():
            turns.load(sp, n, k, dram["y_mid"][j])
        for s in stored:
            sp.sem_inc(s, 16)

        def step(two, par, s, at):
            u, items = at(0), items_of(two, par)
            if s == 0 and next_w:
                load_item(sp, items[0])
            if s + 1 in items:
                load_item(sp, items[s + 1])
            if up:
                sp.wait_ge(g2_max, u - 2 + OFF)
                sp.dma_start(work[:, s % 3, :], dram["gate"][u]).then_inc(gate_in[s % 3], 16)
            sp.wait_ge(acc_out, u + 1 + OFF)
            sp.dma_start(dram[acc_name][u], out[:, s % 2, :, :].rearrange("p a i -> p (a i)")).then_inc(stored[s % 2], 16)

        every_step(sp, step)
        for s in stored:
            sp.wait_ge(s, 16 * (N_BLK * PAIRS // 2 + 1))

    def pe_program(pe):
        turns.start({"pe": pe})
        pe.sem_inc(acc_ready, OFF)
        if first_w:
            with pe.Fori(0, 3) as r:
                for k in range(4):
                    turns.transpose(pe, 4 * r + k, k % 2)
        for n, _, k, j in first_x():
            turns.transpose(pe, n, k)

        def step(two, par, s, at):
            u, items = at(0), items_of(two, par)
            if s == 0:
                x_done = n_first + 4 + per_block * (2 * two + par) - (1 if next_w else 0)
                if isinstance(two, int) and two == 0 and par == 0:
                    x_done = n_first + 4
                pe.wait_ge(turns.high, x_done + OFF)
                pe.wait_ge(turns.low, x_done + OFF)
            pe.wait_ge(acc_out, u - 2 + OFF)
            pe.wait_ge(acc_max, u - 2 + OFF)
            for half in (0, 1):
                i = 2 * s + half
                terms = [(a, b, c) for a, b in ((0, 0), (0, 1), (1, 0)) for c in range(C)]
                for t, (a, b, c) in enumerate(terms):
                    last = nc.tensor.matmul(acc[s % 3][half][:, :], w_hl[:, a, c, P * i:P * i + P],
                                            x_hl[:, par, b, c, :], start=(t == 0), stop=(t == len(terms) - 1))
            last.then_inc(acc_ready, 1)
            if s in items:
                turns.transpose(pe, items[s].n, items[s].slot)

        every_step(pe, step)

    def last_items(two, par, s):
        if s:
            items = items_of(two, par)
            return [items[s - 1]] if s - 1 in items else []
        if not next_w or (isinstance(two, int) and two == 0 and par == 0):
            return []
        return [items_of(two, 0)[5]] if par else [items_of(two - 1, 1)[5]]

    def act_program(act):
        turns.start({"act": act})
        act.sem_inc(acc_out, OFF)
        if up:
            act.sem_inc(gate_done, OFF)
            act.sem_inc(sigmoid_done, OFF)
        if first_w:
            with act.Fori(0, 3) as r:
                for k in range(4):
                    turns.put_high(act, 4 * r + k, k % 2, w_dst(first_w[1], 0, 4 * r + k))
        for n, _, k, j in first_x():
            turns.put_high(act, n, k, x_dst(0, 0, j))

        def step(two, par, s, at):
            u = at(0)
            if u is not None or s == 0:
                for item in last_items(two, par, s):
                    if item.kind == "x":
                        act.wait_ge(acc_ready, 12 * two + (6 * par + OFF))
                    turns.put_high(act, item.n, item.slot, item_dst(item, 0))
            if u is not None:
                act.wait_ge(acc_ready, u + 1 + OFF)
                act.wait_ge(stored[s % 2], 96 * two + (48 * par + 16 * (s // 2) + 16))
                act.wait_ge(acc_max, u - 1 + OFF)
                for half in (0, 1):
                    last = nc.scalar.activation(out[:, s % 2, half, :], acc[s % 3][half][:, :], ACT.Copy)
                last.then_inc(acc_out, 1)
            if up and at(1) is not None:
                u, k = at(1), (s - 1) % 3
                gq = gate_q[:, bass.ds(u, 1), :].rearrange("p a i -> p (a i)")
                loads = 64 * two + (32 * par + 16 * ((s - 1) // 3) + 16)
                act.wait_ge(gate_in[k], loads)
                act.sem_inc(held.act, 1)
                nc.scalar.activation(gq, work[:, k, :], ACT.Copy, scale=sc["gate_c"][:, 0:1]).then_inc(gate_done, 1)
                act.wait_ge(gate_done, u + 1 + OFF)
                act.sem_inc(held.act, 1)
                nc.scalar.activation(work[:, k, :], gq, ACT.Sigmoid, scale=sc["gate_scale"][:, 0:1]).then_inc(sigmoid_done, 1)

        every_step(act, step, 2 if up else 1)

    def dve_program(dve):
        turns.start({"dve": dve})
        dve.sem_inc(acc_max, OFF)
        if up:
            dve.sem_inc(g2_done, OFF)
            dve.sem_inc(g2_max, OFF)
        else:
            nc.vector.tensor_reduce(tops[:, 0:1], dram["yall"][:, :], AX.X, ALU.max).then_inc(col_top, 1)
            dve.wait_ge(top, 1)
            scales.scale(dve, sc["x_scale"], tops[:, 1:2], 1.0, sc["x_inv"])
        if first_w:
            with dve.Fori(0, 3) as r:
                for k in range(4):
                    n = 4 * r + k
                    turns.quantise_w(dve, n, 2 * r + k // 2, 16 * r + 4 * k, k % 2)
                    if k:
                        turns.put_low(dve, n - 1, (k - 1) % 2, w_dst(first_w[1], 1, 4 * r + k - 1),
                                      w_dst(first_w[1], 0, 4 * r + k - 1))
                turns.put_low(dve, 4 * r + 3, 1, w_dst(first_w[1], 1, 4 * r + 3), w_dst(first_w[1], 0, 4 * r + 3))
        for n, half_n, k, j in first_x():
            turns.quantise_x(dve, n, half_n, k, sc["x_inv"])
            turns.put_low(dve, n, k, x_dst(0, 1, j), x_dst(0, 0, j))

        def step(two, par, s, at):
            u, items = at(0), items_of(two, par)
            if u is not None and s in items:
                item = items[s]
                if item.kind == "w":
                    turns.quantise_w(dve, item.n, item.half_n, 4 * n_first + 16 * two + (8 * par + 4 * item.j), item.slot)
                else:
                    turns.quantise_x(dve, item.n, item.half_n, item.slot, sc["x_inv"])
            if u is not None or s == 0:
                for item in last_items(two, par, s):
                    turns.put_low(dve, item.n, item.slot, item_dst(item, 1), item_dst(item, 0))
            if u is not None:
                dve.wait_ge(acc_out, u + 1 + OFF)
                nc.vector.tensor_reduce(cols[:, bass.ds(u, 1)], out[:, s % 2, :, :].rearrange("p a i -> p (a i)"), AX.X,
                                        ALU.max, apply_absolute_value=True).then_inc(acc_max, 1)
            if up and at(2) is not None:
                u, w = at(2), work[:, (s - 2) % 3, :]
                dve.wait_ge(gate_done, u + 1 + OFF)
                dve.wait_ge(sig_done, u + 1 + OFF)
                nc.vector.scalar_tensor_tensor(w, w.bitcast(I32), SIG - 1, gate_q[:, bass.ds(u, 1), :].rearrange(
                    "p a i -> p (a i)"), ALU.min, ALU.mult).then_inc(g2_done, 1)
                dve.wait_ge(g2_done, u + 1 + OFF)
                nc.vector.tensor_reduce(cols2[:, bass.ds(u, 1)], w, AX.X, ALU.max,
                                        apply_absolute_value=True).then_inc(g2_max, 1)

        every_step(dve, step, 2 if up else 1)
        dve.wait_ge(acc_max, N_BLK * PAIRS + OFF)
        nc.vector.tensor_reduce(tops[:, 2:3], cols[:, :], AX.X, ALU.max).then_inc(col_top, 1)
        dve.wait_ge(top, 1 if up else 2)
        if not up:
            scales.scale(dve, sc["gate_scale"], tops[:, 3:4], sc["x_scale"], sc["gate_c"])
        else:
            scales.scale(dve, sc["up_scale"], tops[:, 3:4], sc["x_scale"], sc["up_c"])
            scales.mult(dve, sc["g2_unit"], sc["gate_scale"], 1.0 / SIG)
            dve.wait_ge(g2_max, N_BLK * PAIRS + OFF)
            nc.vector.tensor_reduce(tops[:, 0:1], cols2[:, :], AX.X, ALU.max).then_inc(col_top, 1)
            dve.wait_ge(top, 2)
            scales.scale(dve, sc["g2_scale"], tops[:, 1:2], sc["g2_unit"], sc["g2_c"])
            scales.mult(dve, sc["o_unit"], sc["g2_scale"], sc["up_scale"])

    def pool_program(pool):
        turns.start({"pool": pool})
        if up:
            pool.sem_inc(sig_done, OFF)
        else:
            pool.wait_ge(col_top, 1)
            nc.gpsimd.partition_all_reduce(tops[:, 1:2], tops[:, 0:1], P, RMAX).then_inc(top, 1)
        if first_w:
            with pool.Fori(0, 3) as r:
                for k in range(4):
                    turns.restore_w(pool, 4 * r + k, k % 2)
        for n, _, k, j in first_x():
            turns.restore_x(pool, n, k)

        def step(two, par, s, at):
            u, items = at(0), items_of(two, par)
            if u is not None and s in items:
                restore = turns.restore_w if items[s].kind == "w" else turns.restore_x
                restore(pool, items[s].n, items[s].slot)
            if up and at(1) is not None:
                u, w = at(1), work[:, (s - 1) % 3, :]
                pool.wait_ge(sigmoid_done, u + 1 + OFF)
                pool.sem_inc(held.pool, 1)
                nc.gpsimd.tensor_scalar(w.bitcast(I32), w, SIG, 1.0, ALU.mult, ALU.mult).then_inc(sig_done, 1)

        every_step(pool, step, 1 if up else 0)
        pool.wait_ge(col_top, 1 if up else 2)
        nc.gpsimd.partition_all_reduce(tops[:, 3:4], tops[:, 2:3], P, RMAX).then_inc(top, 1)
        if up:
            pool.wait_ge(col_top, 2)
            nc.gpsimd.partition_all_reduce(tops[:, 1:2], tops[:, 0:1], P, RMAX).then_inc(top, 1)

    return pe_program, act_program, dve_program, pool_program, sp_program


N_GRP = N_BLK * GROUPS


def product_sizes(nc, sb, sem, held, dram, banks, ident, sc, w_hl, gate_q, gates):
    turns = Turns(nc, sb, sem, held, "b", [banks[6], banks[7]], ident)
    up_f = sb("up_f", [P, 2, 2048], F32)
    work = sb("b_work", [P, 3, 2048], F32)
    up_q = sb("b_up_q", [P, 2, 2048], I16)
    cols = sb("b_cols", [P, N_GRP], F32)
    tops = sb("b_tops", [P, 2], F32)
    up_in = [sem("up_in0"), sem("up_in1")]
    stored = [sem("b_stored0"), sem("b_stored1")]
    sigmoid_done, g2_quantised = sem("b_sigmoid_done"), sem("g2_quantised")
    up_quantised = sem("up_quantised")
    g2_done, o_done, o_max = sem("b_g2_done"), sem("b_o_done"), sem("b_o_max")
    sig_done = sem("b_sig_done")
    col_top, top = sem("b_col_top"), sem("b_top")
    scales = Scales(nc, sem, "b_scales")
    w_down = dram["L1_ffn_w_down"]
    g_all = gate_q[:, :, :].rearrange("p u i -> p (u i)")

    def loads(n, slot):
        return 8 * (n - slot) + 16

    def gq(n):
        return g_all[:, bass.ds(n * 2048, 2048)]

    def w_dst(part, g, r):
        return w_hl[:, part, bass.ds(4 * g, 4), P * r:P * r + P]

    def each_group(eng, step):
        for i in range(6):
            step(i, i, lambda lag, i=i: i - lag if i >= lag else None)
        with eng.Fori(1, N_GRP // 6) as six:
            for k in range(6):
                step(6 * six + k, k, lambda lag, k=k: 6 * six + (k - lag))
        for i in (N_GRP, N_GRP + 1):
            step(i, i % 6, lambda lag, i=i: i - lag if i - lag < N_GRP else None)

    def sp_program(sp):
        for s in stored:
            sp.sem_inc(s, 16)
        with sp.Fori(0, GROUPS) as g:
            for r in range(4):
                turns.load(sp, 4 * g + r, r % 2, w_down[P * r:P * r + P, bass.ds(g * 512, 512)])

        def step(i, k, at):
            n = at(0)
            if n is not None:
                sp.wait_ge(o_max, n - 1 + OFF)
                sp.dma_start(up_f[:, k % 2, :].rearrange("p (u i) -> p u i", u=2),
                             dram["up"][bass.ds(2 * n, 2)].rearrange("u p i -> p u i")).then_inc(up_in[k % 2], 16)
            n = at(2)
            if n is not None:
                sp.wait_ge(up_quantised, n + 1 + OFF)
                sp.dma_start(dram["up_q"][n], up_q[:, k % 2, :]).then_inc(stored[k % 2], 16)

        each_group(sp, step)
        for s in stored:
            sp.wait_ge(s, 16 * (N_GRP // 2 + 1))

    def pe_program(pe):
        turns.start({"pe": pe})
        with pe.Fori(0, GROUPS) as g:
            for r in range(4):
                turns.transpose(pe, 4 * g + r, r % 2)

    def act_program(act):
        turns.start({"act": act})
        for s in (sigmoid_done, g2_quantised, up_quantised):
            act.sem_inc(s, OFF)
        with act.Fori(0, GROUPS) as g:
            for r in range(4):
                turns.put_high(act, 4 * g + r, r % 2, w_dst(0, g, r))

        def step(i, k, at):
            n = at(0)
            if n is not None:
                act.wait_ge(g2_quantised, n - 2 + OFF)
                act.sem_inc(held.act, 1)
                nc.scalar.activation(work[:, k % 3, :], gq(n), ACT.Sigmoid,
                                     scale=sc["gate_scale"][:, 0:1]).then_inc(sigmoid_done, 1)
            n = at(2)
            if n is not None:
                act.wait_ge(up_in[k % 2], loads(n, k % 2))
                act.wait_ge(stored[k % 2], loads(n, k % 2))
                nc.scalar.activation(up_q[:, k % 2, :], up_f[:, k % 2, :], ACT.Copy,
                                     scale=sc["up_c"][:, 0:1]).then_inc(up_quantised, 1)
                act.wait_ge(g2_done, n + 1 + OFF)
                act.sem_inc(held.act, 1)
                nc.scalar.activation(gq(n), work[:, (k - 2) % 3, :], ACT.Copy,
                                     scale=sc["g2_c"][:, 0:1]).then_inc(g2_quantised, 1)

        each_group(act, step)

    def dve_program(dve):
        turns.start({"dve": dve})
        for s in (g2_done, o_done, o_max):
            dve.sem_inc(s, OFF)
        with dve.Fori(0, GROUPS) as g:
            for r in range(4):
                n = 4 * g + r
                turns.quantise_w(dve, n, 2 * g + r // 2, 16 * g + 4 * r, r % 2)
                if r:
                    turns.put_low(dve, n - 1, (r - 1) % 2, w_dst(1, g, r - 1), w_dst(0, g, r - 1))
            turns.put_low(dve, 4 * g + 3, 1, w_dst(1, g, 3), w_dst(0, g, 3))

        def step(i, k, at):
            n = at(1)
            if n is not None:
                dve.wait_ge(sig_done, n + 1 + OFF)
                w = work[:, (k - 1) % 3, :]
                nc.vector.scalar_tensor_tensor(w, w.bitcast(I32), SIG - 1, gq(n), ALU.min, ALU.mult).then_inc(g2_done, 1)
            n = at(2)
            if n is not None:
                dve.wait_ge(g2_quantised, n + 1 + OFF)
                dve.wait_ge(up_quantised, n + 1 + OFF)
                nc.vector.tensor_tensor(up_f[:, k % 2, :], gq(n), up_q[:, k % 2, :], ALU.mult).then_inc(o_done, 1)
                dve.wait_ge(o_done, n + 1 + OFF)
                nc.vector.tensor_reduce(cols[:, bass.ds(n, 1)], up_f[:, k % 2, :], AX.X, ALU.max,
                                        apply_absolute_value=True).then_inc(o_max, 1)

        each_group(dve, step)
        dve.wait_ge(o_max, N_GRP + OFF)
        nc.vector.tensor_reduce(tops[:, 0:1], cols[:, :], AX.X, ALU.max).then_inc(col_top, 1)
        dve.wait_ge(top, 1)
        scales.scale(dve, sc["o_scale"], tops[:, 1:2], sc["o_unit"], sc["o_c"])
        scales.mult(dve, sc["out_factor"], sc["o_scale"], gates[:, 3:4])

    def pool_program(pool):
        turns.start({"pool": pool})
        pool.sem_inc(sig_done, OFF)
        with pool.Fori(0, GROUPS) as g:
            for r in range(4):
                turns.restore_w(pool, 4 * g + r, r % 2)

        def step(i, k, at):
            n = at(0)
            if n is None:
                return
            w = work[:, k % 3, :]
            pool.wait_ge(sigmoid_done, n + 1 + OFF)
            pool.sem_inc(held.pool, 1)
            nc.gpsimd.tensor_scalar(w.bitcast(I32), w, SIG, 1.0, ALU.mult, ALU.mult).then_inc(sig_done, 1)

        each_group(pool, step)
        pool.wait_ge(col_top, 1)
        nc.gpsimd.partition_all_reduce(tops[:, 1:2], tops[:, 0:1], P, RMAX).then_inc(top, 1)

    return pe_program, act_program, dve_program, pool_program, sp_program


def down_product(nc, sb, sem, held, dram, banks, sc, w_hl, gate_q):
    up_q = sb("c_up_q", [P, 3, 2048], I16)
    prod = sb("c_prod", [P, 2048], F32)
    o_hl = sb("o_hl", [P, 2, 2, 2048], F32R)
    res = sb("c_res", [P, 4, D], F32)
    up_in = [sem(f"c_up_in{k}") for k in range(3)]
    x_in = [sem(f"c_x_in{j}") for j in range(4)]
    stored = [sem(f"c_stored{j}") for j in range(4)]
    prod_done = sem("c_prod_done")
    o_quantised, high = sem("c_o_quantised"), sem("c_high")
    low = sem("c_low")
    o_used = sem("c_o_used")
    acc_ready = sem("c_acc_ready")
    acc_out = sem("c_acc_out")
    out = dram["out"].rearrange("b (t p) d -> (b t) p d", p=P)
    g_all = gate_q[:, :, :].rearrange("p u i -> p (u i)")
    SLOTS = 2 * GROUPS

    def two_blocks(eng, body):
        with eng.Fori(0, N_BLK // 2) as two:
            for k in range(SLOTS):
                body(SLOTS * two + k, k, two)

    def sp_program(sp):
        for s in stored:
            sp.sem_inc(s, 16)
        with sp.Fori(0, N_BLK) as b:
            for j in range(4):
                sp.wait_ge(stored[j], 16 * b + 16)
                sp.dma_start(res[:, j, :], dram["x_mid"][4 * b + j]).then_inc(x_in[j], 16)
            for j in range(4):
                sp.wait_ge(acc_out, 4 * b + (j + 1 + OFF))
                sp.dma_start(out[4 * b + j], res[:, j, :]).then_inc(stored[j], 16)
        for s in stored:
            sp.wait_ge(s, 16 * (N_BLK + 1))

    def pe_program(pe):
        pe.sem_inc(o_used, OFF)
        pe.sem_inc(acc_ready, OFF)

        def group(n, k, two):
            b, g = divmod(k, GROUPS)
            pe.wait_ge(high, n + 1 + OFF)
            pe.wait_ge(low, n + 1 + OFF)
            if g == 0:
                pe.wait_ge(acc_out, 8 * two + (4 * b - 4 + OFF))
            for i in range(4):
                for j in range(4):
                    for a, b_ in ((0, 0), (0, 1), (1, 0)):
                        last = nc.tensor.matmul(banks[4 * b + j][:, :],
                                                o_hl[:, k % 2, a, 512 * i + P * j:512 * i + P * j + P],
                                                w_hl[:, b_, 4 * g + i, :], start=(g == 0 and i == 0 and (a, b_) == (0, 0)),
                                                stop=(g == GROUPS - 1 and i == 3 and (a, b_) == (1, 0)))
                    if g == GROUPS - 1 and i == 3 and j < 3:
                        last.then_inc(acc_ready, 1)
            last.then_inc(o_used, 1)

        two_blocks(pe, group)

    def act_program(act):
        act.sem_inc(o_quantised, OFF)
        act.sem_inc(high, OFF)

        for n in range(2):
            nc.scalar.dma_start(up_q[:, n, :], dram["up_q"][n]).then_inc(up_in[n], 16)

        def group(n, k, two):
            act.wait_ge(low, n + OFF)
            nc.scalar.dma_start(up_q[:, (k + 2) % 3, :], dram["up_q"][(n + 2) % N_GRP]).then_inc(up_in[(k + 2) % 3], 16)
            act.wait_ge(prod_done, n + 1 + OFF)
            nc.scalar.activation(up_q[:, k % 3, :], prod[:, :], ACT.Copy, scale=sc["o_c"][:, 0:1]).then_inc(o_quantised, 1)
            act.wait_ge(o_quantised, n + 1 + OFF)
            act.wait_ge(o_used, n - 1 + OFF)
            nc.scalar.activation(o_hl[:, k % 2, 0, :], up_q[:, k % 3, :], ACT.Copy).then_inc(high, 1)

        two_blocks(act, group)
        for k in range(2):
            act.wait_ge(up_in[k], 16 * (N_GRP // 3 + 1))

    def dve_program(dve):
        dve.sem_inc(prod_done, OFF)
        dve.sem_inc(low, OFF)
        dve.sem_inc(acc_out, OFF)

        def product(n, k, two):
            dve.wait_ge(up_in[k % 3], 32 * two + (16 * (k // 3) + 16))
            dve.wait_ge(o_quantised, n + OFF)
            nc.vector.tensor_tensor(prod[:, :], g_all[:, bass.ds(n * 2048, 2048)], up_q[:, k % 3, :],
                                    ALU.mult).then_inc(prod_done, 1)

        def low_part(n, k):
            dve.wait_ge(high, n + 1 + OFF)
            nc.vector.tensor_tensor(o_hl[:, k % 2, 1, :], up_q[:, k % 3, :], o_hl[:, k % 2, 0, :].bitcast(F32),
                                    ALU.subtract).then_inc(low, 1)

        def results(b, two):
            for j in range(4):
                if j < 3:
                    dve.wait_ge(acc_ready, 6 * two + (3 * b + j + 1 + OFF))
                else:
                    dve.wait_ge(o_used, SLOTS * two + (GROUPS * (b + 1) + OFF))
                dve.wait_ge(x_in[j], 32 * two + (16 * b + 16))
                nc.vector.scalar_tensor_tensor(res[:, j, :], banks[4 * b + j][:, :], sc["out_factor"][:, 0:1], res[:, j, :],
                                               ALU.mult, ALU.add).then_inc(acc_out, 1)

        def steps(two, last):
            for k in range(SLOTS):
                n = SLOTS * two + k
                if not (last and k == SLOTS - 1):
                    product(n + 1, (k + 1) % SLOTS, two if k + 1 < SLOTS else two + 1)
                low_part(n, k)
                if k == GROUPS:
                    results(0, two)
                if k == 0 and not (isinstance(two, int) and two == 0):
                    results(1, two - 1)

        product(0, 0, 0)
        steps(0, False)
        with dve.Fori(1, N_BLK // 2 - 1) as two:
            steps(two, False)
        steps(N_BLK // 2 - 1, True)
        results(1, N_BLK // 2 - 1)

    def idle(_):
        pass

    return pe_program, act_program, dve_program, idle, sp_program


def run_block(nc, pe_program, act_program, dve_program, pool_program, sp_program):
    with nc.Block() as block:
        @block.sync
        def _(sp):
            sp_program(sp)

        @block.scalar
        def _(act):
            act_program(act)

        @block.tensor
        def _(pe):
            pe_program(pe)

        @block.vector
        def _(dve):
            dve_program(dve)

        @block.gpsimd
        def _(pool):
            pool_program(pool)


def build(nc, dram):
    with ExitStack() as ctx:
        def sem(name):
            return ctx.enter_context(nc.semaphore(name))

        def buffers(stage):
            return lambda name, shape, dt: stage.enter_context(nc.sbuf_tensor(name, shape, dt))

        sb = buffers(ctx)
        held = Held(sem)
        gates = sb("gates", [P, 4], F32)
        ident = sb("ident", [P, P], F32)
        dram["yall"] = sb("yall", [P, B * T], F32)
        sc = {name: sb("the_" + name, [P, 1], F32) for name in SCALARS}
        banks = [ctx.enter_context(nc.psum_tensor(f"bank{k}", [P, 512], F32)) for k in range(8)]
        phase = ctx.enter_context(ExitStack())
        w_ffn = phase.enter_context(nc.sbuf_tensor("w_ffn", [P, C, D], F32))
        with ExitStack() as stage:
            run_block(nc, *fold_weights(nc, buffers(stage), sem, dram, banks, ident, w_ffn))
        with ExitStack() as stage:
            one = phase1(nc, buffers(stage), sem, held, dram, gates, banks, ident, w_ffn)
            run_block(nc, *one)
        phase.close()
        w_hl = sb("w_hl", [P, 2 * C * I], F32R)
        up_hl = w_hl[:, :].rearrange("p (a c i) -> p a c i", a=2, c=C)
        down_hl = w_hl[:, :].rearrange("p (a i d) -> p a i d", a=2, i=IT)
        with ExitStack() as stage:
            gate_hl = buffers(stage)("gate_hl", [P, 2, C, I], F32R)
            run_block(nc, *quantised_products(nc, buffers(stage), sem, held, dram, banks, ident, sc, gate_hl, "gate_stage", "gate", None,
                                              (dram["L1_ffn_w_gate"], gate_hl), (dram["L1_ffn_w_up"], up_hl)))
        gate_q = sb("gate_q", [P, N_BLK * PAIRS, 1024], I16)
        with ExitStack() as stage:
            run_block(nc, *quantised_products(nc, buffers(stage), sem, held, dram, banks, ident, sc, up_hl, "up_stage", "up", gate_q,
                                              None, None))
        with ExitStack() as stage:
            run_block(nc, *product_sizes(nc, buffers(stage), sem, held, dram, banks, ident, sc, down_hl, gate_q, gates))
        with ExitStack() as stage:
            run_block(nc, *down_product(nc, buffers(stage), sem, held, dram, banks, sc, down_hl, gate_q))


INPUTS = ("x", "ctx_2048", "itok_Bx1_68_817", "mask_BxS2_ik0", "g_xattn", "g_ffn", "L0_xattn_b", "L0_ffn_weight",
          "L0_ffn_aux_weight1", "L0_ffn_aux_weight2", "L0_ffn_bias", "L1_xattn_b", "L1_ffn_w_gate", "L1_ffn_w_up",
          "L1_ffn_w_down")


def kernel(**inputs):
    import concourse.bacc as bacc
    from concourse.bass_utils import run_bass_kernel_spmd

    nc = bacc.Bacc("TRN2", target_bir_lowering=False, num_devices=1)
    arrays = {name: np.ascontiguousarray(inputs[name]) for name in INPUTS}
    arrays["ident"] = np.eye(P, dtype=np.float32)
    arrays["iota"] = np.arange(S, dtype=np.float32)
    dram = {name: nc.dram_tensor("in_" + name, a.shape, mybir.dt.from_np(a.dtype), kind="ExternalInput").ap()
            for name, a in arrays.items()}
    dram["out"] = nc.dram_tensor("out", (B, S, D), F32, kind="ExternalOutput").ap()
    for name, shape, dt in SCRATCH:
        dram[name] = nc.dram_tensor(name, shape, dt, kind="Internal").ap()
    build(nc, dram)
    return run_bass_kernel_spmd(nc, [{"in_" + name: a for name, a in arrays.items()}], core_ids=[0]).results[0]["out"]


SCRATCH = (("x_mid", (B * T, P, D), F32), ("y_mid", (B * T, P, D), F32), ("gate", (N_BLK * PAIRS, P, 1024), F32),
           ("up", (N_BLK * PAIRS, P, 1024), F32), ("up_q", (N_GRP, P, 2048), I16))
```

```python
from contextlib import ExitStack

import concourse.bass as bass
import numpy as np
from concourse import mybir

F32 = mybir.dt.float32
F32R = mybir.dt.float32r
BF16 = mybir.dt.bfloat16
F16 = mybir.dt.float16
I32 = mybir.dt.int32
I16 = mybir.dt.int16
U16 = mybir.dt.uint16
ALU = mybir.AluOpType
ACT = mybir.ActivationFunctionType
AX = mybir.AxisListType
RMAX = bass.bass_isa.ReduceOp.max

P = 128
B, S, D = 8, 512, 512
T = S // P
C = D // P
H0, H1 = 16, 8
DH0, DH1 = D // H0, D // H1
G = H0 // 4
OFF = 8
EPS = 1e-5
MASK0, MASK1 = 1e12, 1e30
BIG = 3e38

SEGMENTS = [(layer, t) for layer in (0, 1) for t in range(T)]
UNITS = [(k, layer, t, h) for k, (layer, t) in enumerate(SEGMENTS) for h in range(H1 if layer else H0)]
NU = len(UNITS)
START = {seg: next(u for u, x in enumerate(UNITS) if x[0] == k) for k, seg in enumerate(SEGMENTS)}
END = {seg: START[seg] + (H1 if seg[0] else H0) for seg in SEGMENTS}
Q_TILES = 2, 3
LAG_MAX, LAG_T, LAG_LO, LAG_PV = 1, 3, 4, 5
ST = 3 * DH0
NORMS = ("q", "f", "y")
Q_SCALE = (-DH0 ** -0.5, -DH1 ** -0.5)


class Held:

    def __init__(self, sem):
        self.act, self.dve, self.pool, self.sp = (sem("held_" + e) for e in ("act", "dve", "pool", "sp"))


def bank_of(what):
    if what[0].endswith("_turn") and what[0] != "f_turn":
        return "ad"[what[2] % 2]
    if what[0] == "f_turn":
        return "a"
    return "d" if what[0] == "f_mm" and what[2] == 1 else None


def holds(what):
    return "d" if what[0] == "f_mm" else bank_of(what)


def schedule():
    at, busy = {}, set()

    def put(slot, *what):
        at.setdefault(slot, []).append(what)

    def claim(slot, *uses):
        while any((u, (slot + k) % NU) in busy for u, k in uses):
            slot += 1
        busy.update((u, (slot + k) % NU) for u, k in uses)
        return slot

    def turn(slot, bank):
        return claim(slot, ("PE", 0), (bank, 0), (bank, 1), ("ACT" if bank == "a" else "DVE", 1))

    def norm(slot, j, t):
        slot = claim(slot, ("DVE", 0))
        put(slot, "norm", j, t)
        put(slot + 1, "norm2", j, t)
        slot = claim(slot + 2, ("ACT", 0))
        put(slot, "xn", j, t)
        return slot

    for layer, t in SEGMENTS:
        e = claim(END[layer, t] + LAG_PV, ("DVE", 0))
        assert e == END[layer, t] + LAG_PV
        put(e - 2, "rinv", layer, t)
        put(e, f"end{layer}", t)
    in_x = {}
    for t in (3, 0, 1, 2):
        slot = norm(END[0, t] + LAG_PV + 1, "f", t)
        slot = turn(slot + (1 if t == T - 1 else 2), "a")
        put(slot, "f_turn", t)
        slot = claim(slot + 1, ("PE", 0), ("PE", 1), ("d", 0), ("d", 1), ("d", 2), ("DVE", 2))
        put(slot, "f_mm", t, 0)
        put(slot + 1, "f_mm", t, 1)
        slot = claim(slot + 4, ("ACT", 0))
        put(slot, "f_out", t)
        in_x[t] = slot + 2
        if t == T - 1:
            hasty = norm(in_x[t], "q", (1, t)), claim(slot + 5, ("ACT", 0))
            put(hasty[1], "q_split", (1, t))
            for g in range(G):
                turned = hasty[1] + 2 + g // 2
                busy.update((u, turned) for u in ("PE", "a", "d"))
                busy.update((u, turned + 1) for u in ("ACT", "DVE", "a", "d"))
                put(turned, "q_turn", (1, t), g)
            assert turned < START[1, t]
            hasty += (turned,)
    normed = turned = 0
    for layer, t in ((0, 0), (0, 1), (0, 2), (1, 0), (1, 1), (1, 2), (1, 3), (0, 3)):
        if (layer, t) == (1, T - 1):
            assert normed + 2 < hasty[0] and turned < hasty[1], (normed, turned, hasty)
            normed, _, turned = hasty
            continue
        if layer:
            start, free, due = in_x[t], END[1, t - Q_TILES[1]] if t >= Q_TILES[1] else 0, START[1, t]
        else:
            free, due = END[0, t - 1] if t else 0, START[0, t + 1] if t + 1 < T else NU - 1
            start = max(1, due - 20)
        normed = norm(max(start, normed + 1), "q", (layer, t))
        slot = claim(max(normed + 1, turned + 1), ("ACT", 0))
        put(slot, "q_split", (layer, t))
        turned = max(slot + 2, free)
        for g in range(G):
            turned = turn(turned, "ad"[g % 2])
            put(turned, "q_turn", (layer, t), g)
        assert turned < due or turned == due == NU - 1, (layer, t, turned)
    for t in range(T):
        slot = norm(END[1, t] + LAG_PV + 1, "y", t)
        put(claim(slot + 1, ("DVE", 0)), "y_out", t)
    put(claim(12, ("DVE", 0)), "bias")
    slot = 7
    for kc in range(T):
        slot = claim(slot + 1, ("ACT", 0))
        put(slot, "kv_split", kc)
        slot += 3
        for g in range(G):
            slot = turn(slot, "ad"[g % 2])
            put(slot, "k_turn", kc, g)
    return at


AT = schedule()
JOBS = [w for s in sorted(AT) for w in AT[s]]
WRAP = max(AT) + 2 - NU
assert all(w[0] in ("rinv", "end1", "y_out") or w[1] == "y" for s, jobs in AT.items() if s >= NU for w in jobs)
_first = "q", (0, T - 1)
PROLOGUE = [("norm", *_first), ("norm2", *_first), ("xn", *_first), ("q_split", _first[1]), ("kv_split", 0)]
PROLOGUE += [("q_turn", _first[1], g) for g in range(G)] + [("k_turn", 0, g) for g in range(G)] + [("bias",)]
for _kc in range(1, T):
    PROLOGUE += [("kv_split", _kc)] + [("k_turn", _kc, g) for g in range(G)]


def number(want):
    return tuple({w: n for n, w in enumerate(w for w in jobs if want(w))} for jobs in (PROLOGUE, JOBS))


BANK_NO = {k: number(lambda w: bank_of(w) == k) for k in "ad"}
NORM_NO = {j: number(lambda w: w[:2] == ("norm", j)) for j in NORMS}
KV_NO = number(lambda w: w[0] == "kv_split")
BIAS_NO = number(lambda w: w[0] == "bias")


def emptying_at(slot):
    return [w for w in AT.get(slot - 1, []) if bank_of(w)]


def others_at(slot):
    return [w for w in AT.get(slot, []) if not bank_of(w) and w[0] not in ENDS]


ENDS = ("end0", "end1")


def ends_at(slot):
    return [w for w in AT.get(slot, []) if w[0] in ENDS]


class Place:

    def __init__(self, pair=None, par=0):
        self.pair, self.par = pair, par
        self.bi = None if pair is None else 2 * pair + par
        self.next_par = 0 if pair is None else 1 - par
        self.next_b = 0 if pair is None else (2 * pair + 1 if par == 0 else (2 * pair + 2) % B)

    def count(self, numbers, what, each=1, more=0):
        pre, per = numbers
        if self.bi is None:
            return OFF + each * pre[what] + more
        return self.bi * (each * len(per)) + each * (len(pre) + per[what]) + more + OFF

    def unit(self, u):
        return self.bi * NU + (u + 1 + OFF)

    def nth(self, per, k):
        return self.bi * per + (k + OFF)


def run_slots(eng, slot):
    def batch(now, after):
        for s in range(WRAP, NU):
            slot(s, now, None)
        for s in range(WRAP):
            slot(s, after, now)

    for s in range(WRAP):
        slot(s, Place(0, 0), None)
    with eng.Fori(0, B // 2 - 1) as pair:
        batch(Place(pair, 0), Place(pair, 1))
        batch(Place(pair, 1), Place(pair + 1, 0))
    pair = B // 2 - 1
    batch(Place(pair, 0), Place(pair, 1))
    batch(Place(pair, 1), None)


def units_at(s, now, before, lag=0):
    place, u = (now, s - lag) if s >= lag else (before, s - lag + NU)
    return [(place, u)] if place else []


def steps_at(s, now, before, jobs_at=lambda s: AT.get(s, [])):
    return [(before, w) for w in jobs_at(s + NU) if before] + [(now, w) for w in jobs_at(s) if now]


def tile_of_q0(place, t):
    return (place.par, t + 1) if t + 1 < T else (place.next_par, 0)


def fold_weights(nc, sb, sem, dram, banks, ident, w_ffn):
    w_in = [sb(f"w_in{k}", [P, C, D], F32) for k in range(4)]
    w_leftT = sb("w_leftT", [P, 2, C, P], F32)
    loaded = sem("w_loaded")
    turned = sem("w_turned")
    left_in = sem("w_left_in")
    done = sem("w_done")
    out_in = sem("w_out_in")

    def pe_program(pe):
        def transpose(n):
            left = w_in[1] if n < C else w_in[0]
            if n >= 2:
                pe.wait_ge(left_in, n - 1)
            for c in range(C):
                last = nc.tensor.transpose(banks[n % 2][:, P * c:P * c + P], left[:, n % C, P * c:P * c + P], ident[:, :])
            last.then_inc(turned, 1)

        pe.wait_ge(loaded, 16 * 4)
        transpose(0)
        for n in range(2 * C):
            if n + 1 < 2 * C:
                transpose(n + 1)
            right = w_in[2] if n < C else w_in[3]
            pe.wait_ge(left_in, n + 1)
            if n == C:
                pe.wait_ge(out_in, C)
            elif n >= 2:
                pe.wait_ge(out_in, n - 1)
            for c in range(C):
                last = nc.tensor.matmul(banks[2 + n % 2][:, :], w_leftT[:, n % 2, c, :], right[:, c, :],
                                        start=(c == 0), stop=(c == C - 1))
            last.then_inc(done, 1)

    def dve_program(dve):
        def put_left(n):
            dve.wait_ge(turned, n + 1)
            if n >= 2:
                dve.wait_ge(done, n - 1)
            nc.vector.tensor_copy(w_leftT[:, n % 2, :, :].rearrange("p c i -> p (c i)"), banks[n % 2][:, :]).then_inc(left_in, 1)

        put_left(0)
        for n in range(2 * C):
            if n + 1 < 2 * C:
                put_left(n + 1)
            out = w_in[3] if n < C else w_ffn
            dve.wait_ge(done, n + 1)
            nc.vector.tensor_copy(out[:, n % C, :], banks[2 + n % 2][:, :]).then_inc(out_in, 1)

    def sp_program(sp):
        sp.dma_start(ident[:, :], dram["ident"]).then_inc(loaded, 16)
        for k, name in ((1, "L0_ffn_aux_weight1"), (2, "L0_ffn_aux_weight2"), (0, "L0_ffn_weight")):
            sp.dma_start(w_in[k][:, :, :], dram[name].rearrange("(c p) d -> p c d", p=P)).then_inc(loaded, 16)

    def idle(_):
        pass

    return pe_program, idle, dve_program, idle, sp_program


def phase1(nc, sb, sem, held, dram, gates, banks, ident, w_ffn):
    iota = sb("iota", [P, S], F32)
    half = sb("half", [P, 1], F32)
    b0_row = sb("b0_row", [P, S], F32)
    b1_col = sb("b1_col", [P, 1], F32)
    ffn_bias = sb("ffn_bias", [P, D], F32)
    seq_i = sb("seq_i", [P, B], I32)
    seq_f = sb("seq_f", [P, B], F32)
    nbias = sb("nbias", [P, 2, 2, S], F32)
    x = sb("x", [P, 2, T, D], F32)
    kv = sb("kv", [P, 2 * D], F32)
    kT = sb("kT", [P, 2, H0, S], F32R)
    v = sb("v", [P, 2, T, 3, D], BF16)
    qT = [sb("q0T", [P, Q_TILES[0], H0, P], F32R), sb("q1T", [P, Q_TILES[1], H0, P], F32R)]
    parts = {j: sb("parts_" + j, [P, H0, 3, DH0], F32R) for j in ("q", "k")}
    xn = {j: sb("xn_" + j, [P, D], F32) for j in NORMS}
    stat = {j: sb("stat_" + j, [P, 6], F32) for j in NORMS}
    mv = {j: sb("mv_" + j, [P, 2], F32) for j in NORMS}
    rstd = {j: sb("rstd_" + j, [P, 4], F32) for j in NORMS}
    xnT = sb("xnT", [P, C, P], F32)
    f_out = sb("f_out", [P, D], F32)
    p = sb("p", [P, 3, S], F32)
    pT_hi = sb("pT_hi", [P, 3, S], F16)
    pT_lo = sb("pT_lo", [P, 2, S], F16)
    nmax = sb("nmax", [P, 4], F32)
    rsum = [sb("rsum0", [P, 2, H0], F32), sb("rsum1", [P, 2, H1], F32)]
    rinv = [sb("rinv0", [P, H0], F32), sb("rinv1", [P, H1], F32)]
    o_sb = sb("o_sb", [P, D], F32)
    ymax = sb("ymax", [P, T], F32)
    yall = dram["yall"]

    s_bank, pT_bank, o_bank, misc = banks[0:3], banks[3:5], banks[5], {"a": banks[6], "d": banks[7]}

    consts_in = sem("consts_in")
    gates_ready = sem("gates_ready")
    seq_ready = sem("seq_ready")
    x_in = [sem("x_in0"), sem("x_in1")]
    kv_in = sem("kv_in")
    kv_first = [sem(f"kv_first{kc}") for kc in range(T - 1)]
    mask_in = sem("mask_in")
    x_store, y_store = sem("x_store"), sem("y_store")
    bias_step = sem("bias_step")
    s_ready = sem("s_ready")
    max_ready = sem("max_ready")
    exp_done = sem("exp_done")
    pT_ready = sem("pT_ready")
    hi_done = sem("hi_done")
    lo_done = sem("lo_done")
    pv_done = sem("pv_done")
    filled = {"a": sem("a_filled"), "d": sem("d_filled")}
    freed = {"a": sem("a_freed"), "d": sem("d_freed")}
    stats = {j: sem("stats_" + j) for j in NORMS}
    rs_step = {j: sem("rs_step_" + j) for j in NORMS}
    normed = {j: sem("normed_" + j) for j in NORMS}
    hi_part = {j: sem("hi_part_" + j) for j in parts}
    lo_part = {j: sem("lo_part_" + j) for j in parts}
    v_step = sem("v_step")
    end_step = [sem("end_step0"), sem("end_step1")]
    x_step = [sem("x_step0"), sem("x_step1")]
    f_tanh = sem("f_tanh")
    f_step = sem("f_step")
    y_max = sem("y_max")

    def mask_row(par):
        return nbias[:, par, 1, :].bitcast(I32)

    N_CONSTS = 16 * 7

    def x_tile(place, j, t):
        if j == "q":
            layer, t = t
            par, t = (place.par, t) if layer else tile_of_q0(place, t)
        else:
            par = place.par
        return x[:, par, t, :]

    def emptied(what, place):
        if what[0] == "f_turn":
            return xnT[:, :, :].rearrange("p c i -> p (c i)"), misc["a"][:, :]
        kind, a, g = what
        bank = misc[bank_of(what)][0:ST, :].rearrange("p (k i) -> p k i", k=4)
        if kind == "k_turn":
            return kT[0:ST, place.next_par, 4 * g:4 * g + 4, P * a:P * a + P], bank
        layer, t = a
        t = t if layer else tile_of_q0(place, t)[1]
        return qT[layer][0:ST, t % Q_TILES[layer], 4 * g:4 * g + 4, :], bank

    def wait_turned(eng, place, j, what):
        jobs = PROLOGUE if place.bi is None else JOBS
        turns = [w for w in jobs if w[0] == j + "_turn"]
        before = [w for w in turns if jobs.index(w) < jobs.index(what)]
        if not before and place.bi is None:
            return
        for k in "ad":
            w = [w for w in (before or turns) if bank_of(w) == k][-1]
            n = place.count(BANK_NO[k], w, 1, 1)
            eng.wait_ge(filled[k], n if before else n - len(BANK_NO[k][1]))

    def pe_job(pe, place, what):
        kind, k = what[0], bank_of(what)
        if kind in ("q_turn", "k_turn"):
            j, g = kind[0], what[2]
            if g == 0:
                no, w = (KV_NO, ("kv_split", what[1])) if j == "k" else (NORM_NO[j], ("norm", j, what[1]))
                pe.wait_ge(hi_part[j], place.count(no, w, 1, 1))
                pe.wait_ge(lo_part[j], place.count(no, w, 1, 1))
            pe.wait_ge(freed[k], place.count(BANK_NO[k], what))
            for n in range(4):
                h = 4 * g + n
                src = parts[j][:, h, :, :].bitcast(F32).rearrange("p a d -> p (a d)")
                last = nc.tensor.transpose(misc[k][0:ST, P * n:P * n + P], src, ident[:, :])
            last.then_inc(filled[k], 1)
        elif kind == "f_turn":
            pe.wait_ge(normed["f"], place.count(NORM_NO["f"], ("norm", "f", what[1]), 1, 1))
            pe.wait_ge(freed["a"], place.count(BANK_NO["a"], what))
            for c in range(C):
                last = nc.tensor.transpose(misc["a"][:, P * c:P * c + P], xn["f"][:, P * c:P * c + P], ident[:, :])
            last.then_inc(filled["a"], 1)
        elif kind == "f_mm":
            if what[2] == 0:
                pe.wait_ge(freed["a"], place.count(BANK_NO["a"], ("f_turn", what[1]), 1, 1))
                pe.wait_ge(freed["d"], place.count(BANK_NO["d"], ("f_mm", what[1], 1)))
            for c in range(2 * what[2], 2 * what[2] + 2):
                last = nc.tensor.matmul(misc["d"][:, :], xnT[:, c, :], w_ffn[:, c, :], start=(c == 0), stop=(c == C - 1))
            if what[2] == 1:
                last.then_inc(filled["d"], 1)

    def pe_scores(pe, place, u):
        _, layer, t, h = UNITS[u]
        if h == 0:
            job = t if layer else t - 1
            for k, g in (("a", G - 2), ("d", G - 1)):
                if job >= 0:
                    pe.wait_ge(freed[k], place.count(BANK_NO[k], ("q_turn", (layer, job), g), 1, 1))
                else:
                    pe.wait_ge(freed[k], place.bi * len(BANK_NO[k][1]) + (len(BANK_NO[k][0]) + OFF))
        pe.wait_ge(exp_done, place.unit(u - 3))
        stacks = [2 * h, 2 * h + 1] if layer else [h]
        for n, k in enumerate(stacks):
            last = nc.tensor.matmul(s_bank[u % 3][:, :], qT[layer][0:ST, t % Q_TILES[layer], k, :],
                                    kT[0:ST, place.par, k, :], start=(n == 0), stop=(n == len(stacks) - 1))
        last.then_inc(s_ready, 1)

    def pe_turn(pe, place, u):
        pe.wait_ge(exp_done, place.unit(u))
        pe.wait_ge(lo_done, place.unit(u - 2))
        for c in range(T):
            last = nc.tensor.transpose(pT_bank[u % 2][:, P * c:P * c + P], p[:, u % 3, P * c:P * c + P], ident[:, :])
        last.then_inc(pT_ready, 1)

    def pe_values(pe, place, u):
        k, layer, t, h = UNITS[u]
        dh = DH1 if layer else DH0
        if h == 0:
            was = SEGMENTS[k - 1]
            pe.wait_ge(end_step[was[0]], place.nth(3 * T, 3 * was[1] + 3 - (3 * T if k == 0 else 0)))
        if u == 0:
            pe.wait_ge(v_step, place.bi * (4 * T) + (4 * T + OFF))
        pe.wait_ge(lo_done, place.unit(u))
        terms = [(c, part, n) for c in range(T) for part, n in ((0, 0), (0, 1), (0, 2), (1, 0), (1, 1))]
        for i, (c, part, n) in enumerate(terms):
            pT = pT_lo[:, u % 2, :] if part else pT_hi[:, u % 3, :]
            last = nc.tensor.matmul(o_bank[:, dh * h:dh * h + dh], pT[:, P * c:P * c + P],
                                    v[:, place.par, c, n, dh * h:dh * h + dh], start=(i == 0), stop=(i == len(terms) - 1))
        last.then_inc(pv_done, 1)

    def pe_program(pe):
        for s in (s_ready, pT_ready, pv_done, *filled.values()):
            pe.sem_inc(s, OFF)
        pe.wait_ge(consts_in, N_CONSTS)
        for what in PROLOGUE:
            pe_job(pe, Place(), what)

        def slot(s, now, before):
            for place, u in units_at(s, now, before):
                pe_scores(pe, place, u)
            for place, u in units_at(s, now, before, LAG_T):
                pe_turn(pe, place, u)
            for place, u in units_at(s, now, before, LAG_PV):
                pe_values(pe, place, u)
            for place, what in steps_at(s, now, before):
                pe_job(pe, place, what)

        run_slots(pe, slot)

    def act_job(act, place, what):
        kind = what[0]
        if kind == "q_split":
            act.wait_ge(normed["q"], place.count(NORM_NO["q"], ("norm", "q", what[1]), 1, 1))
            wait_turned(act, place, "q", what)
            split_high("q", xn["q"][:, :])
        elif kind == "xn":
            j, t = what[1:]
            n, what = NORM_NO[j], ("norm", j, t)
            if j in parts:
                act.wait_ge(lo_part[j], place.count(n, what))
            elif j == "f":
                act.wait_ge(filled["a"], place.count(BANK_NO["a"], ("f_turn", (t - 1) % T), 1, 1 - (len(BANK_NO["a"][1]) if t == 0 else 0)))
            else:
                act.wait_ge(y_max, place.count(n, what))
                act.wait_ge(y_store, place.bi * (16 * T) + 16 * (t + 1))
            act.wait_ge(rs_step[j], place.count(n, what, 4, 4))
            nc.scalar.activation(xn[j][:, :], x_tile(place, j, t), ACT.Identity, bias=rstd[j][:, 3:4],
                                 scale=rstd[j][:, 2:3]).then_inc(normed[j], 1)
        elif kind == "kv_split":
            kc = what[1]
            act.wait_ge(*kv_loaded(place, kc))
            wait_turned(act, place, "k", what)
            split_high("k", kv_buffer(place, kc)[:, 0:D])
        elif bank_of(what) == "a":
            act.wait_ge(filled["a"], place.count(BANK_NO["a"], what, 1, 1))
            if kind == "f_turn":
                act.wait_ge(filled["d"], place.count(BANK_NO["d"], ("f_mm", what[1], 1)))
            out, bank = emptied(what, place)
            nc.scalar.activation(out, bank, ACT.Copy).then_inc(freed["a"], 1)
        elif kind == "f_out":
            act.wait_ge(freed["d"], place.count(BANK_NO["d"], ("f_mm", what[1], 1), 1, 1))
            nc.scalar.activation(f_out[:, :], f_out[:, :], ACT.Tanh).then_inc(f_tanh, 1)

    def high_and_low(j):
        if j == "k":
            return parts[j][:, :, 0:2, :], parts[j][:, :, 2, :]
        return parts[j][:, :, 0:3:2, :], parts[j][:, :, 1, :]

    def split_high(j, src):
        src = src.rearrange("p (h d) -> p h d", h=H0).unsqueeze(2).broadcast_to([P, H0, 2, DH0])
        nc.scalar.activation(high_and_low(j)[0], src, ACT.Copy).then_inc(hi_part[j], 1)

    def kv_loaded(place, kc):
        if place.bi is None:
            return (kv_first[kc], 16) if kc < T - 1 else (kv_in, 16)
        return kv_in, place.bi * (16 * T) + 16 * (kc + 2)

    def kv_buffer(place, kc):
        if place.bi is None and 0 < kc < T - 1:
            return x[:, 1, 2 * kc - 2:2 * kc, :].rearrange("p t d -> p (t d)")
        return kv[:, :]

    def act_exp(act, place, u):
        _, layer, t, h = UNITS[u]
        act.wait_ge(max_ready, place.unit(u))
        act.wait_ge(pT_ready, place.unit(u - 3))
        if h == 0:
            act.wait_ge(end_step[layer], place.nth(3 * T, 3 * t - 3))
        nc.scalar.activation(p[:, u % 3, :], s_bank[u % 3][:, :], ACT.Exp, bias=nmax[:, u % 4:u % 4 + 1], scale=-1.0,
                             accum_out=rsum[layer][:, t % 2, h:h + 1]).then_inc(exp_done, 1)

    def act_hi(act, place, u):
        act.wait_ge(pT_ready, place.unit(u))
        act.wait_ge(pv_done, place.unit(u - 3))
        nc.scalar.activation(pT_hi[:, u % 3, :], pT_bank[u % 2][:, :], ACT.Copy).then_inc(hi_done, 1)

    def act_program(act):
        for s in (exp_done, hi_done, freed["a"], *hi_part.values(), *normed.values(), f_tanh):
            act.sem_inc(s, OFF)
        act.wait_ge(consts_in, N_CONSTS)
        nc.scalar.activation(gates[:, :], gates[:, :], ACT.Tanh).then_inc(gates_ready, 1)
        for what in PROLOGUE:
            act_job(act, Place(), what)

        def slot(s, now, before):
            for place, what in steps_at(s, now, before, emptying_at):
                act_job(act, place, what)
            for place, u in units_at(s, now, before, LAG_MAX):
                act_exp(act, place, u)
            for place, u in units_at(s, now, before, LAG_T):
                act_hi(act, place, u)
            for place, what in steps_at(s, now, before, others_at):
                act_job(act, place, what)

        run_slots(act, slot)

    def dve_max(dve, place, u):
        _, layer, t, h = UNITS[u]
        dve.wait_ge(s_ready, place.unit(u))
        dve.wait_ge(exp_done, place.unit(u - 4))
        dve.sem_inc(held.dve, 1)
        out = s_bank[u % 3][:, :]
        nc.vector.tensor_tensor_reduce(out, out, nbias[:, place.par, layer, :], 1.0, BIG, ALU.add, ALU.min,
                                       nmax[:, u % 4:u % 4 + 1]).then_inc(max_ready, 1)

    def dve_lo(dve, place, u):
        dve.wait_ge(hi_done, place.unit(u))
        dve.wait_ge(pv_done, place.unit(u - 2))
        nc.vector.tensor_tensor(pT_lo[:, u % 2, :], pT_bank[u % 2][:, :], pT_hi[:, u % 3, :],
                                ALU.subtract).then_inc(lo_done, 1)

    def dve_job(dve, place, what):
        kind = what[0]
        if kind == "norm":
            j, t = what[1:]
            if j == "q" and t == (0, T - 1):
                par = place.next_par
                if place.bi is None:
                    dve.wait_ge(x_in[0], 16)
                else:
                    dve.wait_ge(x_in[par], place.pair * 16 + (16 if par else 32))
            elif j == "f":
                dve.wait_ge(x_step[0], place.nth(T, t + 1))
            elif j == "q" and t[0] == 1:
                dve.wait_ge(f_step, place.nth(2 * T, 2 * t[1] + 2))
            elif j == "y":
                dve.wait_ge(x_step[1], place.nth(T, t + 1))
            dve.wait_ge(normed[j], place.count(NORM_NO[j], what))
            nc.vector.bn_stats(stat[j][:, :], x_tile(place, j, t)).then_inc(stats[j], 1)
        elif kind == "norm2":
            j, t = what[1:]
            dve.wait_ge(stats[j], place.count(NORM_NO[j], ("norm", j, t), 2, 1))
            dve.sem_inc(held.dve, 1)
            nc.vector.bn_aggr(mv[j][:, :], stat[j][:, :]).then_inc(stats[j], 1)
        elif bank_of(what) == "d" and kind != "f_mm":
            dve.wait_ge(filled["d"], place.count(BANK_NO["d"], what, 1, 1))
            out, bank = emptied(what, place)
            nc.vector.tensor_copy(out, bank).then_inc(freed["d"], 1)
        elif kind == "rinv":
            layer, t = what[1:]
            dve.wait_ge(exp_done, place.unit(END[layer, t] - 1))
            nc.vector.reciprocal(rinv[layer][:, :], rsum[layer][:, t % 2, :]).then_inc(end_step[layer], 1)
            dve.wait_ge(end_step[layer], place.nth(3 * T, 3 * t + 1))
            nc.vector.tensor_scalar(rinv[layer][:, :], rinv[layer][:, :], gates[:, layer:layer + 1], None,
                                    ALU.mult).then_inc(end_step[layer], 1)
        elif kind in ENDS:
            layer, t = int(kind[3]), what[1]
            dh, heads = (DH1, H1) if layer else (DH0, H0)
            dve.wait_ge(end_step[layer], place.nth(3 * T, 3 * t + 2))
            dve.wait_ge(x_step[layer], place.nth(T, t))
            if t == 0:
                dve.sem_inc(held.dve, 1)
                dve.wait_ge(x_step[1 - layer], place.nth(T, T if layer else 0))
            dve.wait_ge(pv_done, place.unit(END[layer, t] - 1))
            nc.vector.tensor_tensor(o_sb[:, :].rearrange("p (h d) -> p h d", h=heads),
                                    o_bank[:, :].rearrange("p (h d) -> p h d", h=heads),
                                    rinv[layer][:, :].unsqueeze(2).broadcast_to([P, heads, dh]),
                                    ALU.mult).then_inc(end_step[layer], 1)
        elif kind == "f_mm" and what[2] == 1:
            dve.wait_ge(filled["d"], place.count(BANK_NO["d"], what, 1, 1))
            dve.wait_ge(f_step, place.nth(2 * T, 2 * what[1]))
            nc.vector.tensor_tensor(f_out[:, :], misc["d"][:, :], ffn_bias[:, :], ALU.add).then_inc(freed["d"], 1)
        elif kind == "y_out":
            t = what[1]
            dve.wait_ge(normed["y"], place.count(NORM_NO["y"], ("norm", "y", t), 1, 1))
            nc.vector.tensor_reduce(yall[:, bass.ds(place.bi * T + t, 1)], xn["y"][:, :], AX.X, ALU.max,
                                    apply_absolute_value=True).then_inc(y_max, 1)
        elif kind == "bias":
            par = place.next_par
            col = seq_f[:, 0:1] if place.bi is None else seq_f[:, bass.ds(place.next_b, 1)]
            dve.wait_ge(mask_in, 16 if place.bi is None else place.bi * 16 + 32)
            nc.vector.tensor_scalar(nbias[:, par, 0, :], iota[:, :], col, MASK0, ALU.is_ge, ALU.mult).then_inc(bias_step, 1)
            nc.vector.tensor_scalar(nbias[:, par, 1, :], mask_row(par), -MASK1, MASK1, ALU.mult, ALU.add).then_inc(bias_step, 1)
            dve.wait_ge(bias_step, place.count(BIAS_NO, what, 4, 2))
            nc.vector.tensor_tensor(nbias[:, par, 0, :], nbias[:, par, 0, :], b0_row[:, :], ALU.subtract).then_inc(bias_step, 1)
            nc.vector.tensor_scalar(nbias[:, par, 1, :], nbias[:, par, 1, :], b1_col[:, 0:1], None,
                                    ALU.subtract).then_inc(bias_step, 1)
            dve.wait_ge(bias_step, place.count(BIAS_NO, what, 4, 4))

    def dve_program(dve):
        for s in (max_ready, lo_done, freed["d"], *stats.values(), y_max, bias_step):
            dve.sem_inc(s, OFF)
        for s in end_step:
            dve.sem_inc(s, OFF)
        dve.wait_ge(consts_in, N_CONSTS)
        nc.vector.tensor_copy(seq_f[:, :], seq_i[:, :]).then_inc(seq_ready, 1)
        nc.vector.memset(half[:, :], -0.5).then_inc(seq_ready, 1)
        dve.wait_ge(seq_ready, 2)
        dve.wait_ge(gates_ready, 1)
        for what in PROLOGUE:
            dve_job(dve, Place(), what)

        def slot(s, now, before):
            for place, what in steps_at(s, now, before, ends_at):
                dve_job(dve, place, what)
            for place, u in units_at(s, now, before, LAG_MAX):
                dve_max(dve, place, u)
            for place, what in steps_at(s, now, before, emptying_at):
                dve_job(dve, place, what)
            for place, u in units_at(s, now, before, LAG_LO):
                dve_lo(dve, place, u)
            for place, what in steps_at(s, now, before, others_at):
                dve_job(dve, place, what)

        run_slots(dve, slot)

    def split_low(pool, place, j, numbers, what, src):
        pool.wait_ge(hi_part[j], place.count(numbers, what, 1, 1))
        high, low = high_and_low(j)
        nc.gpsimd.tensor_tensor(low, src.rearrange("p (h d) -> p h d", h=H0), high[:, :, 0, :].bitcast(F32),
                                ALU.subtract).then_inc(lo_part[j], 1)

    def pool_job(pool, place, what):
        kind = what[0]
        if kind == "norm2":
            j, t = what[1:]
            n, what = NORM_NO[j], ("norm", j, t)
            pool.wait_ge(stats[j], place.count(n, what, 2, 2))
            pool.wait_ge(normed[j], place.count(n, what))
            pool.sem_inc(held.pool, 1)
            nc.gpsimd.tensor_scalar(rstd[j][:, 0:1], mv[j][:, 1:2], EPS, None, ALU.add).then_inc(rs_step[j], 1)
            pool.wait_ge(rs_step[j], place.count(n, what, 4, 1))
            nc.gpsimd.tensor_tensor(rstd[j][:, 1:2], rstd[j][:, 0:1], half[:, :], ALU.pow).then_inc(rs_step[j], 1)
            pool.wait_ge(rs_step[j], place.count(n, what, 4, 2))
            pool.sem_inc(held.pool, 1)
            nc.gpsimd.tensor_scalar(rstd[j][:, 2:3], rstd[j][:, 1:2], Q_SCALE[t[0]] if j == "q" else 1.0, None,
                                    ALU.mult).then_inc(rs_step[j], 1)
            pool.wait_ge(rs_step[j], place.count(n, what, 4, 3))
            pool.sem_inc(held.pool, 1)
            nc.gpsimd.tensor_scalar(rstd[j][:, 3:4], mv[j][:, 0:1], rstd[j][:, 2:3], -1.0, ALU.mult,
                                    ALU.mult).then_inc(rs_step[j], 1)
        elif kind == "q_split":
            split_low(pool, place, "q", NORM_NO["q"], ("norm", "q", what[1]), xn["q"][:, :])
        elif kind == "kv_split":
            kc = what[1]
            pool.wait_ge(*kv_loaded(place, kc))
            split_low(pool, place, "k", KV_NO, what, kv_buffer(place, kc)[:, 0:D])
            vals, out = kv_buffer(place, kc)[:, D:2 * D], v[:, place.next_par, kc]
            if place.bi is not None:
                pool.wait_ge(pv_done, place.unit(-1))
            pool.sem_inc(held.pool, 1)
            nc.gpsimd.tensor_scalar(out[:, 0, :], vals, 1.0, 1.0, ALU.mult, ALU.mult).then_inc(v_step, 1)
            pool.wait_ge(v_step, place.count(KV_NO, what, 4, 1))
            nc.gpsimd.tensor_tensor(vals, vals, out[:, 0, :], ALU.subtract).then_inc(v_step, 1)
            pool.wait_ge(v_step, place.count(KV_NO, what, 4, 2))
            pool.sem_inc(held.pool, 1)
            nc.gpsimd.tensor_scalar(out[:, 1, :], vals, 1.0, 1.0, ALU.mult, ALU.mult).then_inc(v_step, 1)
            pool.wait_ge(v_step, place.count(KV_NO, what, 4, 3))
            nc.gpsimd.tensor_tensor(out[:, 2, :], vals, out[:, 1, :], ALU.subtract).then_inc(v_step, 1)
            pool.wait_ge(v_step, place.count(KV_NO, what, 4, 4))
        elif kind in ("end0", "end1"):
            layer, t = int(kind[3]), what[1]
            xt = x[:, place.par, t, :]
            pool.wait_ge(end_step[layer], place.nth(3 * T, 3 * t + 3))
            nc.gpsimd.tensor_tensor(xt, xt, o_sb[:, :], ALU.add).then_inc(x_step[layer], 1)
        elif kind == "f_out":
            t = what[1]
            xt = x[:, place.par, t, :]
            pool.wait_ge(f_tanh, place.nth(T, t + 1))
            pool.sem_inc(held.pool, 1)
            nc.gpsimd.tensor_scalar(f_out[:, :], f_out[:, :], gates[:, 2:3], 1.0, ALU.mult, ALU.mult).then_inc(f_step, 1)
            pool.wait_ge(f_step, place.nth(2 * T, 2 * t + 1))
            nc.gpsimd.tensor_tensor(xt, xt, f_out[:, :], ALU.add).then_inc(f_step, 1)

    def pool_program(pool):
        for s in (*rs_step.values(), *lo_part.values(), v_step, *x_step, f_step):
            pool.sem_inc(s, OFF)
        pool.wait_ge(seq_ready, 2)
        pool.wait_ge(gates_ready, 1)
        for what in PROLOGUE:
            pool_job(pool, Place(), what)

        def slot(s, now, before):
            for place, what in steps_at(s, now, before):
                pool_job(pool, place, what)

        run_slots(pool, slot)

    def rows(ap, b):
        return ap[b].rearrange("(t p) d -> p t d", p=P)

    def spread(ap, n):
        return ap.partition_broadcast(P)

    def sp_program(sp):
        sp.sem_inc(x_store, 16)
        sp.sem_inc(y_store, 16)
        for kc in range(T - 1):
            load_kv(sp, 0, kc, Place())
        sp.dma_start(iota[:, :], dram["iota"].partition_broadcast(P)).then_inc(consts_in, 16)
        sp.dma_start(b0_row[:, :], dram["L0_xattn_b"].partition_broadcast(P)).then_inc(consts_in, 16)
        sp.dma_start(b1_col[:, :], dram["L1_xattn_b"].partition_broadcast(P)).then_inc(consts_in, 16)
        sp.dma_start(ffn_bias[:, :], dram["L0_ffn_bias"].partition_broadcast(P)).then_inc(consts_in, 16)
        sp.dma_start(seq_i[:, :], dram["itok_Bx1_68_817"].rearrange("b o -> (b o)").partition_broadcast(P)).then_inc(consts_in, 16)
        sp.dma_start(gates[:, 0:2], dram["g_xattn"].partition_broadcast(P)).then_inc(consts_in, 16)
        sp.dma_start(gates[:, 2:4], dram["g_ffn"].partition_broadcast(P)).then_inc(consts_in, 16)
        sp.dma_start(x[:, 0, :, :], rows(dram["x"], 0)).then_inc(x_in[0], 16)
        sp.dma_start(mask_row(0), dram["mask_BxS2_ik0"][0].partition_broadcast(P)).then_inc(mask_in, 16)
        wait_split(sp, Place(), 0)
        load_kv(sp, 0, T - 1)
        load_kv_after(sp, Place(), T - 1)
        with sp.Fori(0, B // 2) as pair:
            for par in (0, 1):
                place = Place(pair, par)
                sp.wait_ge(x_store, place.bi * (16 * T) + 16)
                sp.wait_ge(x_step[1], place.nth(T, 0))
                sp.dma_start(x[:, 1 - par, :, :], rows(dram["x"], place.next_b)).then_inc(x_in[1 - par], 16)
                sp.wait_ge(max_ready, place.unit(-1))
                sp.dma_start(mask_row(1 - par), dram["mask_BxS2_ik0"][place.next_b].partition_broadcast(P)).then_inc(mask_in, 16)
                for what in JOBS:
                    if what[0] == "kv_split":
                        load_kv_after(sp, place, what[1])
                    elif what[0] == "y_out":
                        t = what[1]
                        sp.wait_ge(x_step[1], place.nth(T, t + 1))
                        sp.dma_start(dram["x_mid"][place.bi * T + t], x[:, par, t, :]).then_inc(x_store, 16)
                        sp.wait_ge(normed["y"], place.count(NORM_NO["y"], ("norm", "y", t), 1, 1))
                        sp.dma_start(dram["y_mid"][place.bi * T + t], xn["y"][:, :]).then_inc(y_store, 16)
        sp.wait_ge(x_store, 16 * (B * T + 1))
        sp.wait_ge(y_store, 16 * (B * T + 1))
        sp.wait_ge(kv_in, 16 * (T * B + 2))

    def load_kv(sp, b, kc, place=None):
        out, loaded = (kv[:, :], kv_in) if place is None else (kv_buffer(place, kc), kv_first[kc])
        sp.dma_start(out, dram["ctx_2048"][b, P * kc:P * kc + P, :]).then_inc(loaded, 16)

    def wait_split(sp, place, kc):
        what = ("kv_split", kc)
        sp.wait_ge(hi_part["k"], place.count(KV_NO, what, 1, 1))
        sp.sem_inc(held.sp, 1)
        sp.wait_ge(lo_part["k"], place.count(KV_NO, what, 1, 1))
        sp.sem_inc(held.sp, 1)
        sp.wait_ge(v_step, place.count(KV_NO, what, 4, 4))

    def load_kv_after(sp, place, kc):
        wait_split(sp, place, kc)
        after_next = 1 if place.bi is None else (2 * place.pair + (2 + place.par)) % B
        load_kv(sp, *((place.next_b, kc + 1) if kc + 1 < T else (after_next, 0)))

    return pe_program, act_program, dve_program, pool_program, sp_program


I = 1536
N_BLK = B * S // 512
IT = I // P
PAIRS = IT // 2
GROUPS = IT // 4
QMAX = 32767.0
WMAX = 7.0
WBLK = 32
SIG = 65536.0
ROUND = 1.5 * 2 ** 23
TINY = 1e-12
SCALARS = ("x_scale", "x_inv", "gate_scale", "gate_c", "g2_unit", "g2_scale", "g2_c", "up_scale", "up_c",
           "o_unit", "o_scale", "o_c", "out_factor")


class Turns:

    def __init__(self, nc, sb, sem, held, name, banks, ident):
        self.nc, self.held, self.banks, self.ident = nc, held, banks, ident
        slots = len(banks)
        self.freed = OFF + 1 - slots
        self.raw = sb(name + "_raw", [P, slots, D], F32)
        self.src = sb(name + "_src", [P, slots, D], F32)
        self.size = sb(name + "_size", [P, slots, D // WBLK], F32)
        self.scale = sb(name + "_scale", [P, slots, D // WBLK], F32)
        self.inv = sb(name + "_inv", [P, slots, D // WBLK], F32)
        self.loaded = [sem(f"{name}_loaded{k}") for k in range(slots)]
        self.w_step = sem(name + "_w_step")
        self.quantised = sem(name + "_quantised")
        self.restored = sem(name + "_restored")
        self.turned = sem(name + "_turned")
        self.high = sem(name + "_high")
        self.low = sem(name + "_low")

    def load(self, sp, n, k, source):
        sp.wait_ge(self.restored, n + self.freed)
        sp.dma_start(self.raw[:, k, :], source).then_inc(self.loaded[k], 16)

    def quantise_x(self, dve, n, half_n, k, x_inv):
        dve.wait_ge(self.loaded[k], 16 * half_n + 16)
        self.nc.vector.tensor_scalar(self.raw[:, k, :], self.raw[:, k, :], x_inv[:, 0:1], ROUND,
                                     ALU.mult, ALU.add).then_inc(self.quantised, 1)

    def quantise_w(self, dve, n, half_n, n4, k):
        size, scale, inv = self.size[:, k, :], self.scale[:, k, :], self.inv[:, k, :]
        dve.wait_ge(self.loaded[k], 16 * half_n + 16)
        self.nc.vector.tensor_reduce(size, self.raw[:, k, :].rearrange("p (b w) -> p b w", w=WBLK), AX.X, ALU.max,
                                     apply_absolute_value=True).then_inc(self.w_step, 1)
        dve.wait_ge(self.restored, n + self.freed)
        dve.wait_ge(self.w_step, n4 + 1 + OFF)
        self.nc.vector.tensor_scalar(scale, size, 1.0 / WMAX, TINY, ALU.mult, ALU.max).then_inc(self.w_step, 1)
        dve.wait_ge(self.w_step, n4 + 2 + OFF)
        self.nc.vector.reciprocal(inv, scale).then_inc(self.w_step, 1)
        dve.wait_ge(self.w_step, n4 + 3 + OFF)
        blocks = self.raw[:, k, :].rearrange("p (b w) -> p b w", w=WBLK)
        self.nc.vector.tensor_tensor(blocks, blocks, inv.unsqueeze(2).broadcast_to([P, D // WBLK, WBLK]),
                                     ALU.mult).then_inc(self.w_step, 1)
        dve.wait_ge(self.w_step, n4 + 4 + OFF)
        self.nc.vector.tensor_scalar(self.raw[:, k, :], self.raw[:, k, :], ROUND, -ROUND, ALU.add,
                                     ALU.add).then_inc(self.quantised, 1)

    def restore_x(self, pool, n, k):
        pool.wait_ge(self.quantised, n + 1 + OFF)
        pool.wait_ge(self.turned, n + self.freed)
        pool.sem_inc(self.held.pool, 1)
        self.nc.gpsimd.tensor_scalar(self.src[:, k, :], self.raw[:, k, :], -ROUND, 1.0, ALU.add,
                                     ALU.mult).then_inc(self.restored, 1)

    def restore_w(self, pool, n, k):
        pool.wait_ge(self.quantised, n + 1 + OFF)
        pool.wait_ge(self.turned, n + self.freed)
        self.nc.gpsimd.tensor_tensor(self.src[:, k, :].rearrange("p (b w) -> p b w", w=WBLK),
                                     self.raw[:, k, :].rearrange("p (b w) -> p b w", w=WBLK),
                                     self.scale[:, k, :].unsqueeze(2).broadcast_to([P, D // WBLK, WBLK]),
                                     ALU.mult).then_inc(self.restored, 1)

    def transpose(self, pe, n, k):
        pe.wait_ge(self.restored, n + 1 + OFF)
        pe.wait_ge(self.low, n + self.freed)
        for c in range(4):
            last = self.nc.tensor.transpose(self.banks[k][:, P * c:P * c + P], self.src[:, k, P * c:P * c + P],
                                            self.ident[:, :])
        last.then_inc(self.turned, 1)

    def put_high(self, act, n, k, out):
        act.wait_ge(self.turned, n + 1 + OFF)
        act.sem_inc(self.held.act, 1)
        self.nc.scalar.activation(out, self.banks[k][:, :].rearrange("p (c i) -> p c i", i=P),
                                  ACT.Copy).then_inc(self.high, 1)

    def put_low(self, dve, n, k, out, high):
        dve.wait_ge(self.high, n + 1 + OFF)
        self.nc.vector.tensor_tensor(out, self.banks[k][:, :].rearrange("p (c i) -> p c i", i=P),
                                     high.bitcast(F32), ALU.subtract).then_inc(self.low, 1)

    def start(self, engines):
        for eng, s in (("dve", self.quantised), ("dve", self.w_step), ("dve", self.low), ("pool", self.restored),
                       ("pe", self.turned), ("act", self.high)):
            if eng in engines:
                engines[eng].sem_inc(s, OFF)


class Scales:

    def __init__(self, nc, sem, name):
        self.nc, self.step, self.n = nc, sem(name), 0

    def then(self, dve, inst):
        inst.then_inc(self.step, 1)
        self.n += 1
        dve.wait_ge(self.step, self.n)

    def mult(self, dve, out, a, b):
        self.then(dve, self.nc.vector.tensor_scalar(out[:, 0:1], a[:, 0:1], b if isinstance(b, float) else b[:, 0:1],
                                                    None, ALU.mult))

    def scale(self, dve, scale, size, unit, c):
        self.mult(dve, c, size, unit)
        self.then(dve, self.nc.vector.tensor_scalar(scale[:, 0:1], c[:, 0:1], 1.0 / QMAX, TINY, ALU.mult, ALU.max))
        self.then(dve, self.nc.vector.reciprocal(c[:, 0:1], scale[:, 0:1]))
        self.mult(dve, c, c, unit)


def quantised_products(nc, sb, sem, held, dram, banks, ident, sc, w_hl, name, acc_name, gate_q, first_w, next_w):
    up = gate_q is not None
    turns = Turns(nc, sb, sem, held, name, [banks[6], banks[7]], ident)
    acc = [(banks[2 * k], banks[2 * k + 1]) for k in range(3)]
    x_hl = sb(name + "_x_hl", [P, 2, 2, C, 512], F32R)
    out = sb(name + "_out", [P, 2, 2, 512], F32)
    cols = sb(name + "_cols", [P, N_BLK * PAIRS], F32)
    tops = sb(name + "_tops", [P, 4], F32)
    acc_ready, acc_out, acc_max = sem(name + "_acc_ready"), sem(name + "_acc_out"), sem(name + "_acc_max")
    stored = [sem(name + "_stored0"), sem(name + "_stored1")]
    col_top, top = sem(name + "_col_top"), sem(name + "_top")
    scales = Scales(nc, sem, name + "_scales")
    n_first = IT if first_w else 0
    per_block = 6 if next_w else 4
    if up:
        work = sb(name + "_work", [P, 3, 1024], F32)
        cols2 = sb(name + "_cols2", [P, N_BLK * PAIRS], F32)
        gate_in = [sem(f"{name}_gate_in{k}") for k in range(3)]
        gate_done, sigmoid_done = sem(name + "_gate_done"), sem(name + "_sigmoid_done")
        sig_done = sem(name + "_sig_done")
        g2_done, g2_max = sem(name + "_g2_done"), sem(name + "_g2_max")

    class Item:

        def __init__(self, blk, par, s, idx):
            before = n_first + 4 + per_block * par + idx
            self.n, self.half_n = two_n(per_block, blk, par, before)
            self.slot, self.par = before % 2, par
            self.kind, self.j = ("w", s // 5) if s in (0, 5) else ("x", s - 1)
            self.blk = blk

    def two_n(per, two, par, before):
        return two * (2 * per) + before, two * per + before // 2

    def items_of(two, par):
        steps = range(0, 6) if next_w else range(1, 5)
        return {s: Item(two, par, s, idx) for idx, s in enumerate(steps)}

    def w_item_tile(item):
        return (4 * item.blk + (2 * item.par + item.j)) % IT

    def w_dst(w, part, i):
        return w[:, part, :, bass.ds(i * P, P)]

    def x_dst(par, part, j):
        return x_hl[:, par, part, :, P * j:P * j + P]

    def item_dst(item, part):
        return w_dst(next_w[1], part, w_item_tile(item)) if item.kind == "w" else x_dst(1 - item.par, part, item.j)

    def load_item(sp, item):
        if item.kind == "w":
            source = next_w[0][bass.ds(w_item_tile(item) * P, P), :]
        else:
            source = dram["y_mid"][((2 * item.blk + item.par + 1) % N_BLK) * 4 + item.j]
        turns.load(sp, item.n, item.slot, source)

    def every_step(eng, step, lag=0):
        def blocks(two, at):
            for par in (0, 1):
                for s in range(PAIRS):
                    step(two, par, s, at(12 * two + 6 * par + s))

        blocks(0, lambda u: lambda k: u - k if u >= k else None)
        with eng.Fori(1, N_BLK // 2) as two:
            blocks(two, lambda u: lambda k: u - k)
        for s in range(lag):
            u = N_BLK * PAIRS + s
            step(N_BLK // 2, 0, s, lambda k, u=u: u - k if k and u - k < N_BLK * PAIRS else None)

    def first_x():
        return [(n_first + j, (n_first + j) // 2, j % 2, j) for j in range(4)]

    def sp_program(sp):
        if first_w:
            with sp.Fori(0, 3) as r:
                for k in range(4):
                    turns.load(sp, 4 * r + k, k % 2, first_w[0][bass.ds((4 * r + k) * P, P), :])
        for n, half_n, k, j in first_x():
            turns.load(sp, n, k, dram["y_mid"][j])
        for s in stored:
            sp.sem_inc(s, 16)

        def step(two, par, s, at):
            u, items = at(0), items_of(two, par)
            if s == 0 and next_w:
                load_item(sp, items[0])
            if s + 1 in items:
                load_item(sp, items[s + 1])
            if up:
                sp.wait_ge(g2_max, u - 2 + OFF)
                sp.dma_start(work[:, s % 3, :], dram["gate"][u]).then_inc(gate_in[s % 3], 16)
            sp.wait_ge(acc_out, u + 1 + OFF)
            sp.dma_start(dram[acc_name][u], out[:, s % 2, :, :].rearrange("p a i -> p (a i)")).then_inc(stored[s % 2], 16)

        every_step(sp, step)
        for s in stored:
            sp.wait_ge(s, 16 * (N_BLK * PAIRS // 2 + 1))

    def pe_program(pe):
        turns.start({"pe": pe})
        pe.sem_inc(acc_ready, OFF)
        if first_w:
            with pe.Fori(0, 3) as r:
                for k in range(4):
                    turns.transpose(pe, 4 * r + k, k % 2)
        for n, _, k, j in first_x():
            turns.transpose(pe, n, k)

        def step(two, par, s, at):
            u, items = at(0), items_of(two, par)
            if s == 0:
                x_done = n_first + 4 + per_block * (2 * two + par) - (1 if next_w else 0)
                if isinstance(two, int) and two == 0 and par == 0:
                    x_done = n_first + 4
                pe.wait_ge(turns.high, x_done + OFF)
                pe.wait_ge(turns.low, x_done + OFF)
            pe.wait_ge(acc_out, u - 2 + OFF)
            pe.wait_ge(acc_max, u - 2 + OFF)
            for half in (0, 1):
                i = 2 * s + half
                terms = [(a, b, c) for a, b in ((0, 0), (0, 1), (1, 0)) for c in range(C)]
                for t, (a, b, c) in enumerate(terms):
                    last = nc.tensor.matmul(acc[s % 3][half][:, :], w_hl[:, a, c, P * i:P * i + P],
                                            x_hl[:, par, b, c, :], start=(t == 0), stop=(t == len(terms) - 1))
            last.then_inc(acc_ready, 1)
            if s in items:
                turns.transpose(pe, items[s].n, items[s].slot)

        every_step(pe, step)

    def last_items(two, par, s):
        if s:
            items = items_of(two, par)
            return [items[s - 1]] if s - 1 in items else []
        if not next_w or (isinstance(two, int) and two == 0 and par == 0):
            return []
        return [items_of(two, 0)[5]] if par else [items_of(two - 1, 1)[5]]

    def act_program(act):
        turns.start({"act": act})
        act.sem_inc(acc_out, OFF)
        if up:
            act.sem_inc(gate_done, OFF)
            act.sem_inc(sigmoid_done, OFF)
        if first_w:
            with act.Fori(0, 3) as r:
                for k in range(4):
                    turns.put_high(act, 4 * r + k, k % 2, w_dst(first_w[1], 0, 4 * r + k))
        for n, _, k, j in first_x():
            turns.put_high(act, n, k, x_dst(0, 0, j))

        def step(two, par, s, at):
            u = at(0)
            if u is not None or s == 0:
                for item in last_items(two, par, s):
                    if item.kind == "x":
                        act.wait_ge(acc_ready, 12 * two + (6 * par + OFF))
                    turns.put_high(act, item.n, item.slot, item_dst(item, 0))
            if u is not None:
                act.wait_ge(acc_ready, u + 1 + OFF)
                act.wait_ge(stored[s % 2], 96 * two + (48 * par + 16 * (s // 2) + 16))
                act.wait_ge(acc_max, u - 1 + OFF)
                for half in (0, 1):
                    last = nc.scalar.activation(out[:, s % 2, half, :], acc[s % 3][half][:, :], ACT.Copy)
                last.then_inc(acc_out, 1)
            if up and at(1) is not None:
                u, k = at(1), (s - 1) % 3
                gq = gate_q[:, bass.ds(u, 1), :].rearrange("p a i -> p (a i)")
                loads = 64 * two + (32 * par + 16 * ((s - 1) // 3) + 16)
                act.wait_ge(gate_in[k], loads)
                act.sem_inc(held.act, 1)
                nc.scalar.activation(gq, work[:, k, :], ACT.Copy, scale=sc["gate_c"][:, 0:1]).then_inc(gate_done, 1)
                act.wait_ge(gate_done, u + 1 + OFF)
                act.sem_inc(held.act, 1)
                nc.scalar.activation(work[:, k, :], gq, ACT.Sigmoid, scale=sc["gate_scale"][:, 0:1]).then_inc(sigmoid_done, 1)

        every_step(act, step, 2 if up else 1)

    def dve_program(dve):
        turns.start({"dve": dve})
        dve.sem_inc(acc_max, OFF)
        if up:
            dve.sem_inc(g2_done, OFF)
            dve.sem_inc(g2_max, OFF)
        else:
            nc.vector.tensor_reduce(tops[:, 0:1], dram["yall"][:, :], AX.X, ALU.max).then_inc(col_top, 1)
            dve.wait_ge(top, 1)
            scales.scale(dve, sc["x_scale"], tops[:, 1:2], 1.0, sc["x_inv"])
        if first_w:
            with dve.Fori(0, 3) as r:
                for k in range(4):
                    n = 4 * r + k
                    turns.quantise_w(dve, n, 2 * r + k // 2, 16 * r + 4 * k, k % 2)
                    if k:
                        turns.put_low(dve, n - 1, (k - 1) % 2, w_dst(first_w[1], 1, 4 * r + k - 1),
                                      w_dst(first_w[1], 0, 4 * r + k - 1))
                turns.put_low(dve, 4 * r + 3, 1, w_dst(first_w[1], 1, 4 * r + 3), w_dst(first_w[1], 0, 4 * r + 3))
        for n, half_n, k, j in first_x():
            turns.quantise_x(dve, n, half_n, k, sc["x_inv"])
            turns.put_low(dve, n, k, x_dst(0, 1, j), x_dst(0, 0, j))

        def step(two, par, s, at):
            u, items = at(0), items_of(two, par)
            if u is not None and s in items:
                item = items[s]
                if item.kind == "w":
                    turns.quantise_w(dve, item.n, item.half_n, 4 * n_first + 16 * two + (8 * par + 4 * item.j), item.slot)
                else:
                    turns.quantise_x(dve, item.n, item.half_n, item.slot, sc["x_inv"])
            if u is not None or s == 0:
                for item in last_items(two, par, s):
                    turns.put_low(dve, item.n, item.slot, item_dst(item, 1), item_dst(item, 0))
            if u is not None:
                dve.wait_ge(acc_out, u + 1 + OFF)
                nc.vector.tensor_reduce(cols[:, bass.ds(u, 1)], out[:, s % 2, :, :].rearrange("p a i -> p (a i)"), AX.X,
                                        ALU.max, apply_absolute_value=True).then_inc(acc_max, 1)
            if up and at(2) is not None:
                u, w = at(2), work[:, (s - 2) % 3, :]
                dve.wait_ge(gate_done, u + 1 + OFF)
                dve.wait_ge(sig_done, u + 1 + OFF)
                nc.vector.scalar_tensor_tensor(w, w.bitcast(I32), SIG - 1, gate_q[:, bass.ds(u, 1), :].rearrange(
                    "p a i -> p (a i)"), ALU.min, ALU.mult).then_inc(g2_done, 1)
                dve.wait_ge(g2_done, u + 1 + OFF)
                nc.vector.tensor_reduce(cols2[:, bass.ds(u, 1)], w, AX.X, ALU.max,
                                        apply_absolute_value=True).then_inc(g2_max, 1)

        every_step(dve, step, 2 if up else 1)
        dve.wait_ge(acc_max, N_BLK * PAIRS + OFF)
        nc.vector.tensor_reduce(tops[:, 2:3], cols[:, :], AX.X, ALU.max).then_inc(col_top, 1)
        dve.wait_ge(top, 1 if up else 2)
        if not up:
            scales.scale(dve, sc["gate_scale"], tops[:, 3:4], sc["x_scale"], sc["gate_c"])
        else:
            scales.scale(dve, sc["up_scale"], tops[:, 3:4], sc["x_scale"], sc["up_c"])
            scales.mult(dve, sc["g2_unit"], sc["gate_scale"], 1.0 / SIG)
            dve.wait_ge(g2_max, N_BLK * PAIRS + OFF)
            nc.vector.tensor_reduce(tops[:, 0:1], cols2[:, :], AX.X, ALU.max).then_inc(col_top, 1)
            dve.wait_ge(top, 2)
            scales.scale(dve, sc["g2_scale"], tops[:, 1:2], sc["g2_unit"], sc["g2_c"])
            scales.mult(dve, sc["o_unit"], sc["g2_scale"], sc["up_scale"])

    def pool_program(pool):
        turns.start({"pool": pool})
        if up:
            pool.sem_inc(sig_done, OFF)
        else:
            pool.wait_ge(col_top, 1)
            nc.gpsimd.partition_all_reduce(tops[:, 1:2], tops[:, 0:1], P, RMAX).then_inc(top, 1)
        if first_w:
            with pool.Fori(0, 3) as r:
                for k in range(4):
                    turns.restore_w(pool, 4 * r + k, k % 2)
        for n, _, k, j in first_x():
            turns.restore_x(pool, n, k)

        def step(two, par, s, at):
            u, items = at(0), items_of(two, par)
            if u is not None and s in items:
                restore = turns.restore_w if items[s].kind == "w" else turns.restore_x
                restore(pool, items[s].n, items[s].slot)
            if up and at(1) is not None:
                u, w = at(1), work[:, (s - 1) % 3, :]
                pool.wait_ge(sigmoid_done, u + 1 + OFF)
                pool.sem_inc(held.pool, 1)
                nc.gpsimd.tensor_scalar(w.bitcast(I32), w, SIG, 1.0, ALU.mult, ALU.mult).then_inc(sig_done, 1)

        every_step(pool, step, 1 if up else 0)
        pool.wait_ge(col_top, 1 if up else 2)
        nc.gpsimd.partition_all_reduce(tops[:, 3:4], tops[:, 2:3], P, RMAX).then_inc(top, 1)
        if up:
            pool.wait_ge(col_top, 2)
            nc.gpsimd.partition_all_reduce(tops[:, 1:2], tops[:, 0:1], P, RMAX).then_inc(top, 1)

    return pe_program, act_program, dve_program, pool_program, sp_program


N_GRP = N_BLK * GROUPS


def product_sizes(nc, sb, sem, held, dram, banks, ident, sc, w_hl, gate_q, gates):
    turns = Turns(nc, sb, sem, held, "b", banks[0:GROUPS], ident)
    up_f = sb("up_f", [P, 2, 2048], F32)
    work = sb("b_work", [P, 3, 2048], F32)
    up_q = sb("b_up_q", [P, 2, 2048], I16)
    cols = sb("b_cols", [P, N_GRP], F32)
    tops = sb("b_tops", [P, 2], F32)
    up_in = [sem("up_in0"), sem("up_in1")]
    stored = [sem("b_stored0"), sem("b_stored1")]
    sigmoid_done, g2_quantised = sem("b_sigmoid_done"), sem("g2_quantised")
    up_quantised = sem("up_quantised")
    g2_done, o_done, o_max = sem("b_g2_done"), sem("b_o_done"), sem("b_o_max")
    sig_done = sem("b_sig_done")
    col_top, top = sem("b_col_top"), sem("b_top")
    scales = Scales(nc, sem, "b_scales")
    w_down = dram["L1_ffn_w_down"]
    g_all = gate_q[:, :, :].rearrange("p u i -> p (u i)")

    def loads(n, slot):
        return 8 * (n - slot) + 16

    def gq(n):
        return g_all[:, bass.ds(n * 2048, 2048)]

    def w_dst(part, r, g):
        return w_hl[:, part, 4 * g:4 * g + 4, bass.ds(P * r, P)]

    def each_group(eng, step, w_step):
        def six_steps(six, at):
            for k in range(6):
                with_w = (lambda *what: w_step(six, k // 2, *what)) if k % 2 == 1 else None
                step(6 * six + k, k, at(k), with_w)

        six_steps(0, lambda k: lambda lag: k - lag if k >= lag else None)
        with eng.Fori(1, N_GRP // 6) as six:
            six_steps(six, lambda k: lambda lag: 6 * six + (k - lag))
        for i in (N_GRP, N_GRP + 1):
            step(i, i % 6, lambda lag, i=i: i - lag if i - lag < N_GRP else None, None)

    def sp_program(sp):
        for s in stored:
            sp.sem_inc(s, 16)
        def load_next(r, g):
            sp.wait_ge(turns.restored, GROUPS * r + (g + 1 + OFF))
            load_w((r + 1) % (D // P), g)

        def load_w(r, g):
            sp.dma_start(turns.raw[:, g, :], w_down[bass.ds(P * r, P), 512 * g:512 * g + 512]).then_inc(turns.loaded[g], 16)

        for g in range(GROUPS):
            load_w(0, g)

        def step(i, k, at, with_w):
            if with_w:
                with_w()
            n = at(0)
            if n is not None:
                sp.wait_ge(o_max, n - 1 + OFF)
                sp.dma_start(up_f[:, k % 2, :].rearrange("p (u i) -> p u i", u=2),
                             dram["up"][bass.ds(2 * n, 2)].rearrange("u p i -> p u i")).then_inc(up_in[k % 2], 16)
            n = at(2)
            if n is not None:
                sp.wait_ge(up_quantised, n + 1 + OFF)
                sp.dma_start(dram["up_q"][n], up_q[:, k % 2, :]).then_inc(stored[k % 2], 16)

        each_group(sp, step, load_next)
        for s in stored:
            sp.wait_ge(s, 16 * (N_GRP // 2 + 1))
        for s in turns.loaded:
            sp.wait_ge(s, 16 * (D // P + 1))

    def pe_program(pe):
        turns.start({"pe": pe})
        with pe.Fori(0, D // P) as r:
            for g in range(GROUPS):
                turns.transpose(pe, GROUPS * r + g, g)

    def act_program(act):
        turns.start({"act": act})
        for s in (sigmoid_done, g2_quantised, up_quantised):
            act.sem_inc(s, OFF)
        def step(i, k, at, with_w):
            n = at(0)
            if n is not None:
                act.wait_ge(g2_quantised, n - 2 + OFF)
                act.sem_inc(held.act, 1)
                nc.scalar.activation(work[:, k % 3, :], gq(n), ACT.Sigmoid,
                                     scale=sc["gate_scale"][:, 0:1]).then_inc(sigmoid_done, 1)
            n = at(2)
            if n is not None:
                act.wait_ge(up_in[k % 2], loads(n, k % 2))
                act.wait_ge(stored[k % 2], loads(n, k % 2))
                nc.scalar.activation(up_q[:, k % 2, :], up_f[:, k % 2, :], ACT.Copy,
                                     scale=sc["up_c"][:, 0:1]).then_inc(up_quantised, 1)
                act.wait_ge(g2_done, n + 1 + OFF)
                act.sem_inc(held.act, 1)
                nc.scalar.activation(gq(n), work[:, (k - 2) % 3, :], ACT.Copy,
                                     scale=sc["g2_c"][:, 0:1]).then_inc(g2_quantised, 1)
            if with_w:
                with_w()

        each_group(act, step, lambda r, g: turns.put_high(act, GROUPS * r + g, g, w_dst(0, r, g)))

    def dve_program(dve):
        turns.start({"dve": dve})
        for s in (g2_done, o_done, o_max):
            dve.sem_inc(s, OFF)
        def step(i, k, at, with_w):
            n = at(1)
            if n is not None:
                dve.wait_ge(sig_done, n + 1 + OFF)
                w = work[:, (k - 1) % 3, :]
                nc.vector.scalar_tensor_tensor(w, w.bitcast(I32), SIG - 1, gq(n), ALU.min, ALU.mult).then_inc(g2_done, 1)
            if with_w:
                with_w("quantise")
            n = at(2)
            if n is not None:
                dve.wait_ge(g2_quantised, n + 1 + OFF)
                dve.wait_ge(up_quantised, n + 1 + OFF)
                nc.vector.tensor_tensor(up_f[:, k % 2, :], gq(n), up_q[:, k % 2, :], ALU.mult).then_inc(o_done, 1)
                dve.wait_ge(o_done, n + 1 + OFF)
                nc.vector.tensor_reduce(cols[:, bass.ds(n, 1)], up_f[:, k % 2, :], AX.X, ALU.max,
                                        apply_absolute_value=True).then_inc(o_max, 1)
            if with_w:
                with_w("put away")

        def w_step(r, g, what):
            if what == "quantise":
                turns.quantise_w(dve, GROUPS * r + g, r, 4 * GROUPS * r + 4 * g, g)
            else:
                turns.put_low(dve, GROUPS * r + g, g, w_dst(1, r, g), w_dst(0, r, g))

        each_group(dve, step, w_step)
        dve.wait_ge(o_max, N_GRP + OFF)
        nc.vector.tensor_reduce(tops[:, 0:1], cols[:, :], AX.X, ALU.max).then_inc(col_top, 1)
        dve.wait_ge(top, 1)
        scales.scale(dve, sc["o_scale"], tops[:, 1:2], sc["o_unit"], sc["o_c"])
        scales.mult(dve, sc["out_factor"], sc["o_scale"], gates[:, 3:4])

    def pool_program(pool):
        turns.start({"pool": pool})
        pool.sem_inc(sig_done, OFF)
        def step(i, k, at, with_w):
            n = at(0)
            if n is None:
                return
            w = work[:, k % 3, :]
            pool.wait_ge(sigmoid_done, n + 1 + OFF)
            pool.sem_inc(held.pool, 1)
            nc.gpsimd.tensor_scalar(w.bitcast(I32), w, SIG, 1.0, ALU.mult, ALU.mult).then_inc(sig_done, 1)
            if with_w:
                with_w()

        each_group(pool, step, lambda r, g: turns.restore_w(pool, GROUPS * r + g, g))
        pool.wait_ge(col_top, 1)
        nc.gpsimd.partition_all_reduce(tops[:, 1:2], tops[:, 0:1], P, RMAX).then_inc(top, 1)

    return pe_program, act_program, dve_program, pool_program, sp_program


def down_product(nc, sb, sem, held, dram, banks, sc, w_hl, gate_q):
    up_q = sb("c_up_q", [P, 3, 2048], I16)
    prod = sb("c_prod", [P, 2048], F32)
    o_hl = sb("o_hl", [P, 2, 2, 2048], F32R)
    res = sb("c_res", [P, 4, D], F32)
    up_in = [sem(f"c_up_in{k}") for k in range(3)]
    x_in = [sem(f"c_x_in{j}") for j in range(4)]
    stored = [sem(f"c_stored{j}") for j in range(4)]
    prod_done = sem("c_prod_done")
    o_quantised, high = sem("c_o_quantised"), sem("c_high")
    low = sem("c_low")
    o_used = sem("c_o_used")
    acc_ready = sem("c_acc_ready")
    acc_out = sem("c_acc_out")
    out = dram["out"].rearrange("b (t p) d -> (b t) p d", p=P)
    g_all = gate_q[:, :, :].rearrange("p u i -> p (u i)")
    SLOTS = 2 * GROUPS

    def two_blocks(eng, body):
        with eng.Fori(0, N_BLK // 2) as two:
            for k in range(SLOTS):
                body(SLOTS * two + k, k, two)

    def sp_program(sp):
        for s in stored:
            sp.sem_inc(s, 16)
        with sp.Fori(0, N_BLK) as b:
            for j in range(4):
                sp.wait_ge(stored[j], 16 * b + 16)
                sp.dma_start(res[:, j, :], dram["x_mid"][4 * b + j]).then_inc(x_in[j], 16)
            for j in range(4):
                sp.wait_ge(acc_out, 4 * b + (j + 1 + OFF))
                sp.dma_start(out[4 * b + j], res[:, j, :]).then_inc(stored[j], 16)
        for s in stored:
            sp.wait_ge(s, 16 * (N_BLK + 1))

    def pe_program(pe):
        pe.sem_inc(o_used, OFF)
        pe.sem_inc(acc_ready, OFF)

        def group(n, k, two):
            b, g = divmod(k, GROUPS)
            pe.wait_ge(high, n + 1 + OFF)
            pe.wait_ge(low, n + 1 + OFF)
            if g == 0:
                pe.wait_ge(acc_out, 8 * two + (4 * b - 4 + OFF))
            for i in range(4):
                for j in range(4):
                    for a, b_ in ((0, 0), (0, 1), (1, 0)):
                        last = nc.tensor.matmul(banks[4 * b + j][:, :],
                                                o_hl[:, k % 2, a, 512 * i + P * j:512 * i + P * j + P],
                                                w_hl[:, b_, 4 * g + i, :], start=(g == 0 and i == 0 and (a, b_) == (0, 0)),
                                                stop=(g == GROUPS - 1 and i == 3 and (a, b_) == (1, 0)))
                    if g == GROUPS - 1 and i == 3 and j < 3:
                        last.then_inc(acc_ready, 1)
            last.then_inc(o_used, 1)

        two_blocks(pe, group)

    def act_program(act):
        act.sem_inc(o_quantised, OFF)
        act.sem_inc(high, OFF)

        for n in range(2):
            nc.scalar.dma_start(up_q[:, n, :], dram["up_q"][n]).then_inc(up_in[n], 16)

        def group(n, k, two):
            act.wait_ge(low, n + OFF)
            nc.scalar.dma_start(up_q[:, (k + 2) % 3, :], dram["up_q"][(n + 2) % N_GRP]).then_inc(up_in[(k + 2) % 3], 16)
            act.wait_ge(prod_done, n + 1 + OFF)
            nc.scalar.activation(up_q[:, k % 3, :], prod[:, :], ACT.Copy, scale=sc["o_c"][:, 0:1]).then_inc(o_quantised, 1)
            act.wait_ge(o_quantised, n + 1 + OFF)
            act.wait_ge(o_used, n - 1 + OFF)
            nc.scalar.activation(o_hl[:, k % 2, 0, :], up_q[:, k % 3, :], ACT.Copy).then_inc(high, 1)

        two_blocks(act, group)
        for k in range(2):
            act.wait_ge(up_in[k], 16 * (N_GRP // 3 + 1))

    def dve_program(dve):
        dve.sem_inc(prod_done, OFF)
        dve.sem_inc(low, OFF)
        dve.sem_inc(acc_out, OFF)

        def product(n, k, two):
            dve.wait_ge(up_in[k % 3], 32 * two + (16 * (k // 3) + 16))
            dve.wait_ge(o_quantised, n + OFF)
            nc.vector.tensor_tensor(prod[:, :], g_all[:, bass.ds(n * 2048, 2048)], up_q[:, k % 3, :],
                                    ALU.mult).then_inc(prod_done, 1)

        def low_part(n, k):
            dve.wait_ge(high, n + 1 + OFF)
            nc.vector.tensor_tensor(o_hl[:, k % 2, 1, :], up_q[:, k % 3, :], o_hl[:, k % 2, 0, :].bitcast(F32),
                                    ALU.subtract).then_inc(low, 1)

        def results(b, two):
            for j in range(4):
                if j < 3:
                    dve.wait_ge(acc_ready, 6 * two + (3 * b + j + 1 + OFF))
                else:
                    dve.wait_ge(o_used, SLOTS * two + (GROUPS * (b + 1) + OFF))
                dve.wait_ge(x_in[j], 32 * two + (16 * b + 16))
                nc.vector.scalar_tensor_tensor(res[:, j, :], banks[4 * b + j][:, :], sc["out_factor"][:, 0:1], res[:, j, :],
                                               ALU.mult, ALU.add).then_inc(acc_out, 1)

        def steps(two, last):
            for k in range(SLOTS):
                n = SLOTS * two + k
                if not (last and k == SLOTS - 1):
                    product(n + 1, (k + 1) % SLOTS, two if k + 1 < SLOTS else two + 1)
                low_part(n, k)
                if k == GROUPS:
                    results(0, two)
                if k == 0 and not (isinstance(two, int) and two == 0):
                    results(1, two - 1)

        product(0, 0, 0)
        steps(0, False)
        with dve.Fori(1, N_BLK // 2 - 1) as two:
            steps(two, False)
        steps(N_BLK // 2 - 1, True)
        results(1, N_BLK // 2 - 1)

    def idle(_):
        pass

    return pe_program, act_program, dve_program, idle, sp_program


def run_block(nc, pe_program, act_program, dve_program, pool_program, sp_program):
    with nc.Block() as block:
        @block.sync
        def _(sp):
            sp_program(sp)

        @block.scalar
        def _(act):
            act_program(act)

        @block.tensor
        def _(pe):
            pe_program(pe)

        @block.vector
        def _(dve):
            dve_program(dve)

        @block.gpsimd
        def _(pool):
            pool_program(pool)


def build(nc, dram):
    with ExitStack() as ctx:
        def sem(name):
            return ctx.enter_context(nc.semaphore(name))

        def buffers(stage):
            return lambda name, shape, dt: stage.enter_context(nc.sbuf_tensor(name, shape, dt))

        sb = buffers(ctx)
        held = Held(sem)
        gates = sb("gates", [P, 4], F32)
        ident = sb("ident", [P, P], F32)
        dram["yall"] = sb("yall", [P, B * T], F32)
        sc = {name: sb("the_" + name, [P, 1], F32) for name in SCALARS}
        banks = [ctx.enter_context(nc.psum_tensor(f"bank{k}", [P, 512], F32)) for k in range(8)]
        phase = ctx.enter_context(ExitStack())
        w_ffn = phase.enter_context(nc.sbuf_tensor("w_ffn", [P, C, D], F32))
        with ExitStack() as stage:
            run_block(nc, *fold_weights(nc, buffers(stage), sem, dram, banks, ident, w_ffn))
        with ExitStack() as stage:
            one = phase1(nc, buffers(stage), sem, held, dram, gates, banks, ident, w_ffn)
            run_block(nc, *one)
        phase.close()
        w_hl = sb("w_hl", [P, 2 * C * I], F32R)
        up_hl = w_hl[:, :].rearrange("p (a c i) -> p a c i", a=2, c=C)
        down_hl = w_hl[:, :].rearrange("p (a i d) -> p a i d", a=2, i=IT)
        with ExitStack() as stage:
            gate_hl = buffers(stage)("gate_hl", [P, 2, C, I], F32R)
            run_block(nc, *quantised_products(nc, buffers(stage), sem, held, dram, banks, ident, sc, gate_hl, "gate_stage", "gate", None,
                                              (dram["L1_ffn_w_gate"], gate_hl), (dram["L1_ffn_w_up"], up_hl)))
        gate_q = sb("gate_q", [P, N_BLK * PAIRS, 1024], I16)
        with ExitStack() as stage:
            run_block(nc, *quantised_products(nc, buffers(stage), sem, held, dram, banks, ident, sc, up_hl, "up_stage", "up", gate_q,
                                              None, None))
        with ExitStack() as stage:
            run_block(nc, *product_sizes(nc, buffers(stage), sem, held, dram, banks, ident, sc, down_hl, gate_q, gates))
        with ExitStack() as stage:
            run_block(nc, *down_product(nc, buffers(stage), sem, held, dram, banks, sc, down_hl, gate_q))


INPUTS = ("x", "ctx_2048", "itok_Bx1_68_817", "mask_BxS2_ik0", "g_xattn", "g_ffn", "L0_xattn_b", "L0_ffn_weight",
          "L0_ffn_aux_weight1", "L0_ffn_aux_weight2", "L0_ffn_bias", "L1_xattn_b", "L1_ffn_w_gate", "L1_ffn_w_up",
          "L1_ffn_w_down")


def kernel(**inputs):
    import concourse.bacc as bacc
    from concourse.bass_utils import run_bass_kernel_spmd

    nc = bacc.Bacc("TRN2", target_bir_lowering=False, num_devices=1)
    arrays = {name: np.ascontiguousarray(inputs[name]) for name in INPUTS}
    arrays["ident"] = np.eye(P, dtype=np.float32)
    arrays["iota"] = np.arange(S, dtype=np.float32)
    dram = {name: nc.dram_tensor("in_" + name, a.shape, mybir.dt.from_np(a.dtype), kind="ExternalInput").ap()
            for name, a in arrays.items()}
    dram["out"] = nc.dram_tensor("out", (B, S, D), F32, kind="ExternalOutput").ap()
    for name, shape, dt in SCRATCH:
        dram[name] = nc.dram_tensor(name, shape, dt, kind="Internal").ap()
    build(nc, dram)
    return run_bass_kernel_spmd(nc, [{"in_" + name: a for name, a in arrays.items()}], core_ids=[0]).results[0]["out"]


SCRATCH = (("x_mid", (B * T, P, D), F32), ("y_mid", (B * T, P, D), F32), ("gate", (N_BLK * PAIRS, P, 1024), F32),
           ("up", (N_BLK * PAIRS, P, 1024), F32), ("up_q", (N_GRP, P, 2048), I16))
```
